# Optimizing a Trainium2 kernel written in Bass

```python
import numpy as np
import jax
import jax.numpy as jnp

def _softmax(x, axis=-1):
    return jax.nn.softmax(x, axis=axis)

def _gelu(x):
    return jax.nn.gelu(x, approximate=True)

def _silu(x):
    return jax.nn.silu(x)

def _sigmoid(x):
    return jax.nn.sigmoid(x)

def _layernorm(x, axis=-1, eps=1e-05):
    m = jnp.mean(x, axis=axis, keepdims=True)
    v = jnp.var(x, axis=axis, keepdims=True)
    return (x - m) / jnp.sqrt(v + eps)

def _scatter_add(tgt, idx, src, axis=0):
    return tgt.at[idx].add(src)

def _segment_sum(src, seg, n):
    return jax.ops.segment_sum(src, seg, n)
kernel_name = 'mk_adj_resnorm_d4_adj_r2_96770b'

def setup_inputs(seed: int=0):
    np.random.seed(seed)
    _w = jnp.asarray

    def _rec_inputs():
        import jax
        import jax.numpy as jnp
        _gk = jax.random.key(seed)
        x = -0.0003929 + 0.9999 * jax.random.normal(jax.random.fold_in(_gk, 1), (8, 1024, 256), jnp.float32)
        _w = (1.0 + jnp.arange(1024, dtype=jnp.float32)) ** (-0.5)
        _w = _w / _w.mean()
        _pij = jnp.clip(0.0078125 * _w[:, None] * _w[None, :], 0.0, 1.0)
        _a = jax.random.uniform(jax.random.fold_in(_gk, 2), (8, 1024, 1024)) < _pij
        _a = jnp.logical_or(_a, jnp.eye(1024, dtype=bool))
        _af = _a.astype(jnp.float32)
        _af = _af * jax.random.uniform(jax.random.fold_in(_gk, 3), (8, 1024, 1024), jnp.float32, 0.05, 1)
        adj = _af
        return (x, adj)
    x, adj = _rec_inputs()

    def _L0_gnn_setup():
        import jax, jax.numpy as jnp
        import numpy as np
        EPS = 1e-06
        key = jax.random.key(seed)
        k1, k2, k3 = jax.random.split(key, 3)
        B, N, F, O = (8, 2048, 256, 256)
        x = jax.random.normal(k1, (B, N, F), dtype=jnp.float32)
        adj = jax.random.uniform(k2, (B, N, N), dtype=jnp.float32)
        W = jax.random.normal(k3, (O, 2 * F), dtype=jnp.float32) * (1.0 / np.sqrt(2 * F))
        return {'x': x, 'adj': adj, 'W': W}
    _L0_gnn_all = _L0_gnn_setup()
    _L0_gnn_in = {k: v for k, v in _L0_gnn_all.items() if k in ('W',)}
    del _L0_gnn_all

    def _L1_gnn_setup():
        import jax, jax.numpy as jnp
        import numpy as np
        B, N, DIN, DOUT, K = (4, 1024, 256, 256, 3)
        key = jax.random.key(seed)
        ks = jax.random.split(key, 8)
        X = jax.random.normal(ks[0], (B, N, DIN), dtype=jnp.float32)
        A = jax.random.uniform(ks[1], (B, N, N), dtype=jnp.float32)
        Wv = jax.random.normal(ks[2], (DIN, DOUT), dtype=jnp.float32) * 0.02
        bv = jax.random.normal(ks[3], (DOUT,), dtype=jnp.float32) * 0.02
        aw = jax.random.normal(ks[4], (2 * DOUT, 1), dtype=jnp.float32) * 0.05
        ab = jax.random.normal(ks[5], (1,), dtype=jnp.float32) * 0.05
        Wk = jax.random.normal(ks[6], (K, DIN, DOUT), dtype=jnp.float32) * 0.02
        bk = jax.random.normal(ks[7], (K, DOUT), dtype=jnp.float32) * 0.02
        return {'X': X, 'A': A, 'Wv': Wv, 'bv': bv, 'aw': aw, 'ab': ab, 'Wk': Wk, 'bk': bk}
    _L1_gnn_all = _L1_gnn_setup()
    _L1_gnn_in = {k: v for k, v in _L1_gnn_all.items() if k in ('Wv', 'bv', 'aw', 'ab', 'Wk', 'bk')}
    del _L1_gnn_all

    def _L2_gnn_setup():
        import jax, jax.numpy as jnp
        import numpy as np
        B, N, F_IN, F_HID, F_OUT = (32, 512, 256, 256, 256)

        def _gcn_layer(x, adj, W, b):
            support = jnp.einsum('bnf,fh->bnh', x, W)
            return jnp.einsum('bnm,bmh->bnh', adj, support) + b
        key = jax.random.key(seed)
        ks = jax.random.split(key, 8)

        def xavier(k, fan_in, fan_out):
            bound = float(np.sqrt(6.0 / (fan_in + fan_out)))
            return jax.random.uniform(k, (fan_in, fan_out), jnp.float32, -bound, bound)
        return {'batch_graph': jax.random.normal(ks[0], (B, N, F_IN), jnp.float32), 'adj': jax.random.uniform(ks[1], (B, N, N), jnp.float32), 'W1': xavier(ks[2], F_IN, F_HID), 'b1': jnp.zeros((F_HID,), jnp.float32), 'W2': xavier(ks[3], F_HID, F_HID), 'b2': jnp.zeros((F_HID,), jnp.float32), 'W3': xavier(ks[4], F_HID, F_OUT), 'b3': jnp.zeros((F_OUT,), jnp.float32)}
    _L2_gnn_all = _L2_gnn_setup()
    _L2_gnn_in = {k: v for k, v in _L2_gnn_all.items() if k in ('W1', 'b1', 'W2', 'b2', 'W3', 'b3')}
    del _L2_gnn_all

    def _L3_gnn_setup():
        import jax, jax.numpy as jnp
        import numpy as np
        EMBED_DIM = 256
        NUM_HEADS = 8
        HEAD_DIM = EMBED_DIM // NUM_HEADS
        SCALE = HEAD_DIM ** (-0.5)
        B, S = (16, 512)
        key = jax.random.key(seed)
        ks = jax.random.split(key, 12)
        init = lambda k, shape: jax.random.normal(k, shape, dtype=jnp.float32) * EMBED_DIM ** (-0.5)
        return {'x': jax.random.normal(ks[0], (B, S, EMBED_DIM), dtype=jnp.float32), 'adj_matrix': jax.random.uniform(ks[1], (B, S, S), dtype=jnp.float32), 'bond_matrix': jax.random.uniform(ks[2], (B, S, S), dtype=jnp.float32), 'Wq': init(ks[3], (EMBED_DIM, EMBED_DIM)), 'bq': jnp.zeros((EMBED_DIM,), jnp.float32), 'Wk': init(ks[4], (EMBED_DIM, EMBED_DIM)), 'bk': jnp.zeros((EMBED_DIM,), jnp.float32), 'Wv': init(ks[5], (EMBED_DIM, EMBED_DIM)), 'bv': jnp.zeros((EMBED_DIM,), jnp.float32), 'Wo': init(ks[6], (EMBED_DIM, EMBED_DIM)), 'bo': jnp.zeros((EMBED_DIM,), jnp.float32), 'seq_len': S}
    _L3_gnn_all = _L3_gnn_setup()
    _L3_gnn_in = {k: v for k, v in _L3_gnn_all.items() if k in ('Wq', 'bq', 'Wk', 'bk', 'Wv', 'bv', 'Wo', 'bo')}
    del _L3_gnn_all
    return {'x': x, 'adj': adj, 'L0_gnn_W': _L0_gnn_in['W'], 'L1_gnn_Wv': _L1_gnn_in['Wv'], 'L1_gnn_bv': _L1_gnn_in['bv'], 'L1_gnn_aw': _L1_gnn_in['aw'], 'L1_gnn_ab': _L1_gnn_in['ab'], 'L1_gnn_Wk': _L1_gnn_in['Wk'], 'L1_gnn_bk': _L1_gnn_in['bk'], 'L2_gnn_W1': _L2_gnn_in['W1'], 'L2_gnn_b1': _L2_gnn_in['b1'], 'L2_gnn_W2': _L2_gnn_in['W2'], 'L2_gnn_b2': _L2_gnn_in['b2'], 'L2_gnn_W3': _L2_gnn_in['W3'], 'L2_gnn_b3': _L2_gnn_in['b3'], 'L3_gnn_Wq': _L3_gnn_in['Wq'], 'L3_gnn_bq': _L3_gnn_in['bq'], 'L3_gnn_Wk': _L3_gnn_in['Wk'], 'L3_gnn_bk': _L3_gnn_in['bk'], 'L3_gnn_Wv': _L3_gnn_in['Wv'], 'L3_gnn_bv': _L3_gnn_in['bv'], 'L3_gnn_Wo': _L3_gnn_in['Wo'], 'L3_gnn_bo': _L3_gnn_in['bo']}

def reference(x, adj, L0_gnn_W, L1_gnn_Wv, L1_gnn_bv, L1_gnn_aw, L1_gnn_ab, L1_gnn_Wk, L1_gnn_bk, L2_gnn_W1, L2_gnn_b1, L2_gnn_W2, L2_gnn_b2, L2_gnn_W3, L2_gnn_b3, L3_gnn_Wq, L3_gnn_bq, L3_gnn_Wk, L3_gnn_bk, L3_gnn_Wv, L3_gnn_bv, L3_gnn_Wo, L3_gnn_bo):
    import jax
    import jax.numpy as jnp

    def _L0_gnn_ref(x, adj, W):
        import jax, jax.numpy as jnp
        import numpy as np
        EPS = 1e-06
        deg = jnp.sum(adj, axis=-1, keepdims=True)
        agg = jnp.einsum('bij,bjf->bif', adj, x) / jnp.maximum(deg, EPS)
        cat = jnp.concatenate([x, agg], axis=2)
        out = jnp.einsum('bnf,of->bno', cat, W)
        return jax.nn.relu(out)

    def _L1_gnn_ref(X, A, Wv, bv, aw, ab, Wk, bk):
        import jax, jax.numpy as jnp
        import numpy as np
        B, N, DIN, DOUT, K = (4, 1024, 256, 256, 3)
        d = Wv.shape[1]
        Xw = X @ Wv + bv
        sj = Xw @ aw[:d, 0]
        si = Xw @ aw[d:, 0]
        e = jax.nn.leaky_relu(sj[:, None, :] + si[:, :, None] + ab[0], negative_slope=0.2)
        alpha_matrix = A * jnp.exp(e)
        transition = alpha_matrix / (jnp.sum(alpha_matrix, axis=-1, keepdims=True) + 1e-12)
        H = jnp.zeros(X.shape[:-1] + (d,), dtype=X.dtype)
        Xk = X
        for k in range(Wk.shape[0]):
            H = H + Xk @ Wk[k] + bk[k]
            Xk = jnp.einsum('bij,bjd->bid', transition, Xk)
        return jax.nn.relu(H)

    def _L2_gnn_ref(batch_graph, adj, W1, b1, W2, b2, W3, b3):
        import jax, jax.numpy as jnp
        import numpy as np
        B, N, F_IN, F_HID, F_OUT = (32, 512, 256, 256, 256)

        def _gcn_layer(x, adj, W, b):
            support = jnp.einsum('bnf,fh->bnh', x, W)
            return jnp.einsum('bnm,bmh->bnh', adj, support) + b
        x = jax.nn.relu(_gcn_layer(batch_graph, adj, W1, b1))
        x = jax.nn.relu(_gcn_layer(x, adj, W2, b2))
        out = _gcn_layer(x, adj, W3, b3)
        return out

    def _L3_gnn_ref(x, adj_matrix, bond_matrix, Wq, bq, Wk, bk, Wv, bv, Wo, bo, seq_len):
        import jax, jax.numpy as jnp
        import numpy as np
        EMBED_DIM = 256
        NUM_HEADS = 8
        HEAD_DIM = EMBED_DIM // NUM_HEADS
        SCALE = HEAD_DIM ** (-0.5)
        B, S = (16, 512)
        b = x.shape[0]

        def proj(W, bias):
            y = jnp.einsum('bse,fe->bsf', x, W) + bias
            return y.reshape(b, seq_len, NUM_HEADS, HEAD_DIM).transpose(0, 2, 1, 3)
        q, k, v = (proj(Wq, bq), proj(Wk, bk), proj(Wv, bv))
        scores = jnp.einsum('bhqd,bhkd->bhqk', q, k) * SCALE
        mask = (adj_matrix + bond_matrix)[:, None, :, :]
        scores = scores * mask
        attn = jax.nn.softmax(scores, axis=-1)
        ctx = jnp.einsum('bhqk,bhkd->bhqd', attn, v)
        ctx = ctx.transpose(0, 2, 1, 3).reshape(b, seq_len, EMBED_DIM)
        return jnp.einsum('bse,fe->bsf', ctx, Wo) + bo
    x = _layernorm(x + _L0_gnn_ref(x, adj, L0_gnn_W), axis=-1)
    x = _layernorm(x + _L1_gnn_ref(x, adj, L1_gnn_Wv, L1_gnn_bv, L1_gnn_aw, L1_gnn_ab, L1_gnn_Wk, L1_gnn_bk), axis=-1)
    x = _layernorm(x + _L2_gnn_ref(x, adj, L2_gnn_W1, L2_gnn_b1, L2_gnn_W2, L2_gnn_b2, L2_gnn_W3, L2_gnn_b3), axis=-1)
    x = _layernorm(x + _L3_gnn_ref(x, adj, adj, L3_gnn_Wq, L3_gnn_bq, L3_gnn_Wk, L3_gnn_bk, L3_gnn_Wv, L3_gnn_bv, L3_gnn_Wo, L3_gnn_bo, 1024), axis=-1)
    return x

_drawn_inputs = setup_inputs


def setup_inputs(seed=0):
    import zlib

    import numpy as np

    out = dict(_drawn_inputs(seed))
    spreads = {'L2_gnn_b1': (0.0, 0.1),
     'L2_gnn_b2': (0.0, 0.526),
     'L2_gnn_b3': (0.0, 0.596),
     'L3_gnn_bq': (0.0, 0.8),
     'L3_gnn_bk': (0.0, 0.8),
     'L3_gnn_bv': (0.0, 0.1),
     'L3_gnn_bo': (0.0, 0.1)}
    factors = {'L1_gnn_Wv': 4.639,
     'L1_gnn_bv': 33.16,
     'L1_gnn_aw': 4.533,
     'L3_gnn_Wq': 8.0,
     'L3_gnn_Wk': 8.0}
    for name, (base, spread) in spreads.items():
        noise = np.random.default_rng([zlib.crc32(name.encode()), seed]).standard_normal(out[name].shape)
        drawn = base * np.exp(spread * noise) if base else spread * noise
        out[name] = jnp.asarray(drawn.astype(out[name].dtype))
    for name, factor in factors.items():
        out[name] = (out[name] * factor).astype(out[name].dtype)
    return out
```

```python
from contextlib import ExitStack

import concourse.bass as bass
from concourse import mybir

F32 = mybir.dt.float32
F32R = mybir.dt.float32r
ALU = mybir.AluOpType
ACT = mybir.ActivationFunctionType
AX = mybir.AxisListType

P = 128


def build_program(nc: bass.Bass, d: dict, out: bass.AP):
    B, N, F = d["x"].shape
    NT = N // P
    FT = F // P
    HALVES = N // 512
    TPH = NT // HALVES
    H = 8
    HD = F // H
    G = P // HD
    UNITS = NT * H
    EPS_DEG, EPS_ROW, EPS_LN = 1e-6, 1e-12, 1e-5
    SLOPE = 0.2
    LAG = 3
    QSCALE = 2.0 * HD ** -0.5

    W_L0X, W_L0G, W_K0, W_K1, W_K2, W_G1, W_G2, W_G3, W_Q, W_K, W_V, W_O = range(12)

    TP_UNITS = 4 * 4 + 3 * HALVES * NT
    PR_UNITS = NT + HALVES + 1 + NT // 2 + 1 + NT // 2 + NT + 3 * (NT // 2) + 8 + NT // 2

    x_d = d["x"].rearrange("b (t p) f -> b p t f", p=P)
    adj_d = d["adj"].rearrange("b (t p) m -> b t p m", p=P)
    out_d = out.rearrange("b (t p) f -> b t p f", p=P)
    x3_d = nc.dram_tensor("x3_spill", [NT, P, F], F32, kind="Internal").ap()
    qk_d = nc.dram_tensor("qk_spill", [4, 2, P, N], F32, kind="Internal").ap()

    with ExitStack() as ctx:
        def sb(name, shape, dt=F32, stack=ctx):
            return stack.enter_context(nc.sbuf_tensor(name, shape, dt))

        def sem(name):
            return ctx.enter_context(nc.semaphore(name))

        ident = sb("ident", [P, P])
        ones = sb("ones", [P, P])
        ones_r = sb("ones_r", [P, 2], F32R)
        expo = sb("expo", [P, 1])
        eps_ln = sb("eps_ln", [P, 1])
        zero = sb("zero", [P, 1])
        w_hi = sb("w_hi", [P, 12, FT, F], F32R)
        w_lo = sb("w_lo", [P, 12, FT, F], F32R)
        wsj_hi = sb("wsj_hi", [P, FT, 2], F32R)
        wsj_lo = sb("wsj_lo", [P, FT, 2], F32R)
        wsi_hi = sb("wsi_hi", [P, FT, P], F32R)
        wsi_lo = sb("wsi_lo", [P, FT, P], F32R)
        e_const = sb("e_const", [P, 1])
        cols = sb("cols", [P, 4, FT])
        bias_k = sb("bias_k", [P, F])
        bias_g3 = sb("bias_g3", [P, F])
        bias_o = sb("bias_o", [P, F])
        sel = sb("sel", [H, 2, P])
        adjn = sb("adjn", [P, NT, N])
        xn = sb("xn", [P, NT, F])
        stats = sb("stats", [P, 2, 6])
        mv = sb("mv", [P, 2, 2])
        vare = sb("vare", [P, 2])
        rstd = sb("rstd", [P, 2])
        rdeg = sb("rdeg", [P, NT])
        rsum = sb("rsum", [P, NT])
        sj = sb("sj", [P, NT])
        sj_scaled = sb("sj_scaled", [P, NT])
        nmax = sb("nmax", [P, 4])
        mmax = sb("mmax", [P, 4])
        prow = sb("prow", [P, 2, H])
        rprow = sb("rprow", [P, 2, H])

        with ExitStack() as s:
            t_hi = sb("t_hi", [P, NT, N], F32R, s)
            t_lo = sb("t_lo", [P, NT, N], F32R, s)
        with ExitStack() as s:
            q_stack = sb("q_stack", [P, H, N], F32R, s)
            k_stack = sb("k_stack", [P, H, N], F32R, s)
        with ExitStack() as s:
            st_w0 = sb("st_w0", [P, FT, 2 * F], F32, s)
            st_nat = sb("st_nat", [P, 6, FT, F], F32, s)
            st_sq = sb("st_sq", [P, 5, FT, F], F32, s)
            st_wvt = sb("st_wvt", [P, FT, F], F32, s)
            st_aw = sb("st_aw", [P, FT, 2], F32, s)
            st_bc = sb("st_bc", [P, 2, FT], F32, s)
            st_bb = sb("st_bb", [P, 2, FT, P], F32, s)
            st_wa = sb("st_wa", [P, FT, 2], F32, s)
            st_bk = sb("st_bk", [3, F], F32, s)
            st_row = sb("st_row", [1, 2, F], F32, s)
            st_ab = sb("st_ab", [1, 2], F32, s)
        ctx.enter_context(nc.sbuf_tensor("t_area", [P, 2 * NT * N], F32))

        with ExitStack() as s:
            xt_hi = sb("xt_hi", [P, FT, N], F32R, s)
            xt_lo = sb("xt_lo", [P, FT, N], F32R, s)
            u_hi = sb("u_hi", [P, NT * F], F32R, s)
            u_lo = sb("u_lo", [P, NT * F], F32R, s)
        PSLOTS, RSLOTS = 6, 4
        with ExitStack() as s:
            pt = sb("pt", [P, PSLOTS, NT, P], F32, s)
            c_f = sb("c_f", [P, 2, P], F32, s)
            c_hi = sb("c_hi", [P, 2, P], F32R, s)
            c_lo = sb("c_lo", [P, 2, P], F32R, s)
            rbc = sb("rbc", [P, 2, P], F32, s)
            rt = sb("rt", [H, P], F32, s)
            xr = sb("xr", [P, 2, F], F32, s)
        ctx.enter_context(nc.sbuf_tensor("u_area", [P, 4 * NT * F], F32))

        with ExitStack() as s:
            r = sb("r", [P, RSLOTS, N], F32, s)
        with ExitStack() as s:
            si = sb("si", [P, N], F32, s)
            ev = sb("ev", [P, 2, N], F32, s)
        with ExitStack() as s:
            y = sb("y", [P, 2, F], F32, s)
        ctx.enter_context(nc.sbuf_tensor("r_area", [P, RSLOTS * N], F32))

        ps = ctx.enter_context(nc.psum_tensor("ps", [P, 8, 512], F32))
        ACC, TP, PR = 0, 4, 6

        uh = u_hi[:, :].rearrange("p (t f) -> p t f", f=F)
        ul = u_lo[:, :].rearrange("p (t f) -> p t f", f=F)
        gh = u_hi[:, :].rearrange("p (t n) -> p t n", n=N)
        gl = u_lo[:, :].rearrange("p (t n) -> p t n", n=N)
        f32 = lambda ap: ap.bitcast(F32)

        set_in = sem("set_in")
        set_const = sem("set_const")
        set_ones = sem("set_ones")
        set_pe = sem("set_pe")
        set_act = sem("set_act")
        set_dve = sem("set_dve")
        adj_in = [sem(f"adj_in{t}") for t in range(NT)]
        x_in = [sem(f"x_in{h}") for h in range(2)]
        passed = sem("passed")
        drained = sem("drained")
        x_split_hi = sem("x_split_hi")
        x_split = sem("x_split")
        tp_full = sem("tp_full")
        tp_hi = sem("tp_hi")
        tp_free = sem("tp_free")
        deg_sum = sem("deg_sum")
        deg_ready = sem("deg_ready")
        acc_full = sem("acc_full")
        acc_free = sem("acc_free")
        pr_full = sem("pr_full")
        pr_act = sem("pr_act")
        pr_free = sem("pr_free")
        u_act = sem("u_act")
        u_ready = sem("u_ready")
        e_lin = sem("e_lin")
        e_scaled = sem("e_scaled")
        e_exp = sem("e_exp")
        al_hi = sem("al_hi")
        al_ready = sem("al_ready")
        sj_ready = sem("sj_ready")
        h_sum = sem("h_sum")
        y_ready = sem("y_ready")
        bn_raw = sem("bn_raw")
        xr_free = sem("xr_free")
        h_raw = sem("h_raw")
        h_hi = sem("h_hi")
        h_ready = sem("h_ready")
        stat_ready = sem("stat_ready")
        var_ready = sem("var_ready")
        rstd_ready = sem("rstd_ready")
        ln_done = sem("ln_done")
        spilled = sem("spilled")
        qk_hi = sem("qk_hi")
        qk_out = [sem(f"qk_out{k}") for k in range(4)]
        stacked = [sem(f"stacked{k}") for k in range(4)]
        s_full = sem("s_full")
        masked = sem("masked")
        neg_max = sem("neg_max")
        exp_done = sem("exp_done")
        p_full = sem("p_full")
        p_act = sem("p_act")
        p_dve = sem("p_dve")
        ctx_done = sem("ctx_done")
        rp_ready = sem("rp_ready")
        rt_full = sem("rt_full")
        rt_ready = sem("rt_ready")
        rbc_full = sem("rbc_full")
        rbc_ready = sem("rbc_ready")
        c_raw = sem("c_raw")
        c_hi_ready = sem("c_hi_ready")
        c_ready = sem("c_ready")
        o_full = sem("o_full")
        xr_in = [sem(f"xr_in{k}") for k in range(2)]
        out_done = [sem(f"out_done{k}") for k in range(2)]

        def nth(b, per, n):
            return b * per + n

        TP_X = [0, 4 + 2 * NT, 8 + 4 * NT, 12 + 6 * NT]
        TP_A = [4, 8 + 2 * NT, 12 + 4 * NT]
        PR_L0 = 0
        PR_SI = PR_L0 + NT
        PR_SJ = PR_SI + HALVES
        PR_V = PR_SJ + 1
        PR_SUM = PR_V + NT // 2
        PR_Z = PR_SUM + 1
        PR_H = PR_Z + NT // 2
        PR_G = [PR_H + NT, PR_H + NT + NT // 2, PR_H + 2 * NT]
        PR_QK = PR_G[2] + NT // 2
        PR_VV = PR_QK + 8
        assert PR_VV + NT // 2 == PR_UNITS
        AF_L0, AF_P2, AF_C1, AF_C2, AF_C3, AF_PER = 0, 1, 1 + NT, 2 + NT, 6 + NT, 6 + 2 * NT
        U_G, U_V, U_Z, U_C, U_PER = 0, 4, 4 + NT // 2, 4 + NT, 4 + NT + 3 * NT // 2
        LN_PER = 4 * NT

        block = ctx.enter_context(nc.Block())

        @block.sync
        def _(sp):
            sp.dma_start(st_w0[:, :, :], d["L0_gnn_W"].rearrange("(t p) k -> p t k", p=P)).then_inc(set_in, 16)
            sp.dma_start(st_nat[:, 0:3, :, :].rearrange("p k t n -> p (k t) n"),
                         d["L1_gnn_Wk"].rearrange("k (t p) n -> p (k t) n", p=P)).then_inc(set_in, 16)
            for k, name in enumerate(("L2_gnn_W1", "L2_gnn_W2", "L2_gnn_W3")):
                sp.dma_start(st_nat[:, 3 + k, :, :], d[name].rearrange("(t p) n -> p t n", p=P)).then_inc(set_in, 16)
            for k, name in enumerate(("L3_gnn_Wq", "L3_gnn_Wk", "L3_gnn_Wv", "L3_gnn_Wo", "L1_gnn_Wv")):
                sp.dma_start(st_sq[:, k, :, :], d[name].rearrange("(t p) n -> p t n", p=P)).then_inc(set_in, 16)
            with nc.allow_non_contiguous_dma("bias columns, once"):
                for k in range(2):
                    sp.dma_start(st_aw[:, :, k], d["L1_gnn_aw"][k * F:(k + 1) * F, :]
                                 .rearrange("(t p) o -> p (t o)", p=P)).then_inc(set_in, 16)
                for k, name in enumerate(("L1_gnn_bv", "L3_gnn_bv")):
                    sp.dma_start(st_bc[:, k, :], d[name].rearrange("(t p) -> p t", p=P)).then_inc(set_in, 16)
                for k, name in enumerate(("L2_gnn_b1", "L2_gnn_b2", "L3_gnn_bq", "L3_gnn_bk")):
                    sp.dma_start(cols[:, k, :], d[name].rearrange("(t p) -> p t", p=P)).then_inc(set_in, 16)
            sp.dma_start(st_bk[:, :], d["L1_gnn_bk"]).then_inc(set_in, 16)
            sp.dma_start(st_row[:, 0, :], d["L2_gnn_b3"].rearrange("(a n) -> a n", a=1)).then_inc(set_in, 16)
            sp.dma_start(st_row[:, 1, :], d["L3_gnn_bo"].rearrange("(a n) -> a n", a=1)).then_inc(set_in, 16)
            sp.dma_start(st_ab[:, 0:1], d["L1_gnn_ab"].rearrange("(a n) -> a n", a=1)).then_inc(set_in, 16)
            for h in range(2):
                sp.dma_start(xn[:, TPH * h:TPH * (h + 1), :], x_d[0, :, TPH * h:TPH * (h + 1), :]).then_inc(x_in[h], 16)
            for t in range(NT):
                sp.dma_start(adjn[:, t, :], adj_d[0, t]).then_inc(adj_in[t], 16)

            def element(b, last):
                for t in range(NT):
                    sp.wait_ge(ln_done, nth(b, LN_PER, 2 * NT + t + 1))
                    sp.dma_start(x3_d[t], xn[:, t, :]).then_inc(spilled, 16)
                for n in range(4):
                    ft, m = divmod(n, 2)
                    sp.wait_ge(pr_free, nth(b, PR_UNITS, PR_QK + 2 * n + 2))
                    at = slice(n % 2 * N, (n % 2 + 1) * N)
                    sp.dma_start(qk_d[n, 0], f32(u_hi[:, at])).then_inc(qk_out[n], 16)
                    sp.dma_start(qk_d[n, 1], f32(u_lo[:, at])).then_inc(qk_out[n], 16)
                    sp.wait_ge(qk_out[n], nth(b, 32, 32))
                    hi, lo = (qk_d[n, k].rearrange("(g p) n -> p g n", p=HD) for k in range(2))
                    stack = q_stack if m == 0 else k_stack
                    for part, src in enumerate((hi, lo, hi, lo) if m == 0 else (hi, hi, lo, lo)):
                        sp.dma_start(f32(stack[HD * part:HD * (part + 1), ft * G:(ft + 1) * G, :]),
                                     src).then_inc(stacked[n], 16)
                for t in range(NT):
                    if t == 0:
                        sp.wait_ge(spilled, nth(b, 16 * NT, 16 * NT))
                    if t >= 2:
                        store(b, t - 2)
                        sp.wait_ge(out_done[t % 2], nth(b, 8 * NT, 16 * (t // 2)))
                    sp.dma_start(xr[:, t % 2, :], x3_d[t]).then_inc(xr_in[t % 2], 16)
                    if not last:
                        sp.wait_ge(masked, nth(b, UNITS, H * (t + 1)))
                        sp.dma_start(adjn[:, t, :], adj_d[b + 1, t]).then_inc(adj_in[t], 16)
                if not last:
                    sp.wait_ge(ctx_done, nth(b, 2 * NT, 2 * NT))
                    for h in range(2):
                        sp.dma_start(xn[:, TPH * h:TPH * (h + 1), :],
                                     x_d[b + 1, :, TPH * h:TPH * (h + 1), :]).then_inc(x_in[h], 16)
                store(b, NT - 2)
                store(b, NT - 1)
                for k in range(2):
                    sp.wait_ge(out_done[k], nth(b, 8 * NT, 8 * NT))
                sp.sem_inc(xr_free, 1)

            def store(b, t):
                sp.wait_ge(ln_done, nth(b, LN_PER, 3 * NT + t + 1))
                sp.dma_start(out_d[b, t], xr[:, t % 2, :]).then_inc(out_done[t % 2], 16)

            sp.sem_inc(xr_free, 1)
            with sp.Fori(0, B - 1) as b:
                element(b, False)
            element(B - 1, True)

        SET_LOADS = 16 * (1 + 1 + 3 + 5 + 2 + 2 + 4 + 4)

        @block.gpsimd
        def _(pool):
            pool.memset(ident[:, :], 0.0).then_inc(set_const, 1)
            pool.memset(sel[:, :, :], 1.0).then_inc(set_const, 1)
            pool.memset(expo[:, :], -0.5).then_inc(set_const, 1)
            pool.memset(ones[:, :], 1.0).then_inc(set_const, 1)
            pool.memset(eps_ln[:, :], EPS_LN).then_inc(set_const, 1)
            pool.memset(zero[:, :], 0.0).then_inc(set_const, 1)
            pool.wait_ge(set_const, 6)
            pool.affine_select(out=ident[:, :], in_=ident[:, :], compare_op=ALU.not_equal, fill=1.0, base=0,
                               pattern=[[-1, P]], channel_multiplier=1).then_inc(set_const, 1)
            pool.affine_select(out=sel[:, :, :], in_=sel[:, :, :], compare_op=ALU.is_ge, fill=0.0, base=0,
                               pattern=[[P, 2], [1, P]], channel_multiplier=-HD).then_inc(set_const, 1)
            pool.wait_ge(set_const, 8)
            pool.affine_select(out=sel[:, :, :], in_=sel[:, :, :], compare_op=ALU.is_ge, fill=0.0, base=HD - 1,
                               pattern=[[-P, 2], [-1, P]], channel_multiplier=HD).then_inc(set_const, 1)

            def layer_norm(b, layer):
                for t in range(NT):
                    norm_tile(b, layer, t)

            def norm_tile(b, layer, t):
                k = t % 2
                pool.wait_ge(stat_ready, nth(b, LN_PER, layer * NT + t + 1))
                pool.tensor_tensor(vare[:, k:k + 1], mv[:, k, 1:2], eps_ln[:, :], ALU.add).then_inc(var_ready, 1)
                pool.wait_ge(var_ready, nth(b, LN_PER, layer * NT + t + 1))
                pool.tensor_tensor(rstd[:, k:k + 1], vare[:, k:k + 1], expo[:, 0:1], ALU.pow).then_inc(rstd_ready, 1)

            with pool.Fori(0, B) as b:
                for layer in range(3):
                    layer_norm(b, layer)
                for u in range(UNITS + 12):
                    if u >= 19 and (u - 19) % H == 0 and (u - 19) // H < NT:
                        norm_tile(b, 3, (u - 19) // H)
                    if u < UNITS:
                        pool.wait_ge(masked, nth(b, UNITS, u + 1))
                        if u >= 4:
                            pool.wait_ge(exp_done, nth(b, UNITS, u - 3))
                        pool.tensor_tensor(nmax[:, u % 4:u % 4 + 1], zero[:, :], mmax[:, u % 4:u % 4 + 1],
                                           ALU.subtract).then_inc(neg_max, 1)

        @block.tensor
        def _(pe):
            def three(dst, a_hi, a_lo, b_hi, b_lo, first, last, check=False):
                pe.matmul(dst, a_hi, b_hi, start=first, stop=False, skip_group_check=check)
                pe.matmul(dst, a_hi, b_lo, start=False, stop=False, skip_group_check=check)
                return pe.matmul(dst, a_lo, b_hi, start=False, stop=last, skip_group_check=check)

            pe.wait_ge(set_in, SET_LOADS)
            pe.wait_ge(set_const, 9)
            bank = lambda n: ps[:, TP + n % 2, :].rearrange("p (k o) -> p k o", o=F)
            for n in range(7):
                if n >= 2:
                    pe.wait_ge(set_dve, n - 1)
                for kt in range(FT):
                    for ot in range(FT):
                        src = (st_w0[:, ot, (n * FT + kt) * P:(n * FT + kt + 1) * P] if n < 2 else
                               st_sq[:, n - 2, ot, kt * P:(kt + 1) * P])
                        last = pe.transpose(bank(n)[:, kt, ot * P:(ot + 1) * P], src, ident[:, :])
                last.then_inc(set_pe, 1)
            pe.wait_ge(set_dve, 7)
            for it in range(FT):
                for dt in range(FT):
                    last = pe.matmul(ps[:, PR, 2 * it:2 * it + 2], st_wvt[:, dt, it * P:(it + 1) * P],
                                     st_aw[:, dt, :], start=(dt == 0), stop=(dt == FT - 1))
            pe.wait_ge(set_act, 8)
            pe.wait_ge(set_dve, 8)
            for dt in range(FT):
                pe.matmul(ps[:, PR, 8:10], st_bb[:, 0, dt, :], st_aw[:, dt, :], start=(dt == 0), stop=False)
            last = pe.matmul(ps[:, PR, 8:10], ones[0:1, :], st_ab[0:1, :], start=False, stop=True)
            last.then_inc(set_pe, 1)
            pe.matmul(ps[:, ACC, 0:F], ones[0:3, :], st_bk[:, :], start=True, stop=True)
            pe.matmul(ps[:, ACC + 1, 0:F], ones[0:1, :], st_row[0:1, 0, :], start=True, stop=True)
            pe.matmul(ps[:, ACC + 2, 0:F], ones[0:1, :], st_row[0:1, 1, :], start=True, stop=False)
            for et in range(FT):
                pe.matmul(ps[:, ACC + 2, 0:F], st_bb[:, 1, et, :], f32(w_hi[:, W_O, et, :]), start=False, stop=False)
                last = pe.matmul(ps[:, ACC + 2, 0:F], st_bb[:, 1, et, :], f32(w_lo[:, W_O, et, :]), start=False,
                                 stop=(et == FT - 1))
            last.then_inc(set_pe, 1)

            def transpose_x(b, layer):
                n = TP_X[layer]
                for half in range(HALVES):
                    if layer == 0:
                        pe.wait_ge(x_in[half], nth(b, 16, 16))
                    else:
                        pe.wait_ge(ln_done, nth(b, LN_PER, (layer - 1) * NT + TPH * (half + 1)))
                    for ft in range(FT):
                        if n >= 2:
                            pe.wait_ge(tp_free, nth(b, TP_UNITS, n - 1))
                        for t in range(TPH):
                            last = pe.transpose(ps[:, TP + n % 2, t * P:(t + 1) * P],
                                                xn[:, TPH * half + t, ft * P:(ft + 1) * P], ident[:, :])
                        last.then_inc(tp_full, 1)
                        n += 1

            def transpose_adj(b, layer, j):
                for half in range(HALVES):
                    n = TP_A[layer] + j * HALVES + half
                    pe.wait_ge(tp_free, nth(b, TP_UNITS, n - 1))
                    for t in range(TPH):
                        i = TPH * half + t
                        if layer == 0 and j == 0:
                            pe.wait_ge(adj_in[i], nth(b, 16, 16))
                        last = pe.transpose(ps[:, TP + n % 2, t * P:(t + 1) * P],
                                            adjn[:, i, j * P:(j + 1) * P], ident[:, :])
                    last.then_inc(tp_full, 1)

            def project(dst, w, rows, a_hi=xt_hi, a_lo=xt_lo):
                for ft in range(FT):
                    last = three(dst, a_hi[:, ft, rows * P:(rows + 1) * P], a_lo[:, ft, rows * P:(rows + 1) * P],
                                 w_hi[:, w, ft, :], w_lo[:, w, ft, :], ft == 0, ft == FT - 1)
                return last

            def pr_bank(b, n):
                if n >= 2:
                    pe.wait_ge(pr_free, nth(b, PR_UNITS, n - 1))
                return ps[:, PR + n % 2, :]

            def project_pairs(b, n0, w, xt_units):
                for k in range(NT // 2):
                    pe.wait_ge(*xt_units(k))
                    dst = pr_bank(b, n0 + k)
                    for s in range(2):
                        last = project(dst[:, s * F:(s + 1) * F], w, 2 * k + s)
                    last.then_inc(pr_full, 1)

            def transposed_product(dst, ft, j, half, first, last):
                return three(dst, uh[:, j, ft * P:(ft + 1) * P], ul[:, j, ft * P:(ft + 1) * P],
                             t_hi[:, j, half * 512:(half + 1) * 512], t_lo[:, j, half * 512:(half + 1) * 512],
                             first, last)

            def xt_wait(b, layer):
                return lambda k: (tp_free, nth(b, TP_UNITS, TP_X[layer] + (2 if k < NT // 4 else 4)))

            def row_product(b, t, af):
                k = 0 if af == AF_P2 else NT
                if t >= 4:
                    pe.wait_ge(acc_free, nth(b, 2 * NT, k + t - 3))
                for j in range(NT):
                    last = three(ps[:, ACC + t % 4, 0:F], t_hi[:, j, t * P:(t + 1) * P], t_lo[:, j, t * P:(t + 1) * P],
                                 uh[:, j, :], ul[:, j, :], j == 0, j == NT - 1)
                last.then_inc(acc_full, 1)

            def scores(b, u):
                qt, h = divmod(u, H)
                if u < H:
                    pe.wait_ge(stacked[2 * (h // G)], nth(b, 16 * 4, 16 * 4))
                    pe.wait_ge(stacked[2 * (h // G) + 1], nth(b, 16 * 4, 16 * 4))
                if u >= 2:
                    pe.wait_ge(masked, nth(b, UNITS, u - 1))
                for half in range(HALVES):
                    last = pe.matmul(ps[:, 2 * (u % 2) + half, :], q_stack[:, h, qt * P:(qt + 1) * P],
                                     k_stack[:, h, half * 512:(half + 1) * 512], start=True, stop=True)
                last.then_inc(s_full, 1)

            def transpose_p(b, u):
                pe.wait_ge(exp_done, nth(b, UNITS, u + 1))
                for half in range(HALVES):
                    if u >= 1:
                        pe.wait_ge(p_dve if half == 0 else p_act, nth(b, UNITS, u))
                    for t in range(TPH):
                        last = pe.transpose(ps[:, TP + half, t * P:(t + 1) * P],
                                            r[:, u % RSLOTS, (TPH * half + t) * P:(TPH * half + t + 1) * P], ident[:, :])
                    last.then_inc(p_full, 1)

            def context(b, grp, part):
                qt, g = divmod(grp, 2)
                pe.wait_ge(p_act if part else p_dve, nth(b, UNITS, G * grp + G))
                if g == 0 and qt >= 1 and part == 0:
                    pe.wait_ge(c_raw, nth(b, NT, qt))
                for kt in range(part * TPH, (part + 1) * TPH):
                    for hh in range(G):
                        h = g * G + hh
                        last = pe.matmul(ps[HD * hh:HD * (hh + 1), 6, g * P:(g + 1) * P],
                                         xn[:, kt, h * HD:(h + 1) * HD], pt[:, (grp * G + hh) % PSLOTS, kt, :],
                                         start=(kt == 0), stop=(kt == NT - 1), tile_position=(0, HD * hh))
                if part:
                    last.then_inc(ctx_done, 1)

            def denominators(b, qt):
                pe.wait_ge(rp_ready, nth(b, NT, qt + 1))
                if qt >= 1:
                    pe.wait_ge(h_sum, nth(b, NT, qt))
                pe.matmul(ps[0:H, 7, 0:P], rprow[:, qt % 2, :], ident[:, :], start=True, stop=True).then_inc(rt_full, 1)

            def spread_denominators(b, qt):
                pe.wait_ge(rt_ready, nth(b, NT, qt + 1))
                for g in range(2):
                    last = pe.matmul(ps[:, 7, g * P:(g + 1) * P], sel[:, g, :], rt[:, :], start=True, stop=True)
                last.then_inc(rbc_full, 1)

            def output(b, qt):
                pe.wait_ge(c_ready, nth(b, NT, qt + 1))
                for g in range(2):
                    last = three(ps[:, 7, 0:F], c_hi[:, g, :], c_lo[:, g, :], w_hi[:, W_O, g, :], w_lo[:, W_O, g, :],
                                 g == 0, g == 1)
                last.then_inc(o_full, 1)

            with pe.Fori(0, B) as b:
                pe.wait_ge(drained, b + 1)
                transpose_x(b, 0)
                transpose_adj(b, 0, 0)
                pe.wait_ge(x_split, nth(b, 2, 2))
                for j in range(NT):
                    if j + 1 < NT:
                        transpose_adj(b, 0, j + 1)
                    pe.wait_ge(tp_free, nth(b, TP_UNITS, TP_A[0] + 2 * j + 2))
                    for half in range(HALVES):
                        for ft in range(FT):
                            last = transposed_product(ps[:, ACC + 2 * half + ft, :], ft, j, half, j == 0, j == NT - 1)
                last.then_inc(acc_full, 1)
                for t in range(NT):
                    if t == 0:
                        pe.wait_ge(tp_free, nth(b, TP_UNITS, TP_X[0] + 4))
                    dst = pr_bank(b, PR_L0 + t)
                    project(dst[:, 0:F], W_L0X, t)
                    if t % TPH == 0:
                        pe.wait_ge(u_ready, nth(b, 4 + NT // 2, 2 * (t // TPH) + 2))
                    project(dst[:, F:2 * F], W_L0G, t, gh, gl).then_inc(pr_full, 1)

                transpose_x(b, 1)
                for half in range(HALVES):
                    pe.wait_ge(tp_free, nth(b, TP_UNITS, TP_X[1] + 2 * half + 2))
                    dst = pr_bank(b, PR_SI + half)
                    cols_h = slice(half * 512, (half + 1) * 512)
                    for ft in range(FT):
                        last = three(dst, wsi_hi[:, ft, :], wsi_lo[:, ft, :], xt_hi[:, ft, cols_h],
                                     xt_lo[:, ft, cols_h], ft == 0, ft == FT - 1)
                    last.then_inc(pr_full, 1)
                dst = pr_bank(b, PR_SJ)
                for t in range(NT):
                    for ft in range(FT):
                        last = three(dst[:, 2 * t:2 * t + 2], xt_hi[:, ft, t * P:(t + 1) * P],
                                     xt_lo[:, ft, t * P:(t + 1) * P], wsj_hi[:, ft, :], wsj_lo[:, ft, :],
                                     ft == 0, ft == FT - 1)
                last.then_inc(pr_full, 1)
                transpose_adj(b, 1, 0)
                project_pairs(b, PR_V, W_K2, xt_wait(b, 1))
                pe.wait_ge(pr_free, nth(b, PR_UNITS, PR_V + NT // 2))
                sums = pr_bank(b, PR_SUM)
                for j in range(NT):
                    if j + 1 < NT:
                        transpose_adj(b, 1, j + 1)
                    pe.wait_ge(al_ready, nth(b, 2 * NT, 2 * j + 2))
                    for i in range(NT):
                        dst = ps[:, ACC + i // 2, (i % 2) * F:(i % 2 + 1) * F]
                        a_hi, a_lo = t_hi[:, j, i * P:(i + 1) * P], t_lo[:, j, i * P:(i + 1) * P]
                        three(dst, a_hi, a_lo, uh[:, j, :], ul[:, j, :], j == 0 and i % 2 == 0, j == NT - 1, True)
                        pe.matmul(sums[:, 2 * i:2 * i + 2], a_hi, ones_r[:, :], start=(j == 0 and i == 0),
                                  stop=False, skip_group_check=True)
                        last = pe.matmul(sums[:, 2 * i:2 * i + 2], a_lo, ones_r[:, :], start=False,
                                         stop=(j == NT - 1), skip_group_check=True)
                last.then_inc(pr_full, 1)
                project_pairs(b, PR_Z, W_K1, xt_wait(b, 1))
                pe.wait_ge(u_ready, nth(b, 4 + NT // 2, 4 + NT // 2))
                for t in range(NT):
                    project(pr_bank(b, PR_H + t)[:, 0:F], W_K0, t).then_inc(pr_full, 1)
                    row_product(b, t, AF_P2)

                transpose_x(b, 2)
                transpose_adj(b, 2, 0)
                project_pairs(b, PR_G[0], W_G1, xt_wait(b, 2))
                pe.wait_ge(pr_free, nth(b, PR_UNITS, PR_G[0] + NT // 2))
                pe.wait_ge(acc_free, nth(b, 2 * NT, NT))
                for j in range(NT):
                    if j + 1 < NT:
                        transpose_adj(b, 2, j + 1)
                    pe.wait_ge(tp_free, nth(b, TP_UNITS, TP_A[2] + 2 * j + 2))
                    for half in range(HALVES):
                        for ft in range(FT):
                            last = transposed_product(ps[:, ACC + 2 * half + ft, :], ft, j, half, j == 0, j == NT - 1)
                last.then_inc(acc_full, 1)
                h_wait = lambda c: (lambda k: (h_ready, nth(b, 8, 4 * c + (2 if k < NT // 4 else 4))))
                project_pairs(b, PR_G[1], W_G2, h_wait(0))
                pe.wait_ge(pr_free, nth(b, PR_UNITS, PR_G[1] + NT // 2))
                for half in range(HALVES):
                    for ft in range(FT):
                        for j in range(NT):
                            last = transposed_product(ps[:, ACC + 2 * half + ft, :], ft, j, half, j == 0, j == NT - 1)
                        last.then_inc(acc_full, 1)
                project_pairs(b, PR_G[2], W_G3, h_wait(1))
                pe.wait_ge(pr_free, nth(b, PR_UNITS, PR_G[2] + NT // 2))
                for t in range(NT):
                    row_product(b, t, AF_C3)

                transpose_x(b, 3)
                for ft in range(FT):
                    for m, w in enumerate((W_Q, W_K)):
                        for half in range(HALVES):
                            pe.wait_ge(tp_free, nth(b, TP_UNITS, TP_X[3] + 2 * half + 2))
                            dst = pr_bank(b, PR_QK + 4 * ft + 2 * m + half)
                            cols_h = slice(half * 512, (half + 1) * 512)
                            for et in range(FT):
                                last = three(dst, w_hi[:, w, et, ft * P:(ft + 1) * P],
                                             w_lo[:, w, et, ft * P:(ft + 1) * P], xt_hi[:, et, cols_h],
                                             xt_lo[:, et, cols_h], et == 0, et == FT - 1)
                            last.then_inc(pr_full, 1)
                project_pairs(b, PR_VV, W_V, xt_wait(b, 3))
                pe.wait_ge(pr_free, nth(b, PR_UNITS, PR_UNITS))
                scores(b, 0)
                for s in range(UNITS + 10):
                    if s + 1 < UNITS:
                        scores(b, s + 1)
                    if LAG <= s < UNITS + LAG:
                        transpose_p(b, s - LAG)
                    for part in range(2):
                        if s - part >= LAG + G and (s - part - LAG) % G == 0 and (s - part - LAG) // G <= 2 * NT:
                            context(b, (s - part - LAG) // G - 1, part)
                    if s >= 11 and (s - 11) % H == 0 and (s - 11) // H < NT:
                        denominators(b, (s - 11) // H)
                    if s >= 13 and (s - 13) % H == 0 and (s - 13) // H < NT:
                        spread_denominators(b, (s - 13) // H)
                    if s >= 17 and (s - 17) % H == 0 and (s - 17) // H < NT:
                        output(b, (s - 17) // H)

        @block.scalar
        def _(act):
            copy = lambda dst, src, scale=1.0: nc.scalar.activation(dst, src, ACT.Copy, scale=scale)

            act.wait_ge(set_in, SET_LOADS)
            act.wait_ge(set_const, 9)
            for n, slot in enumerate((W_L0X, W_L0G, W_Q, W_K, W_V, W_O)):
                act.wait_ge(set_pe, n + 1)
                copy(w_hi[:, slot, :, :].rearrange("p k o -> p (k o)"), ps[:, TP + n % 2, :],
                     QSCALE if slot == W_Q else 1.0).then_inc(set_act, 1)
            copy(w_hi[:, W_K0:W_G3 + 1, :, :].rearrange("p w k o -> p (w k o)"),
                 st_nat[:, :, :, :].rearrange("p w k o -> p (w k o)")).then_inc(set_act, 1)
            copy(ones_r[:, :], ones[:, 0:2])
            for k in range(2):
                for t in range(FT):
                    last = copy(st_bb[:, k, t, :], ones[:, :], st_bc[:, k, t:t + 1])
            last.then_inc(set_act, 1)
            copy(cols[:, 2, :], cols[:, 2, :], QSCALE).then_inc(set_act, 1)
            act.wait_ge(set_pe, 8)
            wa = ps[:, PR, 0:2 * FT].rearrange("p (t k) -> p t k", k=2)
            copy(wsj_hi[:, :, :], wa).then_inc(set_act, 1)
            copy(st_wa[:, :, :], wa).then_inc(set_act, 1)
            act.wait_ge(set_act, 11)
            for t in range(FT):
                last = copy(wsi_hi[:, t, :], ones[:, :], st_wa[:, t, 1:2])
            last.then_inc(set_act, 1)
            act.wait_ge(set_pe, 9)
            copy(bias_k[:, :], ps[:, ACC, 0:F])
            copy(bias_g3[:, :], ps[:, ACC + 1, 0:F])
            copy(bias_o[:, :], ps[:, ACC + 2, 0:F]).then_inc(set_act, 1)
            act.wait_ge(set_dve, 12)

            def x_transposed(b, layer):
                for k in range(2 * FT):
                    n, half, ft = TP_X[layer] + k, k // FT, k % FT
                    act.wait_ge(tp_full, nth(b, TP_UNITS, n + 1))
                    copy(xt_hi[:, ft, half * 512:(half + 1) * 512], ps[:, TP + n % 2, :]).then_inc(tp_hi, 1)

            def adj_transposed(b, layer, j):
                for half in range(HALVES):
                    n = TP_A[layer] + j * HALVES + half
                    act.wait_ge(tp_full, nth(b, TP_UNITS, n + 1))
                    copy(t_hi[:, j, half * 512:(half + 1) * 512], ps[:, TP + n % 2, :]).then_inc(tp_hi, 1)

            def rows_from_pr(b, n0, u0):
                for k in range(NT // 2):
                    act.wait_ge(pr_full, nth(b, PR_UNITS, n0 + k + 1))
                    copy(u_hi[:, k * 512:(k + 1) * 512], ps[:, PR + (n0 + k) % 2, :]).then_inc(u_act, 1)

            def hidden(b, c, af):
                for k in range(2 * FT):
                    n, half, ft = 4 * c + k, k // FT, k % FT
                    act.wait_ge(acc_full, nth(b, AF_PER, af(k)))
                    if n >= 2:
                        act.wait_ge(h_ready, nth(b, 8, n - 1))
                    act.activation(ev[:, n % 2, 0:512], ps[:, ACC + k, :], ACT.Relu,
                                   bias=cols[:, c, ft:ft + 1]).then_inc(h_raw, 1)
                    act.wait_ge(h_raw, nth(b, 8, n + 1))
                    copy(xt_hi[:, ft, half * 512:(half + 1) * 512], ev[:, n % 2, 0:512]).then_inc(h_hi, 1)

            with act.Fori(0, B) as b:
                x_transposed(b, 0)
                for h in range(2):
                    act.wait_ge(x_in[h], nth(b, 16, 16))
                    copy(u_hi[:, h * N:(h + 1) * N],
                         xn[:, TPH * h:TPH * (h + 1), :].rearrange("p t f -> p (t f)")).then_inc(x_split_hi, 1)
                for j in range(NT):
                    adj_transposed(b, 0, j)
                act.wait_ge(acc_full, nth(b, AF_PER, AF_L0 + 1))
                for k in range(2 * FT):
                    half, ft = k // FT, k % FT
                    copy(gh[:, ft, half * 512:(half + 1) * 512], ps[:, ACC + k, :]).then_inc(u_act, 1)
                act.wait_ge(deg_ready, nth(b, 2, 1))
                for t in range(NT):
                    n = PR_L0 + t
                    act.wait_ge(pr_full, nth(b, PR_UNITS, n + 1))
                    if t >= 2:
                        act.wait_ge(pr_free, nth(b, PR_UNITS, n - 1))
                    copy(ev[:, t % 2, 0:F], ps[:, PR + n % 2, F:2 * F], rdeg[:, t:t + 1]).then_inc(pr_act, 1)

                x_transposed(b, 1)
                act.wait_ge(pr_free, nth(b, PR_UNITS, PR_SI + HALVES))
                act.wait_ge(sj_ready, nth(b, 1, 1))

                def scaled(j):
                    if j >= 2:
                        act.wait_ge(al_ready, nth(b, 2 * NT, 2 * (j - 2) + 2))
                    act.activation(ev[:, j % 2, :], si[:, :], ACT.Identity, bias=sj_scaled[:, j:j + 1],
                                   scale=SLOPE).then_inc(e_scaled, 1)

                def exponential(j):
                    act.wait_ge(e_lin, nth(b, NT, j + 1))
                    act.activation(ev[:, j % 2, :], ev[:, j % 2, :], ACT.Exp).then_inc(e_exp, 1)

                scaled(0)
                rows_from_pr(b, PR_V, U_V)
                exponential(0)
                for j in range(NT):
                    if j + 1 < NT:
                        scaled(j + 1)
                        exponential(j + 1)
                    act.wait_ge(tp_free, nth(b, TP_UNITS, TP_A[1] + 2 * j + 2))
                    copy(t_hi[:, j, :], ev[:, j % 2, :]).then_inc(al_hi, 1)
                for k in range(NT // 2 + 1):
                    if k < NT // 2:
                        n = PR_Z + k
                        act.wait_ge(pr_full, nth(b, PR_UNITS, n + 1))
                        if k >= 2:
                            act.wait_ge(pr_free, nth(b, PR_UNITS, PR_Z + k - 1))
                        copy(ev[:, k % 2, 0:512], ps[:, PR + n % 2, :]).then_inc(pr_act, 1)
                    if k >= 1:
                        act.wait_ge(pr_free, nth(b, PR_UNITS, PR_Z + k))
                        copy(u_hi[:, (k - 1) * 512:k * 512], ev[:, (k - 1) % 2, 512:1024]).then_inc(u_act, 1)

                x_transposed(b, 2)
                adj_transposed(b, 2, 0)
                rows_from_pr(b, PR_G[0], U_C)
                for j in range(1, NT):
                    adj_transposed(b, 2, j)
                hidden(b, 0, lambda k: AF_C1 + 1)
                rows_from_pr(b, PR_G[1], U_C + NT // 2)
                hidden(b, 1, lambda k: AF_C2 + k + 1)
                rows_from_pr(b, PR_G[2], U_C + NT)

                x_transposed(b, 3)
                for k in range(8):
                    ft, m, half = k // 4, k // 2 % 2, k % 2
                    n = PR_QK + k
                    act.wait_ge(pr_full, nth(b, PR_UNITS, n + 1))
                    if k >= 4 and half == 0:
                        act.wait_ge(qk_out[k // 2 - 2], nth(b, 32, 32))
                    at = (k // 2 % 2) * N + half * 512
                    act.activation(u_hi[:, at:at + 512], ps[:, PR + n % 2, :], ACT.Identity,
                                   bias=cols[:, 2 + m, ft:ft + 1]).then_inc(qk_hi, 1)
                for s in range(UNITS + 8):
                    if LAG <= s < UNITS + LAG:
                        u = s - LAG
                        act.wait_ge(p_full, nth(b, 2 * UNITS, 2 * u + 2))
                        if u >= PSLOTS:
                            act.wait_ge(ctx_done, nth(b, 2 * NT, (u - PSLOTS) // G + 1))
                        copy(pt[:, u % PSLOTS, TPH:NT, :].rearrange("p t q -> p (t q)"),
                             ps[:, TP + 1, :]).then_inc(p_act, 1)
                    if s < UNITS:
                        qt, h = divmod(s, H)
                        act.wait_ge(neg_max, nth(b, UNITS, s + 1))
                        if h == 0 and qt >= 2:
                            act.wait_ge(rp_ready, nth(b, NT, qt - 1))
                        act.activation(r[:, s % RSLOTS, :], r[:, s % RSLOTS, :], ACT.Exp, bias=nmax[:, s % 4:s % 4 + 1],
                                       accum_out=prow[:, qt % 2, h:h + 1]).then_inc(exp_done, 1)
                    if s >= 11 and (s - 11) % H == 0 and (s - 11) // H < NT:
                        qt = (s - 11) // H
                        act.wait_ge(rt_full, nth(b, NT, qt + 1))
                        copy(rt[:, :], ps[0:H, 7, 0:P]).then_inc(rt_ready, 1)
                    if s >= 13 and (s - 13) % H == 0 and (s - 13) // H < NT:
                        qt = (s - 13) // H
                        act.wait_ge(rbc_full, nth(b, NT, qt + 1))
                        if qt >= 1:
                            act.wait_ge(c_raw, nth(b, NT, qt))
                        copy(rbc[:, :, :].rearrange("p g q -> p (g q)"), ps[:, 7, 0:2 * P]).then_inc(rbc_ready, 1)
                    if s >= 15 and (s - 15) % H == 0 and (s - 15) // H < NT:
                        qt = (s - 15) // H
                        act.wait_ge(c_raw, nth(b, NT, qt + 1))
                        if qt >= 1:
                            act.wait_ge(o_full, nth(b, NT, qt))
                        copy(c_hi[:, :, :], c_f[:, :, :]).then_inc(c_hi_ready, 1)

        @block.vector
        def _(dve):
            dve.wait_ge(set_in, SET_LOADS)
            for n, slot in enumerate((W_L0X, W_L0G, W_Q, W_K, W_V, W_O)):
                dve.wait_ge(set_act, n + 1)
                scale = QSCALE if slot == W_Q else 1.0
                dve.scalar_tensor_tensor(out=w_lo[:, slot, :, :].rearrange("p k o -> p (k o)"),
                                         in0=ps[:, TP + n % 2, :], scalar=scale,
                                         in1=f32(w_hi[:, slot, :, :].rearrange("p k o -> p (k o)")),
                                         op0=ALU.mult, op1=ALU.subtract).then_inc(set_dve, 1)
            dve.wait_ge(set_pe, 7)
            dve.tensor_copy(st_wvt[:, :, :].rearrange("p k o -> p (k o)"), ps[:, TP, :]).then_inc(set_dve, 1)
            dve.memset(st_ab[:, 1:2], 0.0).then_inc(set_dve, 1)
            dve.wait_ge(set_act, 7)
            dve.tensor_tensor(w_lo[:, W_K0:W_G3 + 1, :, :].rearrange("p w k o -> p (w k o)"),
                              st_nat[:, :, :, :].rearrange("p w k o -> p (w k o)"),
                              f32(w_hi[:, W_K0:W_G3 + 1, :, :].rearrange("p w k o -> p (w k o)")),
                              ALU.subtract).then_inc(set_dve, 1)
            dve.wait_ge(set_act, 11)
            dve.tensor_tensor(wsj_lo[:, :, :], ps[:, PR, 0:2 * FT].rearrange("p (t k) -> p t k", k=2),
                              f32(wsj_hi[:, :, :]), ALU.subtract).then_inc(set_dve, 1)
            dve.tensor_reduce(e_const[:, :], ps[:, PR, 8:10], AX.X, ALU.add).then_inc(set_dve, 1)
            dve.wait_ge(set_act, 13)
            for t in range(FT):
                last = dve.scalar_tensor_tensor(out=wsi_lo[:, t, :], in0=ones[:, :], scalar=st_wa[:, t, 1:2],
                                                in1=f32(wsi_hi[:, t, :]), op0=ALU.mult, op1=ALU.subtract)
            last.then_inc(set_dve, 1)
            dve.wait_ge(set_dve, 12)
            dve.memset(vare[:, :], 0.0).then_inc(drained, 1)

            def alone():
                dve.sem_inc(passed, 1)

            def rest(dst, value, hi, done):
                dve.tensor_tensor(dst, value, f32(hi), ALU.subtract).then_inc(done, 1)

            def x_transposed(b, layer):
                for k in range(2 * FT):
                    n, half, ft = TP_X[layer] + k, k // FT, k % FT
                    at = slice(half * 512, (half + 1) * 512)
                    dve.wait_ge(tp_hi, nth(b, TP_UNITS - 2 * NT, hi_at(n)))
                    dve.tensor_tensor(xt_lo[:, ft, at], ps[:, TP + n % 2, :], f32(xt_hi[:, ft, at]),
                                      ALU.subtract).then_inc(tp_free, 1)

            def hi_at(n):
                return n + 1 - (2 * NT if n >= TP_A[1] else 0)

            def adj_transposed(b, layer, j):
                for half in range(HALVES):
                    n = TP_A[layer] + j * HALVES + half
                    at = slice(half * 512, (half + 1) * 512)
                    dve.wait_ge(tp_hi, nth(b, TP_UNITS - 2 * NT, hi_at(n)))
                    dve.tensor_tensor(t_lo[:, j, at], ps[:, TP + n % 2, :], f32(t_hi[:, j, at]),
                                      ALU.subtract).then_inc(tp_free, 1)

            def rows_from_pr(b, n0, u0):
                for k in range(NT // 2):
                    at = slice(k * 512, (k + 1) * 512)
                    dve.wait_ge(u_act, nth(b, U_PER, u0 + k + 1))
                    dve.tensor_tensor(u_lo[:, at], ps[:, PR + (n0 + k) % 2, :], f32(u_hi[:, at]),
                                      ALU.subtract).then_inc(pr_free, 1)

            def tile_stats(b, layer, t):
                n = layer * NT + t
                src = y if layer < 3 else xr
                dve.wait_ge(y_ready, nth(b, LN_PER, n + 1))
                dve.bn_stats(stats[:, t % 2, :], src[:, t % 2, :]).then_inc(bn_raw, 1)
                dve.wait_ge(bn_raw, nth(b, LN_PER, n + 1))
                alone()
                dve.bn_aggr(mv[:, t % 2, :], stats[:, t % 2, :]).then_inc(stat_ready, 1)

            def normalise(b, layer, t):
                dve.wait_ge(rstd_ready, nth(b, LN_PER, layer * NT + t + 1))
                src = y[:, t % 2, :] if layer < 3 else xr[:, t % 2, :]
                dst = xn[:, t, :] if layer < 3 else src
                dve.tensor_scalar(dst, src, mv[:, t % 2, 0:1], rstd[:, t % 2:t % 2 + 1],
                                  ALU.subtract, ALU.mult).then_inc(ln_done, 1)

            def relu_residual(b, t):
                dve.scalar_tensor_tensor(out=y[:, t % 2, :], in0=ev[:, t % 2, F:2 * F], scalar=0.0, in1=xn[:, t, :],
                                         op0=ALU.max, op1=ALU.add).then_inc(y_ready, 1)

            def hidden(b, c):
                for k in range(2 * FT):
                    n, half, ft = 4 * c + k, k // FT, k % FT
                    at = slice(half * 512, (half + 1) * 512)
                    dve.wait_ge(h_hi, nth(b, 8, n + 1))
                    rest(xt_lo[:, ft, at], ev[:, n % 2, 0:512], xt_hi[:, ft, at], h_ready)

            with dve.Fori(0, B) as b:
                x_transposed(b, 0)
                dve.wait_ge(xr_free, b + 1)
                for h in range(2):
                    at = slice(h * N, (h + 1) * N)
                    dve.wait_ge(x_split_hi, nth(b, 2, h + 1))
                    rest(u_lo[:, at], xn[:, TPH * h:TPH * (h + 1), :].rearrange("p t f -> p (t f)"), u_hi[:, at], x_split)
                for j in range(NT):
                    adj_transposed(b, 0, j)
                    dve.tensor_reduce(rsum[:, j:j + 1], adjn[:, j, :], AX.X, ALU.add).then_inc(deg_sum, 1)
                dve.wait_ge(deg_sum, nth(b, NT + 1, NT))
                dve.tensor_scalar(rsum[:, :], rsum[:, :], EPS_DEG, None, ALU.max).then_inc(deg_sum, 1)
                dve.wait_ge(deg_sum, nth(b, NT + 1, NT + 1))
                dve.reciprocal(rdeg[:, :], rsum[:, :]).then_inc(deg_ready, 1)
                for k in range(2 * FT):
                    half, ft = k // FT, k % FT
                    at = slice(half * 512, (half + 1) * 512)
                    dve.wait_ge(u_act, nth(b, U_PER, U_G + k + 1))
                    rest(gl[:, ft, at], ps[:, ACC + k, :], gh[:, ft, at], u_ready)
                for t in range(NT + 1):
                    if t < NT:
                        n = PR_L0 + t
                        dve.wait_ge(pr_act, nth(b, NT + NT // 2, t + 1))
                        dve.tensor_tensor(ev[:, t % 2, F:2 * F], ps[:, PR + n % 2, 0:F], ev[:, t % 2, 0:F],
                                          ALU.add).then_inc(pr_free, 1)
                        dve.wait_ge(pr_free, nth(b, PR_UNITS, n + 1))
                        relu_residual(b, t)
                        tile_stats(b, 0, t)
                    if t >= 1:
                        normalise(b, 0, t - 1)

                x_transposed(b, 1)
                for half in range(HALVES):
                    n = PR_SI + half
                    dve.wait_ge(pr_full, nth(b, PR_UNITS, n + 1))
                    dve.tensor_scalar(si[:, half * 512:(half + 1) * 512], ps[:, PR + n % 2, :], e_const[:, 0:1], None,
                                      ALU.add).then_inc(pr_free, 1)
                dve.wait_ge(pr_full, nth(b, PR_UNITS, PR_SJ + 1))
                dve.tensor_copy(sj[:, :], ps[:, PR + PR_SJ % 2, 0:2 * NT].rearrange("p (t k) -> p t k", k=2)[:, :, 0]
                                ).then_inc(pr_free, 1)
                dve.wait_ge(pr_free, nth(b, PR_UNITS, PR_SJ + 1))
                dve.tensor_scalar(sj_scaled[:, :], sj[:, :], SLOPE, None, ALU.mult).then_inc(sj_ready, 1)

                def linear(j):
                    dve.wait_ge(e_scaled, nth(b, NT, j + 1))
                    dve.scalar_tensor_tensor(out=ev[:, j % 2, :], in0=si[:, :], scalar=sj[:, j:j + 1],
                                             in1=ev[:, j % 2, :], op0=ALU.add, op1=ALU.max).then_inc(e_lin, 1)

                linear(0)
                rows_from_pr(b, PR_V, U_V)
                for j in range(NT):
                    if j + 1 < NT:
                        linear(j + 1)
                    dve.wait_ge(e_exp, nth(b, NT, j + 1))
                    for half in range(HALVES):
                        n = TP_A[1] + 2 * j + half
                        at = slice(half * 512, (half + 1) * 512)
                        dve.wait_ge(tp_full, nth(b, TP_UNITS, n + 1))
                        dve.tensor_tensor(ev[:, j % 2, at], ps[:, TP + n % 2, :], ev[:, j % 2, at],
                                          ALU.mult).then_inc(tp_free, 1)
                    dve.wait_ge(al_hi, nth(b, NT, j + 1))
                    for half in range(HALVES):
                        at = slice(half * 512, (half + 1) * 512)
                        rest(t_lo[:, j, at], ev[:, j % 2, at], t_hi[:, j, at], al_ready)
                dve.wait_ge(pr_full, nth(b, PR_UNITS, PR_SUM + 1))
                dve.tensor_scalar(rsum[:, :], ps[:, PR + PR_SUM % 2, 0:2 * NT].rearrange("p (t k) -> p t k", k=2)[:, :, 0],
                                  EPS_ROW, None, ALU.add).then_inc(pr_free, 1)
                dve.wait_ge(pr_free, nth(b, PR_UNITS, PR_SUM + 1))
                dve.reciprocal(rdeg[:, :], rsum[:, :]).then_inc(deg_ready, 1)
                dve.wait_ge(deg_ready, nth(b, 2, 2))
                for k in range(NT // 2 + 1):
                    if k < NT // 2:
                        dve.wait_ge(pr_act, nth(b, NT + NT // 2, NT + k + 1))
                        if k >= 2:
                            dve.wait_ge(u_ready, nth(b, 4 + NT // 2, 4 + k - 1))
                        for s in range(2):
                            t = 2 * k + s
                            last = dve.scalar_tensor_tensor(
                                out=ev[:, k % 2, 512 + s * F:512 + (s + 1) * F],
                                in0=ps[:, ACC + k, s * F:(s + 1) * F], scalar=rdeg[:, t:t + 1],
                                in1=ev[:, k % 2, s * F:(s + 1) * F], op0=ALU.mult, op1=ALU.add)
                        last.then_inc(pr_free, 1)
                    if k >= 1:
                        at = slice((k - 1) * 512, k * 512)
                        dve.wait_ge(u_act, nth(b, U_PER, U_Z + k))
                        rest(u_lo[:, at], ev[:, (k - 1) % 2, 512:1024], u_hi[:, at], u_ready)
                for t in range(NT + 1):
                    if t < NT:
                        n = PR_H + t
                        dve.wait_ge(pr_full, nth(b, PR_UNITS, n + 1))
                        dve.tensor_tensor(ev[:, t % 2, 0:F], ps[:, PR + n % 2, 0:F], bias_k[:, :],
                                          ALU.add).then_inc(pr_free, 1)
                        dve.wait_ge(pr_free, nth(b, PR_UNITS, n + 1))
                        dve.wait_ge(acc_full, nth(b, AF_PER, AF_P2 + t + 1))
                        dve.scalar_tensor_tensor(out=ev[:, t % 2, F:2 * F], in0=ps[:, ACC + t % 4, 0:F],
                                                 scalar=rdeg[:, t:t + 1], in1=ev[:, t % 2, 0:F], op0=ALU.mult,
                                                 op1=ALU.add).then_inc(acc_free, 1)
                        dve.wait_ge(acc_free, nth(b, 2 * NT, t + 1))
                        relu_residual(b, t)
                        tile_stats(b, 1, t)
                    if t >= 1:
                        normalise(b, 1, t - 1)

                x_transposed(b, 2)
                adj_transposed(b, 2, 0)
                rows_from_pr(b, PR_G[0], U_C)
                for j in range(1, NT):
                    adj_transposed(b, 2, j)
                hidden(b, 0)
                rows_from_pr(b, PR_G[1], U_C + NT // 2)
                hidden(b, 1)
                rows_from_pr(b, PR_G[2], U_C + NT)
                for t in range(NT + 1):
                    if t < NT:
                        dve.wait_ge(acc_full, nth(b, AF_PER, AF_C3 + t + 1))
                        dve.tensor_tensor(ev[:, t % 2, 0:F], ps[:, ACC + t % 4, 0:F], bias_g3[:, :],
                                          ALU.add).then_inc(acc_free, 1)
                        dve.wait_ge(acc_free, nth(b, 2 * NT, NT + t + 1))
                        dve.tensor_tensor(y[:, t % 2, :], ev[:, t % 2, 0:F], xn[:, t, :], ALU.add).then_inc(y_ready, 1)
                        tile_stats(b, 2, t)
                    if t >= 1:
                        normalise(b, 2, t - 1)

                x_transposed(b, 3)
                for k in range(8):
                    ft, m, half = k // 4, k // 2 % 2, k % 2
                    n = PR_QK + k
                    dve.wait_ge(qk_hi, nth(b, 8, k + 1))
                    at = (k // 2 % 2) * N + half * 512
                    dve.scalar_tensor_tensor(out=u_lo[:, at:at + 512], in0=ps[:, PR + n % 2, :],
                                             scalar=cols[:, 2 + m, ft:ft + 1], in1=f32(u_hi[:, at:at + 512]),
                                             op0=ALU.add, op1=ALU.subtract).then_inc(pr_free, 1)
                dve.wait_ge(spilled, nth(b, 16 * NT, 16 * NT))
                for k in range(NT // 2):
                    n = PR_VV + k
                    dve.wait_ge(pr_full, nth(b, PR_UNITS, n + 1))
                    dve.tensor_copy(xn[:, 2 * k:2 * k + 2, :].rearrange("p t f -> p (t f)"),
                                    ps[:, PR + n % 2, :]).then_inc(pr_free, 1)
                for s in range(UNITS + 13):
                    if s < UNITS:
                        qt, h = divmod(s, H)
                        dve.wait_ge(s_full, nth(b, UNITS, s + 1))
                        if s >= RSLOTS:
                            dve.wait_ge(p_full, nth(b, 2 * UNITS, 2 * (s - RSLOTS) + 2))
                        if s >= 4:
                            dve.wait_ge(neg_max, nth(b, UNITS, s - 3))
                        alone()
                        dve.tensor_tensor_reduce(
                            out=r[:, s % RSLOTS, :], in0=ps[:, 2 * (s % 2):2 * (s % 2) + 2, :].rearrange("p a c -> p (a c)"),
                            in1=adjn[:, qt, :], scale=1.0, scalar=-3.0e38, op0=ALU.mult, op1=ALU.max,
                            accum_out=mmax[:, s % 4:s % 4 + 1]).then_inc(masked, 1)
                    if LAG <= s < UNITS + LAG:
                        u = s - LAG
                        dve.wait_ge(p_full, nth(b, 2 * UNITS, 2 * u + 1))
                        if u >= PSLOTS:
                            dve.wait_ge(ctx_done, nth(b, 2 * NT, (u - PSLOTS) // G + 1))
                        dve.tensor_copy(pt[:, u % PSLOTS, 0:TPH, :].rearrange("p t q -> p (t q)"),
                                        ps[:, TP, :]).then_inc(p_dve, 1)
                    if s >= 8 and (s - 8) % H == 0 and (s - 8) // H < NT:
                        qt = (s - 8) // H
                        dve.wait_ge(exp_done, nth(b, UNITS, H * (qt + 1)))
                        if qt >= 2:
                            dve.wait_ge(rt_full, nth(b, NT, qt - 1))
                        dve.reciprocal(rprow[:, qt % 2, :], prow[:, qt % 2, :]).then_inc(rp_ready, 1)
                    if s >= 14 and (s - 14) % H == 0 and (s - 14) // H < NT:
                        qt = (s - 14) // H
                        dve.wait_ge(rbc_ready, nth(b, NT, qt + 1))
                        dve.wait_ge(ctx_done, nth(b, 2 * NT, 2 * qt + 2))
                        dve.tensor_tensor(c_f[:, :, :].rearrange("p g q -> p (g q)"), ps[:, 6, 0:2 * P],
                                          rbc[:, :, :].rearrange("p g q -> p (g q)"), ALU.mult).then_inc(c_raw, 1)
                    if s >= 16 and (s - 16) % H == 0 and (s - 16) // H < NT:
                        qt = (s - 16) // H
                        dve.wait_ge(c_hi_ready, nth(b, NT, qt + 1))
                        rest(c_lo[:, :, :], c_f[:, :, :], c_hi[:, :, :], c_ready)
                    if s >= 18 and (s - 18) % H == 0 and (s - 18) // H < NT:
                        qt = (s - 18) // H
                        dve.wait_ge(o_full, nth(b, NT, qt + 1))
                        dve.wait_ge(xr_in[qt % 2], nth(b, 8 * NT, 16 * (qt // 2 + 1)))
                        dve.tensor_tensor(xr[:, qt % 2, :], ps[:, 7, 0:F], xr[:, qt % 2, :],
                                          ALU.add).then_inc(h_sum, 1)
                        dve.wait_ge(h_sum, nth(b, NT, qt + 1))
                        if qt == NT - 1:
                            dve.sem_inc(drained, 1)
                        dve.tensor_tensor(xr[:, qt % 2, :], xr[:, qt % 2, :], bias_o[:, :], ALU.add).then_inc(y_ready, 1)
                        tile_stats(b, 3, qt)
                    if s >= 20 and (s - 20) % H == 0 and (s - 20) // H < NT:
                        normalise(b, 3, (s - 20) // H)


def kernel(**inputs):
    import numpy as np
    import concourse.bacc as bacc
    from concourse.bass_utils import run_bass_kernel_spmd

    nc = bacc.Bacc("TRN2", target_bir_lowering=False, num_devices=1)
    nc.disable_value_cache = True
    arrays, drams = {}, {}
    for name, value in inputs.items():
        a = np.ascontiguousarray(value)
        arrays[f"in_{name}"] = a
        drams[name] = nc.dram_tensor(f"in_{name}", a.shape, mybir.dt.from_np(a.dtype), kind="ExternalInput").ap()
    shape = arrays["in_x"].shape
    out = nc.dram_tensor("out", shape, F32, kind="ExternalOutput").ap()
    build_program(nc, drams, out)
    got = run_bass_kernel_spmd(nc, [arrays], core_ids=[0])
    return got.results[0]["out"]
```

```python
from contextlib import ExitStack

import concourse.bass as bass
from concourse import mybir

F32 = mybir.dt.float32
F32R = mybir.dt.float32r
ALU = mybir.AluOpType
ACT = mybir.ActivationFunctionType
AX = mybir.AxisListType

P = 128


def build_program(nc: bass.Bass, d: dict, out: bass.AP):
    B, N, F = d["x"].shape
    NT = N // P
    FT = F // P
    HALVES = N // 512
    TPH = NT // HALVES
    H = 8
    HD = F // H
    G = P // HD
    UNITS = NT * H
    EPS_DEG, EPS_ROW, EPS_LN = 1e-6, 1e-12, 1e-5
    SLOPE = 0.2
    LAG = 3
    QSCALE = 2.0 * HD ** -0.5

    STACK = 3 * HD
    COPIES = 2 * G * HALVES

    W_L0X, W_L0G, W_K0, W_K1, W_K2, W_G1, W_G2, W_G3, W_Q, W_K, W_V, W_O = range(12)

    TP_UNITS = 4 * 4 + 3 * HALVES * NT
    PR_UNITS = NT + HALVES + 1 + NT // 2 + 1 + NT // 2 + NT + 3 * (NT // 2) + 8 + NT // 2

    x_d = d["x"].rearrange("b (t p) f -> b p t f", p=P)
    adj_d = d["adj"].rearrange("b (t p) m -> b t p m", p=P)
    out_d = out.rearrange("b (t p) f -> b t p f", p=P)
    x3_d = nc.dram_tensor("x3_spill", [NT, P, F], F32, kind="Internal").ap()
    qk_d = nc.dram_tensor("qk_spill", [2, 2, P, N], F32, kind="Internal").ap()

    with ExitStack() as ctx:
        def sb(name, shape, dt=F32, stack=ctx):
            return stack.enter_context(nc.sbuf_tensor(name, shape, dt))

        def sem(name):
            return ctx.enter_context(nc.semaphore(name))

        placer = sb("placer", [P, (4 * G + 2) * HD], F32R)
        ident = sb("ident", [P, P])[:, :]
        ones_2 = sb("ones_2", [P, 2])
        expo = sb("expo", [P, 1])
        eps_ln = sb("eps_ln", [P, 1])
        zero = sb("zero", [P, 1])
        w_hi = sb("w_hi", [P, 12, FT, F], F32R)
        w_lo = sb("w_lo", [P, 12, FT, F], F32R)
        wsj_hi = sb("wsj_hi", [P, FT, 2], F32R)
        wsj_lo = sb("wsj_lo", [P, FT, 2], F32R)
        wsj_pair = sb("wsj_pair", [P, FT, 2], F32R)
        e_const = sb("e_const", [P, 1])
        cols = sb("cols", [P, 4, FT])
        bias_k = sb("bias_k", [P, F])
        bias_g3 = sb("bias_g3", [P, F])
        bias_o = sb("bias_o", [P, F])
        sel = sb("sel", [H, 2, P])
        adjn = sb("adjn", [P, NT, N])
        xn = sb("xn", [P, NT, F])
        stats = sb("stats", [P, 4, 6])
        mv = sb("mv", [P, 4, 2])
        vare = sb("vare", [P, 4])
        rstd = sb("rstd", [P, 4])
        nmean = sb("nmean", [P, 4])
        shift = sb("shift", [P, 4])
        rdeg = sb("rdeg", [P, NT])
        rsum = sb("rsum", [P, NT])
        sj = sb("sj", [P, NT])
        sj_scaled = sb("sj_scaled", [P, NT])
        nmax = sb("nmax", [P, 4])
        mmax = sb("mmax", [P, 4])
        prow = sb("prow", [P, 2, H])
        rprow = sb("rprow", [P, 2, H])

        with ExitStack() as s:
            t_hi = sb("t_hi", [P, NT, N], F32R, s)
            t_lo = sb("t_lo", [P, NT, N], F32R, s)
        with ExitStack() as s:
            e_area = sb("e_area", [P, 2, NT, N], F32, s)
        with ExitStack() as s:
            q_stack = sb("q_stack", [P, H, N], F32R, s)
            k_stack = sb("k_stack", [P, H, N], F32R, s)
        with ExitStack() as s:
            ones = sb("ones", [P, P], F32, s)
            st_w0 = sb("st_w0", [P, FT, 2 * F], F32, s)
            st_nat = sb("st_nat", [P, 6, FT, F], F32, s)
            st_sq = sb("st_sq", [P, 5, FT, F], F32, s)
            st_wvt = sb("st_wvt", [P, FT, F], F32, s)
            st_aw = sb("st_aw", [P, FT, 2], F32, s)
            st_bc = sb("st_bc", [P, 2, FT], F32, s)
            st_bb = sb("st_bb", [P, 2, FT, P], F32, s)
            st_bk = sb("st_bk", [3, F], F32, s)
            st_row = sb("st_row", [1, 2, F], F32, s)
            st_ab = sb("st_ab", [1, 2], F32, s)
        ctx.enter_context(nc.sbuf_tensor("t_area", [P, 2 * NT * N], F32))

        with ExitStack() as s:
            xt_hi = sb("xt_hi", [P, FT, N], F32R, s)
            xt_lo = sb("xt_lo", [P, FT, N], F32R, s)
            u_hi = sb("u_hi", [P, NT * F], F32R, s)
            u_lo = sb("u_lo", [P, NT * F], F32R, s)
        PSLOTS, RSLOTS = 6, 4
        with ExitStack() as s:
            pt = sb("pt", [P, PSLOTS, NT, P], F32, s)
            c_f = sb("c_f", [P, 2, P], F32, s)
            c_hi = sb("c_hi", [P, 2, P], F32R, s)
            c_lo = sb("c_lo", [P, 2, P], F32R, s)
            rbc = sb("rbc", [P, 2, P], F32, s)
            rt = sb("rt", [H, P], F32, s)
            xr = sb("xr", [P, 2, F], F32, s)
        ctx.enter_context(nc.sbuf_tensor("u_area", [P, 4 * NT * F], F32))

        with ExitStack() as s:
            r = sb("r", [P, RSLOTS, N], F32, s)
        with ExitStack() as s:
            si = sb("si", [P, N], F32, s)
            ev = sb("ev", [P, 2, N], F32, s)
            asum = sb("asum", [P, N], F32, s)
        with ExitStack() as s:
            qk0_hi = sb("qk0_hi", [P, 2, N], F32R, s)
            qk0_lo = sb("qk0_lo", [P, 2, N], F32R, s)
        with ExitStack() as s:
            y = sb("y", [P, 4, F], F32, s)
        ctx.enter_context(nc.sbuf_tensor("r_area", [P, RSLOTS * N], F32))

        ps = ctx.enter_context(nc.psum_tensor("ps", [P, 8, 512], F32))
        ACC, TP, PR = 0, 4, 6

        uh = u_hi[:, :].rearrange("p (t f) -> p t f", f=F)
        ul = u_lo[:, :].rearrange("p (t f) -> p t f", f=F)
        gh = u_hi[:, :].rearrange("p (t n) -> p t n", n=N)
        gl = u_lo[:, :].rearrange("p (t n) -> p t n", n=N)
        f32 = lambda ap: ap.bitcast(F32)

        set_in = sem("set_in")
        set_const = sem("set_const")
        set_ones = sem("set_ones")
        set_pe = sem("set_pe")
        set_act = sem("set_act")
        set_dve = sem("set_dve")
        adj_in = [sem(f"adj_in{t}") for t in range(NT)]
        x_in = [sem(f"x_in{h}") for h in range(2)]
        passed = sem("passed")
        drained = sem("drained")
        x_split_hi = sem("x_split_hi")
        x_split = sem("x_split")
        tp_full = sem("tp_full")
        tp_hi = sem("tp_hi")
        tp_free = sem("tp_free")
        deg_sum = sem("deg_sum")
        deg_ready = sem("deg_ready")
        acc_full = sem("acc_full")
        acc_free = sem("acc_free")
        pr_full = sem("pr_full")
        pr_act = sem("pr_act")
        pr_free = sem("pr_free")
        u_act = sem("u_act")
        u_ready = sem("u_ready")
        e_lin = sem("e_lin")
        e_scaled = sem("e_scaled")
        e_exp = sem("e_exp")
        al_hi = sem("al_hi")
        al_ready = sem("al_ready")
        al_summed = sem("al_summed")
        sj_ready = sem("sj_ready")
        h_sum = sem("h_sum")
        y_ready = sem("y_ready")
        bn_raw = sem("bn_raw")
        xr_free = sem("xr_free")
        h_raw = sem("h_raw")
        h_hi = sem("h_hi")
        h_ready = sem("h_ready")
        stat_ready = sem("stat_ready")
        var_ready = sem("var_ready")
        rstd_ready = sem("rstd_ready")
        neg_mean = sem("neg_mean")
        shift_ready = sem("shift_ready")
        ln_done = sem("ln_done")
        spilled = sem("spilled")
        qk_hi = sem("qk_hi")
        qk_out = [sem(f"qk_out{k}") for k in range(2)]
        stacked = [sem(f"stacked{k}") for k in range(2)]
        copies_full = sem("copies_full")
        copies_act = sem("copies_act")
        copies_dve = sem("copies_dve")
        s_full = sem("s_full")
        masked = sem("masked")
        neg_max = sem("neg_max")
        exp_done = sem("exp_done")
        p_full = sem("p_full")
        p_act = sem("p_act")
        p_dve = sem("p_dve")
        ctx_done = sem("ctx_done")
        rp_ready = sem("rp_ready")
        rt_full = sem("rt_full")
        rt_ready = sem("rt_ready")
        rbc_full = sem("rbc_full")
        rbc_ready = sem("rbc_ready")
        c_raw = sem("c_raw")
        c_hi_ready = sem("c_hi_ready")
        c_ready = sem("c_ready")
        o_full = sem("o_full")
        xr_in = [sem(f"xr_in{k}") for k in range(2)]
        out_done = [sem(f"out_done{k}") for k in range(2)]

        def nth(b, per, n):
            return b * per + n

        def qk_place(k, staged, kept):
            m, half = k // 2 % 2, k % 2
            return (staged[:, m * N + half * 512:m * N + (half + 1) * 512] if k < 4 else
                    kept[:, m, half * 512:(half + 1) * 512])

        def copies_place(n):
            h, m, half = n // 4, n // 2 % 2, n % 2
            return (q_stack, k_stack)[m][0:STACK, h, half * 512:(half + 1) * 512]

        TP_X = [0, 4 + 2 * NT, 8 + 4 * NT, 12 + 6 * NT]
        TP_A = [4, 8 + 2 * NT, 12 + 4 * NT]
        PR_L0 = 0
        PR_SI = PR_L0 + NT
        PR_SJ = PR_SI + HALVES
        PR_V = PR_SJ + 1
        PR_SUM = PR_V + NT // 2
        PR_Z = PR_SUM + 1
        PR_H = PR_Z + NT // 2
        PR_G = [PR_H + NT, PR_H + NT + NT // 2, PR_H + 2 * NT]
        PR_QK = PR_G[2] + NT // 2
        PR_VV = PR_QK + 8
        assert PR_VV + NT // 2 == PR_UNITS
        AF_L0, AF_P2, AF_C1, AF_C2, AF_C3, AF_PER = 0, 1, 1 + NT, 2 + NT, 6 + NT, 6 + 2 * NT
        U_G, U_V, U_Z, U_C, U_PER = 0, 4, 4 + NT // 2, 4 + NT, 4 + NT + 3 * NT // 2
        LN_PER = 4 * NT

        block = ctx.enter_context(nc.Block())

        @block.sync
        def _(sp):
            sp.dma_start(st_w0[:, :, :], d["L0_gnn_W"].rearrange("(t p) k -> p t k", p=P)).then_inc(set_in, 16)
            sp.dma_start(st_nat[:, 0:3, :, :].rearrange("p k t n -> p (k t) n"),
                         d["L1_gnn_Wk"].rearrange("k (t p) n -> p (k t) n", p=P)).then_inc(set_in, 16)
            for k, name in enumerate(("L2_gnn_W1", "L2_gnn_W2", "L2_gnn_W3")):
                sp.dma_start(st_nat[:, 3 + k, :, :], d[name].rearrange("(t p) n -> p t n", p=P)).then_inc(set_in, 16)
            for k, name in enumerate(("L3_gnn_Wq", "L3_gnn_Wk", "L3_gnn_Wv", "L3_gnn_Wo", "L1_gnn_Wv")):
                sp.dma_start(st_sq[:, k, :, :], d[name].rearrange("(t p) n -> p t n", p=P)).then_inc(set_in, 16)
            with nc.allow_non_contiguous_dma("bias columns, once"):
                for k in range(2):
                    sp.dma_start(st_aw[:, :, k], d["L1_gnn_aw"][k * F:(k + 1) * F, :]
                                 .rearrange("(t p) o -> p (t o)", p=P)).then_inc(set_in, 16)
                for k, name in enumerate(("L1_gnn_bv", "L3_gnn_bv")):
                    sp.dma_start(st_bc[:, k, :], d[name].rearrange("(t p) -> p t", p=P)).then_inc(set_in, 16)
                for k, name in enumerate(("L2_gnn_b1", "L2_gnn_b2", "L3_gnn_bq", "L3_gnn_bk")):
                    sp.dma_start(cols[:, k, :], d[name].rearrange("(t p) -> p t", p=P)).then_inc(set_in, 16)
            sp.dma_start(st_bk[:, :], d["L1_gnn_bk"]).then_inc(set_in, 16)
            sp.dma_start(st_row[:, 0, :], d["L2_gnn_b3"].rearrange("(a n) -> a n", a=1)).then_inc(set_in, 16)
            sp.dma_start(st_row[:, 1, :], d["L3_gnn_bo"].rearrange("(a n) -> a n", a=1)).then_inc(set_in, 16)
            sp.dma_start(st_ab[:, 0:1], d["L1_gnn_ab"].rearrange("(a n) -> a n", a=1)).then_inc(set_in, 16)
            for h in range(2):
                sp.dma_start(xn[:, TPH * h:TPH * (h + 1), :], x_d[0, :, TPH * h:TPH * (h + 1), :]).then_inc(x_in[h], 16)
            for t in range(NT):
                sp.dma_start(adjn[:, t, :], adj_d[0, t]).then_inc(adj_in[t], 16)

            def element(b, last):
                for t in range(NT):
                    sp.wait_ge(ln_done, nth(b, LN_PER, 2 * NT + t + 1))
                    sp.dma_start(x3_d[t], xn[:, t, :]).then_inc(spilled, 16)
                for n in range(2):
                    sp.wait_ge(pr_free, nth(b, PR_UNITS, PR_QK + 2 * n + 2))
                    at = slice(n * N, (n + 1) * N)
                    sp.dma_start(qk_d[n, 0], f32(u_hi[:, at])).then_inc(qk_out[n], 16)
                    sp.dma_start(qk_d[n, 1], f32(u_lo[:, at])).then_inc(qk_out[n], 16)
                    sp.wait_ge(qk_out[n], nth(b, 32, 32))
                    hi, lo = (qk_d[n, k].rearrange("(g p) n -> p g n", p=HD) for k in range(2))
                    stack = q_stack if n == 0 else k_stack
                    for part, src in enumerate((hi, hi, lo) if n == 0 else (lo, hi, hi)):
                        sp.dma_start(f32(stack[HD * part:HD * (part + 1), G:2 * G, :]),
                                     src).then_inc(stacked[n], 16)
                for t in range(NT):
                    if t == 0:
                        sp.wait_ge(spilled, nth(b, 16 * NT, 16 * NT))
                    if t >= 2:
                        store(b, t - 2)
                        sp.wait_ge(out_done[t % 2], nth(b, 8 * NT, 16 * (t // 2)))
                    sp.dma_start(xr[:, t % 2, :], x3_d[t]).then_inc(xr_in[t % 2], 16)
                    if not last:
                        sp.wait_ge(masked, nth(b, UNITS, H * (t + 1)))
                        sp.dma_start(adjn[:, t, :], adj_d[b + 1, t]).then_inc(adj_in[t], 16)
                if not last:
                    sp.wait_ge(ctx_done, nth(b, 2 * NT, 2 * NT))
                    for h in range(2):
                        sp.dma_start(xn[:, TPH * h:TPH * (h + 1), :],
                                     x_d[b + 1, :, TPH * h:TPH * (h + 1), :]).then_inc(x_in[h], 16)
                store(b, NT - 2)
                store(b, NT - 1)
                for k in range(2):
                    sp.wait_ge(out_done[k], nth(b, 8 * NT, 8 * NT))
                sp.sem_inc(xr_free, 1)

            def store(b, t):
                sp.wait_ge(ln_done, nth(b, LN_PER, 3 * NT + t + 1))
                sp.dma_start(out_d[b, t], xr[:, t % 2, :]).then_inc(out_done[t % 2], 16)

            sp.sem_inc(xr_free, 1)
            with sp.Fori(0, B - 1) as b:
                element(b, False)
            element(B - 1, True)

        SET_LOADS = 16 * (1 + 1 + 3 + 5 + 2 + 2 + 4 + 4)

        @block.gpsimd
        def _(pool):
            pool.memset(ident, 0.0).then_inc(set_const, 1)
            pool.memset(sel[:, :, :], 1.0).then_inc(set_const, 1)
            pool.memset(expo[:, :], -0.5).then_inc(set_const, 1)
            pool.memset(ones[:, :], 1.0).then_inc(set_const, 1)
            pool.memset(eps_ln[:, :], EPS_LN).then_inc(set_const, 1)
            pool.memset(zero[:, :], 0.0).then_inc(set_const, 1)
            pool.wait_ge(set_const, 6)
            pool.affine_select(out=ident, in_=ident, compare_op=ALU.not_equal, fill=1.0, base=0,
                               pattern=[[-1, P]], channel_multiplier=1).then_inc(set_const, 1)
            pool.affine_select(out=sel[:, :, :], in_=sel[:, :, :], compare_op=ALU.is_ge, fill=0.0, base=0,
                               pattern=[[P, 2], [1, P]], channel_multiplier=-HD).then_inc(set_const, 1)
            pool.wait_ge(set_const, 8)
            pool.affine_select(out=sel[:, :, :], in_=sel[:, :, :], compare_op=ALU.is_ge, fill=0.0, base=HD - 1,
                               pattern=[[-P, 2], [-1, P]], channel_multiplier=HD).then_inc(set_const, 1)

            def layer_norm(b, layer):
                for t in range(NT):
                    norm_tile(b, layer, t)

            def norm_tile(b, layer, t):
                k = t % 4
                pool.wait_ge(stat_ready, nth(b, LN_PER, layer * NT + t + 1))
                pool.tensor_tensor(vare[:, k:k + 1], mv[:, k, 1:2], eps_ln[:, :], ALU.add).then_inc(var_ready, 1)
                if layer < 3:
                    pool.tensor_tensor(nmean[:, k:k + 1], zero[:, :], mv[:, k, 0:1], ALU.subtract).then_inc(neg_mean, 1)
                pool.wait_ge(var_ready, nth(b, LN_PER, layer * NT + t + 1))
                pool.tensor_tensor(rstd[:, k:k + 1], vare[:, k:k + 1], expo[:, 0:1], ALU.pow).then_inc(rstd_ready, 1)
                if layer < 3:
                    pool.wait_ge(neg_mean, nth(b, 3 * NT, layer * NT + t + 1))
                    pool.wait_ge(rstd_ready, nth(b, LN_PER, layer * NT + t + 1))
                    pool.tensor_tensor(shift[:, k:k + 1], nmean[:, k:k + 1], rstd[:, k:k + 1],
                                       ALU.mult).then_inc(shift_ready, 1)

            with pool.Fori(0, B) as b:
                layer_norm(b, 0)
                for j in range(NT):
                    pool.wait_ge(tp_free, nth(b, TP_UNITS, TP_A[1] + 2 * j + 2))
                    if j >= 1:
                        pool.wait_ge(al_summed, nth(b, NT, j))
                    so_far = asum[:, :] if j >= 1 else zero[:, 0:1].broadcast_to([P, N])
                    pool.tensor_tensor(asum[:, :], ev[:, j % 2, :], so_far, ALU.add).then_inc(al_summed, 1)
                for layer in (1, 2):
                    layer_norm(b, layer)
                for u in range(UNITS + 12):
                    if u >= 19 and (u - 19) % H == 0 and (u - 19) // H < NT:
                        norm_tile(b, 3, (u - 19) // H)
                    if u < UNITS:
                        pool.wait_ge(masked, nth(b, UNITS, u + 1))
                        if u >= 4:
                            pool.wait_ge(exp_done, nth(b, UNITS, u - 3))
                        pool.tensor_tensor(nmax[:, u % 4:u % 4 + 1], zero[:, :], mmax[:, u % 4:u % 4 + 1],
                                           ALU.subtract).then_inc(neg_max, 1)

        @block.tensor
        def _(pe):
            def three(dst, a_hi, a_lo, b_hi, b_lo, first, last, check=False):
                pe.matmul(dst, a_hi, b_hi, start=first, stop=False, skip_group_check=check)
                pe.matmul(dst, a_hi, b_lo, start=False, stop=False, skip_group_check=check)
                return pe.matmul(dst, a_lo, b_hi, start=False, stop=last, skip_group_check=check)

            pe.wait_ge(set_in, SET_LOADS)
            pe.wait_ge(set_const, 9)
            bank = lambda n: ps[:, TP + n % 2, :].rearrange("p (k o) -> p k o", o=F)
            for n in range(7):
                if n >= 2:
                    pe.wait_ge(set_dve, n - 1)
                for kt in range(FT):
                    for ot in range(FT):
                        src = (st_w0[:, ot, (n * FT + kt) * P:(n * FT + kt + 1) * P] if n < 2 else
                               st_sq[:, n - 2, ot, kt * P:(kt + 1) * P])
                        last = pe.transpose(bank(n)[:, kt, ot * P:(ot + 1) * P], src, ident)
                last.then_inc(set_pe, 1)
            pe.wait_ge(set_dve, 7)
            for it in range(FT):
                for dt in range(FT):
                    last = pe.matmul(ps[:, PR, 2 * it:2 * it + 2], st_wvt[:, dt, it * P:(it + 1) * P],
                                     st_aw[:, dt, :], start=(dt == 0), stop=(dt == FT - 1))
            pe.wait_ge(set_act, 9)
            pe.wait_ge(set_dve, 8)
            for dt in range(FT):
                pe.matmul(ps[:, PR, 8:10], st_bb[:, 0, dt, :], st_aw[:, dt, :], start=(dt == 0), stop=False)
            last = pe.matmul(ps[:, PR, 8:10], ones[0:1, :], st_ab[0:1, :], start=False, stop=True)
            last.then_inc(set_pe, 1)
            pe.matmul(ps[:, ACC, 0:F], ones[0:3, :], st_bk[:, :], start=True, stop=True)
            pe.matmul(ps[:, ACC + 1, 0:F], ones[0:1, :], st_row[0:1, 0, :], start=True, stop=True)
            pe.matmul(ps[:, ACC + 2, 0:F], ones[0:1, :], st_row[0:1, 1, :], start=True, stop=False)
            for et in range(FT):
                pe.matmul(ps[:, ACC + 2, 0:F], st_bb[:, 1, et, :], f32(w_hi[:, W_O, et, :]), start=False, stop=False)
                last = pe.matmul(ps[:, ACC + 2, 0:F], st_bb[:, 1, et, :], f32(w_lo[:, W_O, et, :]), start=False,
                                 stop=(et == FT - 1))
            last.then_inc(set_pe, 1)

            def transpose_x(b, layer):
                n = TP_X[layer]
                for half in range(HALVES):
                    if layer == 0:
                        pe.wait_ge(x_in[half], nth(b, 16, 16))
                    else:
                        pe.wait_ge(ln_done, nth(b, LN_PER, (layer - 1) * NT + TPH * (half + 1)))
                    for ft in range(FT):
                        if n >= 2:
                            pe.wait_ge(tp_free, nth(b, TP_UNITS, n - 1))
                        for t in range(TPH):
                            last = pe.transpose(ps[:, TP + n % 2, t * P:(t + 1) * P],
                                                xn[:, TPH * half + t, ft * P:(ft + 1) * P], ident)
                        last.then_inc(tp_full, 1)
                        n += 1

            def transpose_adj(b, layer, j):
                for half in range(HALVES):
                    n = TP_A[layer] + j * HALVES + half
                    pe.wait_ge(tp_free, nth(b, TP_UNITS, n - 1))
                    for t in range(TPH):
                        i = TPH * half + t
                        if layer == 0 and j == 0:
                            pe.wait_ge(adj_in[i], nth(b, 16, 16))
                        last = pe.transpose(ps[:, TP + n % 2, t * P:(t + 1) * P],
                                            adjn[:, i, j * P:(j + 1) * P], ident)
                    last.then_inc(tp_full, 1)

            def project(dst, w, rows, a_hi=xt_hi, a_lo=xt_lo):
                for ft in range(FT):
                    last = three(dst, a_hi[:, ft, rows * P:(rows + 1) * P], a_lo[:, ft, rows * P:(rows + 1) * P],
                                 w_hi[:, w, ft, :], w_lo[:, w, ft, :], ft == 0, ft == FT - 1)
                return last

            def pr_bank(b, n):
                if n >= 2:
                    pe.wait_ge(pr_free, nth(b, PR_UNITS, n - 1))
                return ps[:, PR + n % 2, :]

            def project_pairs(b, n0, w, xt_units):
                for k in range(NT // 2):
                    pe.wait_ge(*xt_units(k))
                    dst = pr_bank(b, n0 + k)
                    for s in range(2):
                        last = project(dst[:, s * F:(s + 1) * F], w, 2 * k + s)
                    last.then_inc(pr_full, 1)

            def transposed_product(dst, ft, j, half, first, last):
                return three(dst, uh[:, j, ft * P:(ft + 1) * P], ul[:, j, ft * P:(ft + 1) * P],
                             t_hi[:, j, half * 512:(half + 1) * 512], t_lo[:, j, half * 512:(half + 1) * 512],
                             first, last)

            def repeated(w, ft):
                return w[:, ft, 1:2].broadcast_to([P, P])

            def xt_wait(b, layer):
                return lambda k: (tp_free, nth(b, TP_UNITS, TP_X[layer] + (2 if k < NT // 4 else 4)))

            def row_product(b, t, af):
                k = 0 if af == AF_P2 else NT
                if t >= 4:
                    pe.wait_ge(acc_free, nth(b, 2 * NT, k + t - 3))
                for j in range(NT):
                    last = three(ps[:, ACC + t % 4, 0:F], t_hi[:, j, t * P:(t + 1) * P], t_lo[:, j, t * P:(t + 1) * P],
                                 uh[:, j, :], ul[:, j, :], j == 0, j == NT - 1)
                last.then_inc(acc_full, 1)

            def stack_copies(b, n):
                h, m, half = n // 4, n // 2 % 2, n % 2
                if n >= 4:
                    pe.wait_ge(copies_dve if n % 2 else copies_act, nth(b, COPIES // 2, n // 2 - 1))
                at = slice(half * 512, (half + 1) * 512)
                block = lambda k, count: placer[:, (4 * h + k) * HD:(4 * h + k + count) * HD]
                dst = ps[0:STACK, ACC + n % 4, :]
                if m == 0:
                    pe.matmul(dst, block(2, 3), qk0_hi[:, 0, at], start=True, stop=False)
                    last = pe.matmul(dst, block(0, 3), qk0_lo[:, 0, at], start=False, stop=True)
                else:
                    pe.matmul(dst, block(1, 3), qk0_hi[:, 1, at], start=True, stop=False)
                    last = pe.matmul(dst, block(3, 3), qk0_lo[:, 1, at], start=False, stop=True)
                last.then_inc(copies_full, 1)

            def scores(b, u):
                qt, h = divmod(u, H)
                if u == 0:
                    pe.wait_ge(copies_act, nth(b, COPIES // 2, COPIES // 2))
                    pe.wait_ge(copies_dve, nth(b, COPIES // 2, COPIES // 2))
                if u == G:
                    pe.wait_ge(stacked[0], nth(b, 16 * 3, 16 * 3))
                    pe.wait_ge(stacked[1], nth(b, 16 * 3, 16 * 3))
                if u >= 2:
                    pe.wait_ge(masked, nth(b, UNITS, u - 1))
                for half in range(HALVES):
                    last = pe.matmul(ps[:, 2 * (u % 2) + half, :], q_stack[0:STACK, h, qt * P:(qt + 1) * P],
                                     k_stack[0:STACK, h, half * 512:(half + 1) * 512], start=True, stop=True)
                last.then_inc(s_full, 1)

            def transpose_p(b, u):
                pe.wait_ge(exp_done, nth(b, UNITS, u + 1))
                for half in range(HALVES):
                    if u >= 1:
                        pe.wait_ge(p_dve if half == 0 else p_act, nth(b, UNITS, u))
                    for t in range(TPH):
                        last = pe.transpose(ps[:, TP + half, t * P:(t + 1) * P],
                                            r[:, u % RSLOTS, (TPH * half + t) * P:(TPH * half + t + 1) * P], ident)
                    last.then_inc(p_full, 1)

            def context(b, grp, part):
                qt, g = divmod(grp, 2)
                pe.wait_ge(p_act if part else p_dve, nth(b, UNITS, G * grp + G))
                if g == 0 and qt >= 1 and part == 0:
                    pe.wait_ge(c_raw, nth(b, NT, qt))
                for kt in range(part * TPH, (part + 1) * TPH):
                    for hh in range(G):
                        h = g * G + hh
                        last = pe.matmul(ps[HD * hh:HD * (hh + 1), 6, g * P:(g + 1) * P],
                                         xn[:, kt, h * HD:(h + 1) * HD], pt[:, (grp * G + hh) % PSLOTS, kt, :],
                                         start=(kt == 0), stop=(kt == NT - 1), tile_position=(0, HD * hh))
                if part:
                    last.then_inc(ctx_done, 1)

            def denominators(b, qt):
                pe.wait_ge(rp_ready, nth(b, NT, qt + 1))
                if qt >= 1:
                    pe.wait_ge(h_sum, nth(b, NT, qt))
                pe.matmul(ps[0:H, 7, 0:P], rprow[:, qt % 2, :], ident[:, :], start=True, stop=True).then_inc(rt_full, 1)

            def spread_denominators(b, qt):
                pe.wait_ge(rt_ready, nth(b, NT, qt + 1))
                for g in range(2):
                    last = pe.matmul(ps[:, 7, g * P:(g + 1) * P], sel[:, g, :], rt[:, :], start=True, stop=True)
                last.then_inc(rbc_full, 1)

            def output(b, qt):
                pe.wait_ge(c_ready, nth(b, NT, qt + 1))
                for g in range(2):
                    last = three(ps[:, 7, 0:F], c_hi[:, g, :], c_lo[:, g, :], w_hi[:, W_O, g, :], w_lo[:, W_O, g, :],
                                 g == 0, g == 1)
                last.then_inc(o_full, 1)

            with pe.Fori(0, B) as b:
                pe.wait_ge(drained, b + 1)
                transpose_x(b, 0)
                transpose_adj(b, 0, 0)
                pe.wait_ge(x_split, nth(b, 2, 2))
                for j in range(NT):
                    if j + 1 < NT:
                        transpose_adj(b, 0, j + 1)
                    pe.wait_ge(tp_free, nth(b, TP_UNITS, TP_A[0] + 2 * j + 2))
                    for half in range(HALVES):
                        for ft in range(FT):
                            last = transposed_product(ps[:, ACC + 2 * half + ft, :], ft, j, half, j == 0, j == NT - 1)
                last.then_inc(acc_full, 1)
                for t in range(NT):
                    if t == 0:
                        pe.wait_ge(tp_free, nth(b, TP_UNITS, TP_X[0] + 4))
                    dst = pr_bank(b, PR_L0 + t)
                    project(dst[:, 0:F], W_L0X, t)
                    if t % TPH == 0:
                        pe.wait_ge(u_ready, nth(b, 4 + NT // 2, 2 * (t // TPH) + 2))
                    project(dst[:, F:2 * F], W_L0G, t, gh, gl).then_inc(pr_full, 1)

                transpose_x(b, 1)
                for half in range(HALVES):
                    pe.wait_ge(tp_free, nth(b, TP_UNITS, TP_X[1] + 2 * half + 2))
                    dst = pr_bank(b, PR_SI + half)
                    cols_h = slice(half * 512, (half + 1) * 512)
                    for ft in range(FT):
                        last = three(dst, repeated(wsj_hi, ft), repeated(wsj_lo, ft), xt_hi[:, ft, cols_h],
                                     xt_lo[:, ft, cols_h], ft == 0, ft == FT - 1)
                    last.then_inc(pr_full, 1)
                dst = pr_bank(b, PR_SJ)
                for t in range(NT):
                    for ft in range(FT):
                        for part in (xt_hi, xt_lo):
                            last = pe.matmul(dst[:, 2 * t:2 * t + 2], part[:, ft, t * P:(t + 1) * P], wsj_pair[:, ft, :],
                                             start=(ft == 0 and part is xt_hi), stop=(ft == FT - 1 and part is xt_lo))
                last.then_inc(pr_full, 1)
                transpose_adj(b, 1, 0)
                project_pairs(b, PR_V, W_K2, xt_wait(b, 1))
                pe.wait_ge(pr_free, nth(b, PR_UNITS, PR_V + NT // 2))
                transpose_adj(b, 1, 1)
                for j in range(NT):
                    if j + 2 < NT:
                        transpose_adj(b, 1, j + 2)
                    pe.wait_ge(al_ready, nth(b, 2 * NT, 2 * j + 2))
                    for i in range(NT):
                        dst = ps[:, ACC + i // 2, (i % 2) * F:(i % 2 + 1) * F]
                        a_hi, a_lo = t_hi[:, j, i * P:(i + 1) * P], t_lo[:, j, i * P:(i + 1) * P]
                        three(dst, a_hi, a_lo, uh[:, j, :], ul[:, j, :], j == 0 and i % 2 == 0, j == NT - 1, True)
                pe.wait_ge(al_summed, nth(b, NT, NT))
                sums = pr_bank(b, PR_SUM)
                for i in range(NT):
                    last = pe.matmul(sums[:, 2 * i:2 * i + 2], asum[:, i * P:(i + 1) * P], ones_2[:, :],
                                     start=True, stop=True)
                last.then_inc(pr_full, 1)
                project_pairs(b, PR_Z, W_K1, xt_wait(b, 1))
                pe.wait_ge(u_ready, nth(b, 4 + NT // 2, 4 + NT // 2))
                for t in range(NT):
                    project(pr_bank(b, PR_H + t)[:, 0:F], W_K0, t).then_inc(pr_full, 1)
                    row_product(b, t, AF_P2)

                transpose_x(b, 2)
                transpose_adj(b, 2, 0)
                project_pairs(b, PR_G[0], W_G1, xt_wait(b, 2))
                pe.wait_ge(pr_free, nth(b, PR_UNITS, PR_G[0] + NT // 2))
                pe.wait_ge(acc_free, nth(b, 2 * NT, NT))
                for j in range(NT):
                    if j + 1 < NT:
                        transpose_adj(b, 2, j + 1)
                    pe.wait_ge(tp_free, nth(b, TP_UNITS, TP_A[2] + 2 * j + 2))
                    for half in range(HALVES):
                        for ft in range(FT):
                            last = transposed_product(ps[:, ACC + 2 * half + ft, :], ft, j, half, j == 0, j == NT - 1)
                last.then_inc(acc_full, 1)
                h_wait = lambda c: (lambda k: (h_ready, nth(b, 8, 4 * c + (2 if k < NT // 4 else 4))))
                project_pairs(b, PR_G[1], W_G2, h_wait(0))
                pe.wait_ge(pr_free, nth(b, PR_UNITS, PR_G[1] + NT // 2))
                for half in range(HALVES):
                    for ft in range(FT):
                        for j in range(NT):
                            last = transposed_product(ps[:, ACC + 2 * half + ft, :], ft, j, half, j == 0, j == NT - 1)
                        last.then_inc(acc_full, 1)
                project_pairs(b, PR_G[2], W_G3, h_wait(1))
                pe.wait_ge(pr_free, nth(b, PR_UNITS, PR_G[2] + NT // 2))
                for t in range(NT):
                    row_product(b, t, AF_C3)

                transpose_x(b, 3)
                for ft in (1, 0):
                    for m, w in enumerate((W_Q, W_K)):
                        for half in range(HALVES):
                            pe.wait_ge(tp_free, nth(b, TP_UNITS, TP_X[3] + 2 * half + 2))
                            dst = pr_bank(b, PR_QK + 4 * (1 - ft) + 2 * m + half)
                            cols_h = slice(half * 512, (half + 1) * 512)
                            for et in range(FT):
                                last = three(dst, w_hi[:, w, et, ft * P:(ft + 1) * P],
                                             w_lo[:, w, et, ft * P:(ft + 1) * P], xt_hi[:, et, cols_h],
                                             xt_lo[:, et, cols_h], et == 0, et == FT - 1)
                            last.then_inc(pr_full, 1)
                project_pairs(b, PR_VV, W_V, xt_wait(b, 3))
                pe.wait_ge(pr_free, nth(b, PR_UNITS, PR_UNITS))
                for n in range(COPIES):
                    stack_copies(b, n)
                scores(b, 0)
                for s in range(UNITS + 10):
                    if s + 1 < UNITS:
                        scores(b, s + 1)
                    if LAG <= s < UNITS + LAG:
                        transpose_p(b, s - LAG)
                    for part in range(2):
                        if s - part >= LAG + G and (s - part - LAG) % G == 0 and (s - part - LAG) // G <= 2 * NT:
                            context(b, (s - part - LAG) // G - 1, part)
                    if s >= 11 and (s - 11) % H == 0 and (s - 11) // H < NT:
                        denominators(b, (s - 11) // H)
                    if s >= 13 and (s - 13) % H == 0 and (s - 13) // H < NT:
                        spread_denominators(b, (s - 13) // H)
                    if s >= 17 and (s - 17) % H == 0 and (s - 17) // H < NT:
                        output(b, (s - 17) // H)

        @block.scalar
        def _(act):
            copy = lambda dst, src, scale=1.0: nc.scalar.activation(dst, src, ACT.Copy, scale=scale)

            act.wait_ge(set_in, SET_LOADS)
            act.wait_ge(set_const, 9)
            for n, slot in enumerate((W_L0X, W_L0G, W_Q, W_K, W_V, W_O)):
                act.wait_ge(set_pe, n + 1)
                copy(w_hi[:, slot, :, :].rearrange("p k o -> p (k o)"), ps[:, TP + n % 2, :],
                     QSCALE if slot == W_Q else 1.0).then_inc(set_act, 1)
            copy(w_hi[:, W_K0:W_G3 + 1, :, :].rearrange("p w k o -> p (w k o)"),
                 st_nat[:, :, :, :].rearrange("p w k o -> p (w k o)")).then_inc(set_act, 1)
            copy(ones_2[:, :], ones[:, 0:2])
            for k in range(0, 4 * G * HD, P):
                copy(placer[:, k:k + P], ones[:, :], 0.0)
            copy(placer[:, 4 * G * HD:], ones[:, 0:2 * HD], 0.0).then_inc(set_act, 1)
            act.wait_ge(set_act, 8)
            for h in range(G):
                for k in (2, 3):
                    copy(placer[:, (4 * h + k) * HD:(4 * h + k + 1) * HD], ident[:, HD * h:HD * (h + 1)])
            for k in range(2):
                for t in range(FT):
                    last = copy(st_bb[:, k, t, :], ones[:, :], st_bc[:, k, t:t + 1])
            last.then_inc(set_act, 1)
            copy(cols[:, 2, :], cols[:, 2, :], QSCALE).then_inc(set_act, 1)
            act.wait_ge(set_pe, 8)
            wa = ps[:, PR, 0:2 * FT].rearrange("p (t k) -> p t k", k=2)
            copy(wsj_hi[:, :, :], wa).then_inc(set_act, 1)
            act.wait_ge(set_pe, 9)
            copy(bias_k[:, :], ps[:, ACC, 0:F])
            copy(bias_g3[:, :], ps[:, ACC + 1, 0:F])
            copy(bias_o[:, :], ps[:, ACC + 2, 0:F]).then_inc(set_act, 1)
            act.wait_ge(set_dve, 11)
            copy(wsj_pair[:, :, 0], f32(wsj_hi[:, :, 0]))
            copy(wsj_pair[:, :, 1], f32(wsj_lo[:, :, 0]))

            def x_transposed(b, layer):
                for k in range(2 * FT):
                    n, half, ft = TP_X[layer] + k, k // FT, k % FT
                    act.wait_ge(tp_full, nth(b, TP_UNITS, n + 1))
                    copy(xt_hi[:, ft, half * 512:(half + 1) * 512], ps[:, TP + n % 2, :]).then_inc(tp_hi, 1)

            def adj_transposed(b, layer, j):
                for half in range(HALVES):
                    n = TP_A[layer] + j * HALVES + half
                    act.wait_ge(tp_full, nth(b, TP_UNITS, n + 1))
                    copy(t_hi[:, j, half * 512:(half + 1) * 512], ps[:, TP + n % 2, :]).then_inc(tp_hi, 1)

            def rows_from_pr(b, n0, u0):
                for k in range(NT // 2):
                    act.wait_ge(pr_full, nth(b, PR_UNITS, n0 + k + 1))
                    copy(u_hi[:, k * 512:(k + 1) * 512], ps[:, PR + (n0 + k) % 2, :]).then_inc(u_act, 1)

            def hidden(b, c, af):
                for k in range(2 * FT):
                    n, half, ft = 4 * c + k, k // FT, k % FT
                    act.wait_ge(acc_full, nth(b, AF_PER, af(k)))
                    if n >= 2:
                        act.wait_ge(h_ready, nth(b, 8, n - 1))
                    act.activation(ev[:, n % 2, 0:512], ps[:, ACC + k, :], ACT.Relu,
                                   bias=cols[:, c, ft:ft + 1]).then_inc(h_raw, 1)
                    act.wait_ge(h_raw, nth(b, 8, n + 1))
                    copy(xt_hi[:, ft, half * 512:(half + 1) * 512], ev[:, n % 2, 0:512]).then_inc(h_hi, 1)

            def normalise(b, layer, t):
                act.wait_ge(shift_ready, nth(b, 3 * NT, layer * NT + t + 1))
                act.activation(xn[:, t, :], y[:, t % 4, :], ACT.Identity, bias=shift[:, t % 4:t % 4 + 1],
                               scale=rstd[:, t % 4:t % 4 + 1]).then_inc(ln_done, 1)

            with act.Fori(0, B) as b:
                x_transposed(b, 0)
                for h in range(2):
                    act.wait_ge(x_in[h], nth(b, 16, 16))
                    copy(u_hi[:, h * N:(h + 1) * N],
                         xn[:, TPH * h:TPH * (h + 1), :].rearrange("p t f -> p (t f)")).then_inc(x_split_hi, 1)
                for j in range(NT):
                    adj_transposed(b, 0, j)
                act.wait_ge(acc_full, nth(b, AF_PER, AF_L0 + 1))
                for k in range(2 * FT):
                    half, ft = k // FT, k % FT
                    copy(gh[:, ft, half * 512:(half + 1) * 512], ps[:, ACC + k, :]).then_inc(u_act, 1)
                act.wait_ge(deg_ready, nth(b, 2, 1))
                for t in range(NT):
                    n = PR_L0 + t
                    act.wait_ge(pr_full, nth(b, PR_UNITS, n + 1))
                    if t >= 2:
                        act.wait_ge(pr_free, nth(b, PR_UNITS, n - 1))
                    copy(ev[:, t % 2, 0:F], ps[:, PR + n % 2, F:2 * F], rdeg[:, t:t + 1]).then_inc(pr_act, 1)
                    if t >= 2:
                        normalise(b, 0, t - 2)
                for t in (NT - 2, NT - 1):
                    normalise(b, 0, t)

                x_transposed(b, 1)
                act.wait_ge(pr_free, nth(b, PR_UNITS, PR_SI + HALVES))
                act.wait_ge(sj_ready, nth(b, 1, 1))

                def scaled(j):
                    act.activation(e_area[:, 1, j, :], si[:, :], ACT.Identity, bias=sj_scaled[:, j:j + 1],
                                   scale=SLOPE).then_inc(e_scaled, 1)

                def exponential(j):
                    act.wait_ge(e_lin, nth(b, NT, j + 1))
                    act.activation(e_area[:, 1, j, :], e_area[:, 1, j, :], ACT.Exp).then_inc(e_exp, 1)

                scaled(0)
                rows_from_pr(b, PR_V, U_V)
                exponential(0)
                scaled(1)
                exponential(1)
                scaled(2)
                for j in range(NT):
                    act.wait_ge(tp_free, nth(b, TP_UNITS, TP_A[1] + 2 * j + 2))
                    copy(t_hi[:, j, :], ev[:, j % 2, :]).then_inc(al_hi, 1)
                    if j + 2 < NT:
                        exponential(j + 2)
                    if j + 3 < NT:
                        scaled(j + 3)
                for k in range(NT // 2 + 1):
                    if k < NT // 2:
                        n = PR_Z + k
                        act.wait_ge(pr_full, nth(b, PR_UNITS, n + 1))
                        if k >= 2:
                            act.wait_ge(pr_free, nth(b, PR_UNITS, PR_Z + k - 1))
                        copy(ev[:, k % 2, 0:512], ps[:, PR + n % 2, :]).then_inc(pr_act, 1)
                    if k >= 1:
                        act.wait_ge(pr_free, nth(b, PR_UNITS, PR_Z + k))
                        copy(u_hi[:, (k - 1) * 512:k * 512], ev[:, (k - 1) % 2, 512:1024]).then_inc(u_act, 1)

                for t in range(NT):
                    normalise(b, 1, t)

                x_transposed(b, 2)
                adj_transposed(b, 2, 0)
                rows_from_pr(b, PR_G[0], U_C)
                for j in range(1, NT):
                    adj_transposed(b, 2, j)
                hidden(b, 0, lambda k: AF_C1 + 1)
                rows_from_pr(b, PR_G[1], U_C + NT // 2)
                hidden(b, 1, lambda k: AF_C2 + k + 1)
                rows_from_pr(b, PR_G[2], U_C + NT)
                for t in range(NT):
                    normalise(b, 2, t)

                x_transposed(b, 3)
                for k in range(8):
                    ft, m, half = 1 - k // 4, k // 2 % 2, k % 2
                    n = PR_QK + k
                    act.wait_ge(pr_full, nth(b, PR_UNITS, n + 1))
                    act.activation(qk_place(k, u_hi, qk0_hi), ps[:, PR + n % 2, :], ACT.Identity,
                                   bias=cols[:, 2 + m, ft:ft + 1]).then_inc(qk_hi, 1)
                for n in range(0, COPIES, 2):
                    act.wait_ge(copies_full, nth(b, COPIES, n + 1))
                    copy(copies_place(n), ps[0:STACK, ACC + n % 4, :]).then_inc(copies_act, 1)
                for k in range(2):
                    act.wait_ge(qk_out[k], nth(b, 32, 32))
                for s in range(UNITS + 8):
                    if LAG <= s < UNITS + LAG:
                        u = s - LAG
                        act.wait_ge(p_full, nth(b, 2 * UNITS, 2 * u + 2))
                        if u >= PSLOTS:
                            act.wait_ge(ctx_done, nth(b, 2 * NT, (u - PSLOTS) // G + 1))
                        copy(pt[:, u % PSLOTS, TPH:NT, :].rearrange("p t q -> p (t q)"),
                             ps[:, TP + 1, :]).then_inc(p_act, 1)
                    if s < UNITS:
                        qt, h = divmod(s, H)
                        act.wait_ge(neg_max, nth(b, UNITS, s + 1))
                        if h == 0 and qt >= 2:
                            act.wait_ge(rp_ready, nth(b, NT, qt - 1))
                        act.activation(r[:, s % RSLOTS, :], r[:, s % RSLOTS, :], ACT.Exp, bias=nmax[:, s % 4:s % 4 + 1],
                                       accum_out=prow[:, qt % 2, h:h + 1]).then_inc(exp_done, 1)
                    if s >= 11 and (s - 11) % H == 0 and (s - 11) // H < NT:
                        qt = (s - 11) // H
                        act.wait_ge(rt_full, nth(b, NT, qt + 1))
                        copy(rt[:, :], ps[0:H, 7, 0:P]).then_inc(rt_ready, 1)
                    if s >= 13 and (s - 13) % H == 0 and (s - 13) // H < NT:
                        qt = (s - 13) // H
                        act.wait_ge(rbc_full, nth(b, NT, qt + 1))
                        if qt >= 1:
                            act.wait_ge(c_raw, nth(b, NT, qt))
                        copy(rbc[:, :, :].rearrange("p g q -> p (g q)"), ps[:, 7, 0:2 * P]).then_inc(rbc_ready, 1)
                    if s >= 15 and (s - 15) % H == 0 and (s - 15) // H < NT:
                        qt = (s - 15) // H
                        act.wait_ge(c_raw, nth(b, NT, qt + 1))
                        if qt >= 1:
                            act.wait_ge(o_full, nth(b, NT, qt))
                        copy(c_hi[:, :, :], c_f[:, :, :]).then_inc(c_hi_ready, 1)

        @block.vector
        def _(dve):
            dve.wait_ge(set_in, SET_LOADS)
            for n, slot in enumerate((W_L0X, W_L0G, W_Q, W_K, W_V, W_O)):
                dve.wait_ge(set_act, n + 1)
                scale = QSCALE if slot == W_Q else 1.0
                dve.scalar_tensor_tensor(out=w_lo[:, slot, :, :].rearrange("p k o -> p (k o)"),
                                         in0=ps[:, TP + n % 2, :], scalar=scale,
                                         in1=f32(w_hi[:, slot, :, :].rearrange("p k o -> p (k o)")),
                                         op0=ALU.mult, op1=ALU.subtract).then_inc(set_dve, 1)
            dve.wait_ge(set_pe, 7)
            dve.tensor_copy(st_wvt[:, :, :].rearrange("p k o -> p (k o)"), ps[:, TP, :]).then_inc(set_dve, 1)
            dve.memset(st_ab[:, 1:2], 0.0).then_inc(set_dve, 1)
            dve.wait_ge(set_act, 7)
            dve.tensor_tensor(w_lo[:, W_K0:W_G3 + 1, :, :].rearrange("p w k o -> p (w k o)"),
                              st_nat[:, :, :, :].rearrange("p w k o -> p (w k o)"),
                              f32(w_hi[:, W_K0:W_G3 + 1, :, :].rearrange("p w k o -> p (w k o)")),
                              ALU.subtract).then_inc(set_dve, 1)
            dve.wait_ge(set_act, 11)
            dve.tensor_tensor(wsj_lo[:, :, :], ps[:, PR, 0:2 * FT].rearrange("p (t k) -> p t k", k=2),
                              f32(wsj_hi[:, :, :]), ALU.subtract).then_inc(set_dve, 1)
            dve.tensor_reduce(e_const[:, :], ps[:, PR, 8:10], AX.X, ALU.add).then_inc(set_dve, 1)
            dve.wait_ge(set_act, 12)
            dve.wait_ge(set_dve, 11)
            dve.memset(vare[:, :], 0.0).then_inc(drained, 1)

            def alone():
                dve.sem_inc(passed, 1)

            def rest(dst, value, hi, done):
                dve.tensor_tensor(dst, value, f32(hi), ALU.subtract).then_inc(done, 1)

            def x_transposed(b, layer):
                for k in range(2 * FT):
                    n, half, ft = TP_X[layer] + k, k // FT, k % FT
                    at = slice(half * 512, (half + 1) * 512)
                    dve.wait_ge(tp_hi, nth(b, TP_UNITS - 2 * NT, hi_at(n)))
                    dve.tensor_tensor(xt_lo[:, ft, at], ps[:, TP + n % 2, :], f32(xt_hi[:, ft, at]),
                                      ALU.subtract).then_inc(tp_free, 1)

            def hi_at(n):
                return n + 1 - (2 * NT if n >= TP_A[1] else 0)

            def adj_transposed(b, layer, j):
                for half in range(HALVES):
                    n = TP_A[layer] + j * HALVES + half
                    at = slice(half * 512, (half + 1) * 512)
                    dve.wait_ge(tp_hi, nth(b, TP_UNITS - 2 * NT, hi_at(n)))
                    dve.tensor_tensor(t_lo[:, j, at], ps[:, TP + n % 2, :], f32(t_hi[:, j, at]),
                                      ALU.subtract).then_inc(tp_free, 1)

            def rows_from_pr(b, n0, u0):
                for k in range(NT // 2):
                    at = slice(k * 512, (k + 1) * 512)
                    dve.wait_ge(u_act, nth(b, U_PER, u0 + k + 1))
                    dve.tensor_tensor(u_lo[:, at], ps[:, PR + (n0 + k) % 2, :], f32(u_hi[:, at]),
                                      ALU.subtract).then_inc(pr_free, 1)

            def tile_stats(b, layer, t):
                raw_stats(b, layer, t)
                mean_variance(b, layer, t)

            def raw_stats(b, layer, t):
                src = y[:, t % 4, :] if layer < 3 else xr[:, t % 2, :]
                dve.wait_ge(y_ready, nth(b, LN_PER, layer * NT + t + 1))
                dve.bn_stats(stats[:, t % 4, :], src).then_inc(bn_raw, 1)

            def mean_variance(b, layer, t):
                dve.wait_ge(bn_raw, nth(b, LN_PER, layer * NT + t + 1))
                alone()
                dve.bn_aggr(mv[:, t % 4, :], stats[:, t % 4, :]).then_inc(stat_ready, 1)

            def normalise(b, layer, t):
                dve.wait_ge(rstd_ready, nth(b, LN_PER, layer * NT + t + 1))
                dve.tensor_scalar(xr[:, t % 2, :], xr[:, t % 2, :], mv[:, t % 4, 0:1], rstd[:, t % 4:t % 4 + 1],
                                  ALU.subtract, ALU.mult).then_inc(ln_done, 1)

            def y_free(b, layer, t):
                if t >= 4:
                    dve.wait_ge(ln_done, nth(b, LN_PER, layer * NT + t - 3))

            def relu_residual(b, layer, t):
                y_free(b, layer, t)
                dve.scalar_tensor_tensor(out=y[:, t % 4, :], in0=ev[:, t % 2, F:2 * F], scalar=0.0, in1=xn[:, t, :],
                                         op0=ALU.max, op1=ALU.add).then_inc(y_ready, 1)

            def hidden(b, c):
                for k in range(2 * FT):
                    n, half, ft = 4 * c + k, k // FT, k % FT
                    at = slice(half * 512, (half + 1) * 512)
                    dve.wait_ge(h_hi, nth(b, 8, n + 1))
                    rest(xt_lo[:, ft, at], ev[:, n % 2, 0:512], xt_hi[:, ft, at], h_ready)

            with dve.Fori(0, B) as b:
                x_transposed(b, 0)
                dve.wait_ge(xr_free, b + 1)
                for h in range(2):
                    at = slice(h * N, (h + 1) * N)
                    dve.wait_ge(x_split_hi, nth(b, 2, h + 1))
                    rest(u_lo[:, at], xn[:, TPH * h:TPH * (h + 1), :].rearrange("p t f -> p (t f)"), u_hi[:, at], x_split)
                for j in range(NT):
                    adj_transposed(b, 0, j)
                    dve.tensor_reduce(rsum[:, j:j + 1], adjn[:, j, :], AX.X, ALU.add).then_inc(deg_sum, 1)
                dve.wait_ge(deg_sum, nth(b, NT + 1, NT))
                dve.tensor_scalar(rsum[:, :], rsum[:, :], EPS_DEG, None, ALU.max).then_inc(deg_sum, 1)
                dve.wait_ge(deg_sum, nth(b, NT + 1, NT + 1))
                dve.reciprocal(rdeg[:, :], rsum[:, :]).then_inc(deg_ready, 1)
                for k in range(2 * FT):
                    half, ft = k // FT, k % FT
                    at = slice(half * 512, (half + 1) * 512)
                    dve.wait_ge(u_act, nth(b, U_PER, U_G + k + 1))
                    rest(gl[:, ft, at], ps[:, ACC + k, :], gh[:, ft, at], u_ready)
                for t in range(NT + 1):
                    if t < NT:
                        n = PR_L0 + t
                        dve.wait_ge(pr_act, nth(b, NT + NT // 2, t + 1))
                        dve.tensor_tensor(ev[:, t % 2, F:2 * F], ps[:, PR + n % 2, 0:F], ev[:, t % 2, 0:F],
                                          ALU.add).then_inc(pr_free, 1)
                    if t >= 1:
                        raw_stats(b, 0, t - 1)
                    if t < NT:
                        dve.wait_ge(pr_free, nth(b, PR_UNITS, n + 1))
                        relu_residual(b, 0, t)
                    if t >= 1:
                        mean_variance(b, 0, t - 1)

                x_transposed(b, 1)
                for half in range(HALVES):
                    n = PR_SI + half
                    dve.wait_ge(pr_full, nth(b, PR_UNITS, n + 1))
                    dve.tensor_scalar(si[:, half * 512:(half + 1) * 512], ps[:, PR + n % 2, :], e_const[:, 0:1], None,
                                      ALU.add).then_inc(pr_free, 1)
                dve.wait_ge(pr_full, nth(b, PR_UNITS, PR_SJ + 1))
                dve.tensor_reduce(sj[:, :], ps[:, PR + PR_SJ % 2, 0:2 * NT].rearrange("p (t k) -> p t k", k=2),
                                  AX.X, ALU.add).then_inc(pr_free, 1)
                dve.wait_ge(pr_free, nth(b, PR_UNITS, PR_SJ + 1))
                dve.tensor_scalar(sj_scaled[:, :], sj[:, :], SLOPE, None, ALU.mult).then_inc(sj_ready, 1)

                def linear(j):
                    dve.wait_ge(e_scaled, nth(b, NT, j + 1))
                    dve.scalar_tensor_tensor(out=e_area[:, 1, j, :], in0=si[:, :], scalar=sj[:, j:j + 1],
                                             in1=e_area[:, 1, j, :], op0=ALU.add, op1=ALU.max).then_inc(e_lin, 1)

                def alpha_rest(j):
                    dve.wait_ge(al_hi, nth(b, NT, j + 1))
                    for half in range(HALVES):
                        at = slice(half * 512, (half + 1) * 512)
                        rest(t_lo[:, j, at], ev[:, j % 2, at], t_hi[:, j, at], al_ready)

                linear(0)
                rows_from_pr(b, PR_V, U_V)
                linear(1)
                for j in range(NT):
                    dve.wait_ge(e_exp, nth(b, NT, j + 1))
                    if j >= 2:
                        dve.wait_ge(al_ready, nth(b, 2 * NT, 2 * (j - 2) + 2))
                        dve.wait_ge(al_summed, nth(b, NT, j - 1))
                    for half in range(HALVES):
                        n = TP_A[1] + 2 * j + half
                        at = slice(half * 512, (half + 1) * 512)
                        dve.wait_ge(tp_full, nth(b, TP_UNITS, n + 1))
                        dve.tensor_tensor(ev[:, j % 2, at], ps[:, TP + n % 2, :], e_area[:, 1, j, at],
                                          ALU.mult).then_inc(tp_free, 1)
                    if j >= 1:
                        alpha_rest(j - 1)
                    if j + 2 < NT:
                        linear(j + 2)
                alpha_rest(NT - 1)
                dve.wait_ge(pr_full, nth(b, PR_UNITS, PR_SUM + 1))
                dve.tensor_scalar(rsum[:, :], ps[:, PR + PR_SUM % 2, 0:2 * NT].rearrange("p (t k) -> p t k", k=2)[:, :, 0],
                                  EPS_ROW, None, ALU.add).then_inc(pr_free, 1)
                dve.wait_ge(pr_free, nth(b, PR_UNITS, PR_SUM + 1))
                dve.reciprocal(rdeg[:, :], rsum[:, :]).then_inc(deg_ready, 1)
                dve.wait_ge(deg_ready, nth(b, 2, 2))
                for k in range(NT // 2 + 1):
                    if k < NT // 2:
                        dve.wait_ge(pr_act, nth(b, NT + NT // 2, NT + k + 1))
                        if k >= 2:
                            dve.wait_ge(u_ready, nth(b, 4 + NT // 2, 4 + k - 1))
                        for s in range(2):
                            t = 2 * k + s
                            last = dve.scalar_tensor_tensor(
                                out=ev[:, k % 2, 512 + s * F:512 + (s + 1) * F],
                                in0=ps[:, ACC + k, s * F:(s + 1) * F], scalar=rdeg[:, t:t + 1],
                                in1=ev[:, k % 2, s * F:(s + 1) * F], op0=ALU.mult, op1=ALU.add)
                        last.then_inc(pr_free, 1)
                    if k >= 1:
                        at = slice((k - 1) * 512, k * 512)
                        dve.wait_ge(u_act, nth(b, U_PER, U_Z + k))
                        rest(u_lo[:, at], ev[:, (k - 1) % 2, 512:1024], u_hi[:, at], u_ready)
                for t in range(NT + 1):
                    if t < NT:
                        n = PR_H + t
                        dve.wait_ge(pr_full, nth(b, PR_UNITS, n + 1))
                        dve.tensor_tensor(ev[:, t % 2, 0:F], ps[:, PR + n % 2, 0:F], bias_k[:, :],
                                          ALU.add).then_inc(pr_free, 1)
                        dve.wait_ge(pr_free, nth(b, PR_UNITS, n + 1))
                        dve.wait_ge(acc_full, nth(b, AF_PER, AF_P2 + t + 1))
                        dve.scalar_tensor_tensor(out=ev[:, t % 2, F:2 * F], in0=ps[:, ACC + t % 4, 0:F],
                                                 scalar=rdeg[:, t:t + 1], in1=ev[:, t % 2, 0:F], op0=ALU.mult,
                                                 op1=ALU.add).then_inc(acc_free, 1)
                        dve.wait_ge(acc_free, nth(b, 2 * NT, t + 1))
                        relu_residual(b, 1, t)
                        tile_stats(b, 1, t)

                x_transposed(b, 2)
                adj_transposed(b, 2, 0)
                rows_from_pr(b, PR_G[0], U_C)
                for j in range(1, NT):
                    adj_transposed(b, 2, j)
                hidden(b, 0)
                rows_from_pr(b, PR_G[1], U_C + NT // 2)
                hidden(b, 1)
                rows_from_pr(b, PR_G[2], U_C + NT)
                for t in range(NT + 1):
                    if t < NT:
                        dve.wait_ge(acc_full, nth(b, AF_PER, AF_C3 + t + 1))
                        dve.tensor_tensor(ev[:, t % 2, 0:F], ps[:, ACC + t % 4, 0:F], bias_g3[:, :],
                                          ALU.add).then_inc(acc_free, 1)
                        dve.wait_ge(acc_free, nth(b, 2 * NT, NT + t + 1))
                        y_free(b, 2, t)
                        dve.tensor_tensor(y[:, t % 4, :], ev[:, t % 2, 0:F], xn[:, t, :], ALU.add).then_inc(y_ready, 1)
                        tile_stats(b, 2, t)

                x_transposed(b, 3)
                for k in range(8):
                    ft, m, half = 1 - k // 4, k // 2 % 2, k % 2
                    n = PR_QK + k
                    dve.wait_ge(qk_hi, nth(b, 8, k + 1))
                    dve.scalar_tensor_tensor(out=qk_place(k, u_lo, qk0_lo), in0=ps[:, PR + n % 2, :],
                                             scalar=cols[:, 2 + m, ft:ft + 1], in1=f32(qk_place(k, u_hi, qk0_hi)),
                                             op0=ALU.add, op1=ALU.subtract).then_inc(pr_free, 1)
                dve.wait_ge(spilled, nth(b, 16 * NT, 16 * NT))
                for k in range(NT // 2):
                    n = PR_VV + k
                    dve.wait_ge(pr_full, nth(b, PR_UNITS, n + 1))
                    dve.tensor_copy(xn[:, 2 * k:2 * k + 2, :].rearrange("p t f -> p (t f)"),
                                    ps[:, PR + n % 2, :]).then_inc(pr_free, 1)
                for n in range(1, COPIES, 2):
                    dve.wait_ge(copies_full, nth(b, COPIES, n + 1))
                    dve.tensor_copy(copies_place(n), ps[0:STACK, ACC + n % 4, :]).then_inc(copies_dve, 1)
                for k in range(2):
                    dve.wait_ge(qk_out[k], nth(b, 32, 32))
                for s in range(UNITS + 13):
                    if s < UNITS:
                        qt, h = divmod(s, H)
                        dve.wait_ge(s_full, nth(b, UNITS, s + 1))
                        if s >= RSLOTS:
                            dve.wait_ge(p_full, nth(b, 2 * UNITS, 2 * (s - RSLOTS) + 2))
                        if s >= 4:
                            dve.wait_ge(neg_max, nth(b, UNITS, s - 3))
                        alone()
                        dve.tensor_tensor_reduce(
                            out=r[:, s % RSLOTS, :], in0=ps[:, 2 * (s % 2):2 * (s % 2) + 2, :].rearrange("p a c -> p (a c)"),
                            in1=adjn[:, qt, :], scale=1.0, scalar=-3.0e38, op0=ALU.mult, op1=ALU.max,
                            accum_out=mmax[:, s % 4:s % 4 + 1]).then_inc(masked, 1)
                    if LAG <= s < UNITS + LAG:
                        u = s - LAG
                        dve.wait_ge(p_full, nth(b, 2 * UNITS, 2 * u + 1))
                        if u >= PSLOTS:
                            dve.wait_ge(ctx_done, nth(b, 2 * NT, (u - PSLOTS) // G + 1))
                        dve.tensor_copy(pt[:, u % PSLOTS, 0:TPH, :].rearrange("p t q -> p (t q)"),
                                        ps[:, TP, :]).then_inc(p_dve, 1)
                    if s >= 8 and (s - 8) % H == 0 and (s - 8) // H < NT:
                        qt = (s - 8) // H
                        dve.wait_ge(exp_done, nth(b, UNITS, H * (qt + 1)))
                        if qt >= 2:
                            dve.wait_ge(rt_full, nth(b, NT, qt - 1))
                        dve.reciprocal(rprow[:, qt % 2, :], prow[:, qt % 2, :]).then_inc(rp_ready, 1)
                    if s >= 14 and (s - 14) % H == 0 and (s - 14) // H < NT:
                        qt = (s - 14) // H
                        dve.wait_ge(rbc_ready, nth(b, NT, qt + 1))
                        dve.wait_ge(ctx_done, nth(b, 2 * NT, 2 * qt + 2))
                        dve.tensor_tensor(c_f[:, :, :].rearrange("p g q -> p (g q)"), ps[:, 6, 0:2 * P],
                                          rbc[:, :, :].rearrange("p g q -> p (g q)"), ALU.mult).then_inc(c_raw, 1)
                    if s >= 16 and (s - 16) % H == 0 and (s - 16) // H < NT:
                        qt = (s - 16) // H
                        dve.wait_ge(c_hi_ready, nth(b, NT, qt + 1))
                        rest(c_lo[:, :, :], c_f[:, :, :], c_hi[:, :, :], c_ready)
                    if s >= 18 and (s - 18) % H == 0 and (s - 18) // H < NT:
                        qt = (s - 18) // H
                        dve.wait_ge(o_full, nth(b, NT, qt + 1))
                        dve.wait_ge(xr_in[qt % 2], nth(b, 8 * NT, 16 * (qt // 2 + 1)))
                        dve.tensor_tensor(xr[:, qt % 2, :], ps[:, 7, 0:F], xr[:, qt % 2, :],
                                          ALU.add).then_inc(h_sum, 1)
                        dve.wait_ge(h_sum, nth(b, NT, qt + 1))
                        if qt == NT - 1:
                            dve.sem_inc(drained, 1)
                        dve.tensor_tensor(xr[:, qt % 2, :], xr[:, qt % 2, :], bias_o[:, :], ALU.add).then_inc(y_ready, 1)
                        tile_stats(b, 3, qt)
                    if s >= 20 and (s - 20) % H == 0 and (s - 20) // H < NT:
                        normalise(b, 3, (s - 20) // H)


def kernel(**inputs):
    import numpy as np
    import concourse.bacc as bacc
    from concourse.bass_utils import run_bass_kernel_spmd

    nc = bacc.Bacc("TRN2", target_bir_lowering=False, num_devices=1)
    nc.disable_value_cache = True
    arrays, drams = {}, {}
    for name, value in inputs.items():
        a = np.ascontiguousarray(value)
        arrays[f"in_{name}"] = a
        drams[name] = nc.dram_tensor(f"in_{name}", a.shape, mybir.dt.from_np(a.dtype), kind="ExternalInput").ap()
    shape = arrays["in_x"].shape
    out = nc.dram_tensor("out", shape, F32, kind="ExternalOutput").ap()
    build_program(nc, drams, out)
    got = run_bass_kernel_spmd(nc, [arrays], core_ids=[0])
    return got.results[0]["out"]
```

```python
from contextlib import ExitStack

import concourse.bass as bass
from concourse import mybir

F32 = mybir.dt.float32
F32R = mybir.dt.float32r
ALU = mybir.AluOpType
ACT = mybir.ActivationFunctionType
AX = mybir.AxisListType

P = 128


def build_program(nc: bass.Bass, d: dict, out: bass.AP):
    B, N, F = d["x"].shape
    NT = N // P
    FT = F // P
    HALVES = N // 512
    TPH = NT // HALVES
    H = 8
    HD = F // H
    G = P // HD
    UNITS = NT * H
    EPS_DEG, EPS_ROW, EPS_LN = 1e-6, 1e-12, 1e-5
    SLOPE = 0.2
    LAG = 3
    QSCALE = 2.0 * HD ** -0.5

    STACK = 3 * HD
    COPIES = 2 * G * HALVES

    W_L0X, W_L0G, W_K0, W_K1, W_K2, W_G1, W_G2, W_G3, W_Q, W_K, W_V, W_O = range(12)

    TP_UNITS = 4 * 4 + 3 * HALVES * NT
    PAIRS = NT // 2
    QK = [(1, 0, 0), (1, 1, 0), (0, 0, 0), (1, 0, 1), (1, 1, 1), (0, 1, 0), (0, 0, 1), (0, 1, 1)]
    PR_ORDER = ([("layer 0", t) for t in range(NT)] +
                [("si", 0), ("sj", 0), ("v", 0), ("v", 1), ("si", 1)] + [("v", k) for k in range(2, PAIRS)] + [("sj", 1)] +
                [("z", k) for k in range(PAIRS)] + [("h", t) for t in range(NT)] +
                [(f"conv {c}", k) for c in range(3) for k in range(PAIRS)] +
                [("qk", part) for part in QK] + [("values", k) for k in range(PAIRS)])
    pr = {unit: n for n, unit in enumerate(PR_ORDER)}
    PR_UNITS = len(PR_ORDER)

    x_d = d["x"].rearrange("b (t p) f -> b p t f", p=P)
    adj_d = d["adj"].rearrange("b (t p) m -> b t p m", p=P)
    out_d = out.rearrange("b (t p) f -> b t p f", p=P)
    x3_d = nc.dram_tensor("x3_spill", [NT, P, F], F32, kind="Internal").ap()
    qk_d = nc.dram_tensor("qk_spill", [2, 2, P, N], F32, kind="Internal").ap()

    with ExitStack() as ctx:
        def sb(name, shape, dt=F32, stack=ctx):
            return stack.enter_context(nc.sbuf_tensor(name, shape, dt))

        def sem(name):
            return ctx.enter_context(nc.semaphore(name))

        placer = sb("placer", [P, (4 * G + 2) * HD], F32R)
        ident = sb("ident", [P, P])[:, :]
        ones_2 = sb("ones_2", [P, 2])
        expo = sb("expo", [P, 1])
        eps_ln = sb("eps_ln", [P, 1])
        zero = sb("zero", [P, 1])
        w_hi = sb("w_hi", [P, 12, FT, F], F32R)
        w_lo = sb("w_lo", [P, 12, FT, F], F32R)
        wsj_hi = sb("wsj_hi", [P, FT, 2], F32R)
        wsj_lo = sb("wsj_lo", [P, FT, 2], F32R)
        wsj_pair = sb("wsj_pair", [P, FT, 2], F32R)
        e_const = sb("e_const", [P, 1])
        cols = sb("cols", [P, 4, FT])
        bias_k = sb("bias_k", [P, F])
        bias_g3 = sb("bias_g3", [P, F])
        bias_o = sb("bias_o", [P, F])
        sel = sb("sel", [H, 2, P])
        adjn = sb("adjn", [P, NT, N])
        xn = sb("xn", [P, NT, F])
        stats = sb("stats", [P, 4, 6])
        mv = sb("mv", [P, 4, 2])
        vare = sb("vare", [P, 4])
        rstd = sb("rstd", [P, 4])
        nmean = sb("nmean", [P, 4])
        shift = sb("shift", [P, 4])
        rdeg = sb("rdeg", [P, NT])
        rsum = sb("rsum", [P, NT])
        sj = sb("sj", [P, NT])
        sj_scaled = sb("sj_scaled", [P, NT])
        nmax = sb("nmax", [P, 4])
        mmax = sb("mmax", [P, 4])
        prow = sb("prow", [P, 2, H])
        rprow = sb("rprow", [P, 2, H])

        with ExitStack() as s:
            t_hi = sb("t_hi", [P, NT, N], F32R, s)
            t_lo = sb("t_lo", [P, NT, N], F32R, s)
        with ExitStack() as s:
            e_area = sb("e_area", [P, 2, NT, N], F32, s)
        with ExitStack() as s:
            q_stack = sb("q_stack", [P, H, N], F32R, s)
            k_stack = sb("k_stack", [P, H, N], F32R, s)
        with ExitStack() as s:
            ones = sb("ones", [P, P], F32, s)
            st_w0 = sb("st_w0", [P, FT, 2 * F], F32, s)
            st_nat = sb("st_nat", [P, 6, FT, F], F32, s)
            st_sq = sb("st_sq", [P, 5, FT, F], F32, s)
            st_wvt = sb("st_wvt", [P, FT, F], F32, s)
            st_aw = sb("st_aw", [P, FT, 2], F32, s)
            st_bc = sb("st_bc", [P, 2, FT], F32, s)
            st_bb = sb("st_bb", [P, 2, FT, P], F32, s)
            st_bk = sb("st_bk", [3, F], F32, s)
            st_row = sb("st_row", [1, 2, F], F32, s)
            st_ab = sb("st_ab", [1, 2], F32, s)
        ctx.enter_context(nc.sbuf_tensor("t_area", [P, 2 * NT * N], F32))

        with ExitStack() as s:
            xt_hi = sb("xt_hi", [P, FT, N], F32R, s)
            xt_lo = sb("xt_lo", [P, FT, N], F32R, s)
            u_hi = sb("u_hi", [P, NT * F], F32R, s)
            u_lo = sb("u_lo", [P, NT * F], F32R, s)
        PSLOTS, RSLOTS = 6, 4
        with ExitStack() as s:
            pt = sb("pt", [P, PSLOTS, NT, P], F32, s)
            c_f = sb("c_f", [P, 2, P], F32, s)
            c_hi = sb("c_hi", [P, 2, P], F32R, s)
            c_lo = sb("c_lo", [P, 2, P], F32R, s)
            rbc = sb("rbc", [P, 2, P], F32, s)
            rt = sb("rt", [H, P], F32, s)
            xr = sb("xr", [P, 2, F], F32, s)
        ctx.enter_context(nc.sbuf_tensor("u_area", [P, 4 * NT * F], F32))

        with ExitStack() as s:
            r = sb("r", [P, RSLOTS, N], F32, s)
        with ExitStack() as s:
            si = sb("si", [P, N], F32, s)
            ev = sb("ev", [P, 2, N], F32, s)
            asum = sb("asum", [P, N], F32, s)
        with ExitStack() as s:
            qk0_hi = sb("qk0_hi", [P, 2, N], F32R, s)
            qk0_lo = sb("qk0_lo", [P, 2, N], F32R, s)
        with ExitStack() as s:
            y = sb("y", [P, 4, F], F32, s)
        ctx.enter_context(nc.sbuf_tensor("r_area", [P, RSLOTS * N], F32))

        ps = ctx.enter_context(nc.psum_tensor("ps", [P, 8, 512], F32))
        ACC, TP, PR = 0, 4, 6

        uh = u_hi[:, :].rearrange("p (t f) -> p t f", f=F)
        ul = u_lo[:, :].rearrange("p (t f) -> p t f", f=F)
        gh = u_hi[:, :].rearrange("p (t n) -> p t n", n=N)
        gl = u_lo[:, :].rearrange("p (t n) -> p t n", n=N)
        f32 = lambda ap: ap.bitcast(F32)

        set_in = sem("set_in")
        set_const = sem("set_const")
        set_pe = sem("set_pe")
        set_act = sem("set_act")
        set_dve = sem("set_dve")
        adj_in = [sem(f"adj_in{t}") for t in range(NT)]
        x_in = [sem(f"x_in{h}") for h in range(2)]
        passed = sem("passed")
        drained = sem("drained")
        x_split_hi = sem("x_split_hi")
        x_split = sem("x_split")
        tp_full = sem("tp_full")
        tp_hi = sem("tp_hi")
        tp_free = sem("tp_free")
        deg_sum = sem("deg_sum")
        deg_ready = sem("deg_ready")
        acc_full = sem("acc_full")
        acc_free = sem("acc_free")
        pr_full = sem("pr_full")
        pr_act = sem("pr_act")
        pr_free = sem("pr_free")
        u_act = sem("u_act")
        u_ready = sem("u_ready")
        e_lin = sem("e_lin")
        e_scaled = sem("e_scaled")
        e_exp = sem("e_exp")
        al_hi = sem("al_hi")
        al_ready = sem("al_ready")
        al_summed = sem("al_summed")
        sums_full = sem("sums_full")
        hop_full = sem("hop_full")
        sums_read = sem("sums_read")
        sj_ready = sem("sj_ready")
        h_sum = sem("h_sum")
        y_ready = sem("y_ready")
        bn_raw = sem("bn_raw")
        xr_free = sem("xr_free")
        h_raw = sem("h_raw")
        h_hi = sem("h_hi")
        h_ready = sem("h_ready")
        stat_ready = sem("stat_ready")
        var_ready = sem("var_ready")
        rstd_ready = sem("rstd_ready")
        neg_mean = sem("neg_mean")
        xr_biased = sem("xr_biased")
        shift_ready = sem("shift_ready")
        ln_done = sem("ln_done")
        spilled = sem("spilled")
        qk_hi = sem("qk_hi")
        qk_out = [sem(f"qk_out{k}") for k in range(2)]
        stacked = [sem(f"stacked{k}") for k in range(2)]
        copies_full = sem("copies_full")
        copies_act = sem("copies_act")
        copies_dve = sem("copies_dve")
        s_full = sem("s_full")
        masked = sem("masked")
        neg_max = sem("neg_max")
        exp_done = sem("exp_done")
        p_full = sem("p_full")
        p_act = sem("p_act")
        p_dve = sem("p_dve")
        ctx_done = sem("ctx_done")
        rp_ready = sem("rp_ready")
        rt_full = sem("rt_full")
        rt_ready = sem("rt_ready")
        rbc_full = sem("rbc_full")
        rbc_ready = sem("rbc_ready")
        c_raw = sem("c_raw")
        c_hi_ready = sem("c_hi_ready")
        c_ready = sem("c_ready")
        o_full = sem("o_full")
        xr_in = [sem(f"xr_in{k}") for k in range(2)]
        out_done = [sem(f"out_done{k}") for k in range(2)]

        def nth(b, per, n):
            return b * per + n

        def qk_place(part, staged, kept):
            ft, m, half = part
            return (staged[:, m * N + half * 512:m * N + (half + 1) * 512] if ft == 1 else
                    kept[:, m, half * 512:(half + 1) * 512])

        def copies_place(n):
            h, m, half = n // 4, n // 2 % 2, n % 2
            return (q_stack, k_stack)[m][0:STACK, h, half * 512:(half + 1) * 512]

        def tp_x(layer, half):
            first = layer * (4 + 2 * NT)
            return first + (2 * NT if layer == 0 else 0) + (4 if layer == 2 else 2) * half

        def tp_a(layer, j):
            first = layer * (4 + 2 * NT)
            return first + (2 * j if layer == 0 else 2 if layer == 2 and j == 0 else 4 + 2 * j)

        AF_L0, AF_P2, AF_C1, AF_C2, AF_C3, AF_PER = 0, 4, 4 + NT, 8 + NT, 12 + NT, 12 + 2 * NT
        U_G, U_V, U_Z, U_C, U_PER = 0, 4, 4 + PAIRS, 4 + 2 * PAIRS, 4 + 5 * PAIRS
        LN_PER = 4 * NT

        block = ctx.enter_context(nc.Block())

        @block.sync
        def _(sp):
            sp.dma_start(st_w0[:, :, :], d["L0_gnn_W"].rearrange("(t p) k -> p t k", p=P)).then_inc(set_in, 16)
            sp.dma_start(st_nat[:, 0:3, :, :].rearrange("p k t n -> p (k t) n"),
                         d["L1_gnn_Wk"].rearrange("k (t p) n -> p (k t) n", p=P)).then_inc(set_in, 16)
            for k, name in enumerate(("L2_gnn_W1", "L2_gnn_W2", "L2_gnn_W3")):
                sp.dma_start(st_nat[:, 3 + k, :, :], d[name].rearrange("(t p) n -> p t n", p=P)).then_inc(set_in, 16)
            for k, name in enumerate(("L3_gnn_Wq", "L3_gnn_Wk", "L3_gnn_Wv", "L3_gnn_Wo", "L1_gnn_Wv")):
                sp.dma_start(st_sq[:, k, :, :], d[name].rearrange("(t p) n -> p t n", p=P)).then_inc(set_in, 16)
            with nc.allow_non_contiguous_dma("bias columns, once"):
                for k in range(2):
                    sp.dma_start(st_aw[:, :, k], d["L1_gnn_aw"][k * F:(k + 1) * F, :]
                                 .rearrange("(t p) o -> p (t o)", p=P)).then_inc(set_in, 16)
                for k, name in enumerate(("L1_gnn_bv", "L3_gnn_bv")):
                    sp.dma_start(st_bc[:, k, :], d[name].rearrange("(t p) -> p t", p=P)).then_inc(set_in, 16)
                for k, name in enumerate(("L2_gnn_b1", "L2_gnn_b2", "L3_gnn_bq", "L3_gnn_bk")):
                    sp.dma_start(cols[:, k, :], d[name].rearrange("(t p) -> p t", p=P)).then_inc(set_in, 16)
            sp.dma_start(st_bk[:, :], d["L1_gnn_bk"]).then_inc(set_in, 16)
            sp.dma_start(st_row[:, 0, :], d["L2_gnn_b3"].rearrange("(a n) -> a n", a=1)).then_inc(set_in, 16)
            sp.dma_start(st_row[:, 1, :], d["L3_gnn_bo"].rearrange("(a n) -> a n", a=1)).then_inc(set_in, 16)
            sp.dma_start(st_ab[:, 0:1], d["L1_gnn_ab"].rearrange("(a n) -> a n", a=1)).then_inc(set_in, 16)
            for h in range(2):
                sp.dma_start(xn[:, TPH * h:TPH * (h + 1), :], x_d[0, :, TPH * h:TPH * (h + 1), :]).then_inc(x_in[h], 16)
            for t in range(NT):
                sp.dma_start(adjn[:, t, :], adj_d[0, t]).then_inc(adj_in[t], 16)

            def element(b, last):
                for t in range(NT):
                    sp.wait_ge(ln_done, nth(b, LN_PER, 2 * NT + t + 1))
                    sp.dma_start(x3_d[t], xn[:, t, :]).then_inc(spilled, 16)
                for n in range(2):
                    sp.wait_ge(pr_free, nth(b, PR_UNITS, pr["qk", (1, n, 1)] + 1))
                    at = slice(n * N, (n + 1) * N)
                    sp.dma_start(qk_d[n, 0], f32(u_hi[:, at])).then_inc(qk_out[n], 16)
                    sp.dma_start(qk_d[n, 1], f32(u_lo[:, at])).then_inc(qk_out[n], 16)
                    sp.wait_ge(qk_out[n], nth(b, 32, 32))
                    hi, lo = (qk_d[n, k].rearrange("(g p) n -> p g n", p=HD) for k in range(2))
                    stack = q_stack if n == 0 else k_stack
                    for part, src in enumerate((hi, hi, lo) if n == 0 else (lo, hi, hi)):
                        sp.dma_start(f32(stack[HD * part:HD * (part + 1), G:2 * G, :]),
                                     src).then_inc(stacked[n], 16)
                for t in range(NT):
                    if t == 0:
                        sp.wait_ge(spilled, nth(b, 16 * NT, 16 * NT))
                    if t >= 2:
                        store(b, t - 2)
                        sp.wait_ge(out_done[t % 2], nth(b, 8 * NT, 16 * (t // 2)))
                    sp.dma_start(xr[:, t % 2, :], x3_d[t]).then_inc(xr_in[t % 2], 16)
                    if not last:
                        sp.wait_ge(masked, nth(b, UNITS, H * (t + 1)))
                        sp.dma_start(adjn[:, t, :], adj_d[b + 1, t]).then_inc(adj_in[t], 16)
                if not last:
                    sp.wait_ge(ctx_done, nth(b, 2 * NT, 2 * NT))
                    for h in range(2):
                        sp.dma_start(xn[:, TPH * h:TPH * (h + 1), :],
                                     x_d[b + 1, :, TPH * h:TPH * (h + 1), :]).then_inc(x_in[h], 16)
                store(b, NT - 2)
                store(b, NT - 1)
                for k in range(2):
                    sp.wait_ge(out_done[k], nth(b, 8 * NT, 8 * NT))
                sp.sem_inc(xr_free, 1)

            def store(b, t):
                sp.wait_ge(ln_done, nth(b, LN_PER, 3 * NT + t + 1))
                sp.dma_start(out_d[b, t], xr[:, t % 2, :]).then_inc(out_done[t % 2], 16)

            sp.sem_inc(xr_free, 1)
            with sp.Fori(0, B - 1) as b:
                element(b, False)
            element(B - 1, True)

        SET_LOADS = 16 * (1 + 1 + 3 + 5 + 2 + 2 + 4 + 4)

        @block.gpsimd
        def _(pool):
            pool.memset(ident, 0.0).then_inc(set_const, 1)
            pool.memset(sel[:, :, :], 1.0).then_inc(set_const, 1)
            pool.memset(expo[:, :], -0.5).then_inc(set_const, 1)
            pool.memset(ones[:, :], 1.0).then_inc(set_const, 1)
            pool.memset(eps_ln[:, :], EPS_LN).then_inc(set_const, 1)
            pool.memset(zero[:, :], 0.0).then_inc(set_const, 1)
            pool.wait_ge(set_const, 6)
            pool.affine_select(out=ident, in_=ident, compare_op=ALU.not_equal, fill=1.0, base=0,
                               pattern=[[-1, P]], channel_multiplier=1).then_inc(set_const, 1)
            pool.affine_select(out=sel[:, :, :], in_=sel[:, :, :], compare_op=ALU.is_ge, fill=0.0, base=0,
                               pattern=[[P, 2], [1, P]], channel_multiplier=-HD).then_inc(set_const, 1)
            pool.wait_ge(set_const, 8)
            pool.affine_select(out=sel[:, :, :], in_=sel[:, :, :], compare_op=ALU.is_ge, fill=0.0, base=HD - 1,
                               pattern=[[-P, 2], [-1, P]], channel_multiplier=HD).then_inc(set_const, 1)

            def layer_norm(b, layer):
                for t in range(NT):
                    norm_tile(b, layer, t)

            def norm_tile(b, layer, t):
                k = t % 4
                pool.wait_ge(stat_ready, nth(b, LN_PER, layer * NT + t + 1))
                pool.tensor_tensor(vare[:, k:k + 1], mv[:, k, 1:2], eps_ln[:, :], ALU.add).then_inc(var_ready, 1)
                pool.tensor_tensor(nmean[:, k:k + 1], zero[:, :], mv[:, k, 0:1], ALU.subtract).then_inc(neg_mean, 1)
                pool.wait_ge(var_ready, nth(b, LN_PER, layer * NT + t + 1))
                pool.tensor_tensor(rstd[:, k:k + 1], vare[:, k:k + 1], expo[:, 0:1], ALU.pow).then_inc(rstd_ready, 1)
                pool.wait_ge(neg_mean, nth(b, LN_PER, layer * NT + t + 1))
                pool.wait_ge(rstd_ready, nth(b, LN_PER, layer * NT + t + 1))
                pool.tensor_tensor(shift[:, k:k + 1], nmean[:, k:k + 1], rstd[:, k:k + 1],
                                   ALU.mult).then_inc(shift_ready, 1)

            with pool.Fori(0, B) as b:
                layer_norm(b, 0)
                for j in range(NT):
                    pool.wait_ge(tp_free, nth(b, TP_UNITS, tp_a(1, j) + 2))
                    if j >= 1:
                        pool.wait_ge(al_summed, nth(b, NT, j))
                    so_far = asum[:, :] if j >= 1 else zero[:, 0:1].broadcast_to([P, N])
                    pool.tensor_tensor(asum[:, :], ev[:, j % 2, :], so_far, ALU.add).then_inc(al_summed, 1)
                for layer in (1, 2):
                    layer_norm(b, layer)
                for u in range(UNITS + 12):
                    if u >= 19 and (u - 19) % H == 0 and (u - 19) // H < NT:
                        norm_tile(b, 3, (u - 19) // H)
                    if u >= 14 and (u - 14) % H == 0 and (u - 14) // H < NT:
                        qt = (u - 14) // H
                        pool.wait_ge(xr_in[qt % 2], nth(b, 8 * NT, 16 * (qt // 2 + 1)))
                        pool.tensor_tensor(xr[:, qt % 2, :], xr[:, qt % 2, :], bias_o[:, :], ALU.add).then_inc(xr_biased, 1)
                    if u < UNITS:
                        pool.wait_ge(masked, nth(b, UNITS, u + 1))
                        if u >= 4:
                            pool.wait_ge(exp_done, nth(b, UNITS, u - 3))
                        pool.tensor_tensor(nmax[:, u % 4:u % 4 + 1], zero[:, :], mmax[:, u % 4:u % 4 + 1],
                                           ALU.subtract).then_inc(neg_max, 1)

        @block.tensor
        def _(pe):
            def three(dst, a_hi, a_lo, b_hi, b_lo, first, last, check=False):
                pe.matmul(dst, a_hi, b_hi, start=first, stop=False, skip_group_check=check)
                pe.matmul(dst, a_hi, b_lo, start=False, stop=False, skip_group_check=check)
                return pe.matmul(dst, a_lo, b_hi, start=False, stop=last, skip_group_check=check)

            pe.wait_ge(set_in, SET_LOADS)
            pe.wait_ge(set_const, 9)
            bank = lambda n: ps[:, TP + n % 2, :].rearrange("p (k o) -> p k o", o=F)
            for n in range(7):
                if n >= 2:
                    pe.wait_ge(set_dve, n - 1)
                for kt in range(FT):
                    for ot in range(FT):
                        src = (st_w0[:, ot, (n * FT + kt) * P:(n * FT + kt + 1) * P] if n < 2 else
                               st_sq[:, n - 2, ot, kt * P:(kt + 1) * P])
                        last = pe.transpose(bank(n)[:, kt, ot * P:(ot + 1) * P], src, ident)
                last.then_inc(set_pe, 1)
            pe.wait_ge(set_dve, 7)
            for it in range(FT):
                for dt in range(FT):
                    last = pe.matmul(ps[:, PR, 2 * it:2 * it + 2], st_wvt[:, dt, it * P:(it + 1) * P],
                                     st_aw[:, dt, :], start=(dt == 0), stop=(dt == FT - 1))
            pe.wait_ge(set_act, 9)
            pe.wait_ge(set_dve, 8)
            for dt in range(FT):
                pe.matmul(ps[:, PR, 8:10], st_bb[:, 0, dt, :], st_aw[:, dt, :], start=(dt == 0), stop=False)
            last = pe.matmul(ps[:, PR, 8:10], ones[0:1, :], st_ab[0:1, :], start=False, stop=True)
            last.then_inc(set_pe, 1)
            pe.matmul(ps[:, ACC, 0:F], ones[0:3, :], st_bk[:, :], start=True, stop=True)
            pe.matmul(ps[:, ACC + 1, 0:F], ones[0:1, :], st_row[0:1, 0, :], start=True, stop=True)
            pe.matmul(ps[:, ACC + 2, 0:F], ones[0:1, :], st_row[0:1, 1, :], start=True, stop=False)
            for et in range(FT):
                pe.matmul(ps[:, ACC + 2, 0:F], st_bb[:, 1, et, :], f32(w_hi[:, W_O, et, :]), start=False, stop=False)
                last = pe.matmul(ps[:, ACC + 2, 0:F], st_bb[:, 1, et, :], f32(w_lo[:, W_O, et, :]), start=False,
                                 stop=(et == FT - 1))
            last.then_inc(set_pe, 1)

            def transpose_x(b, layer):
                for half in range(HALVES):
                    transpose_x_half(b, layer, half)

            def transpose_x_half(b, layer, half):
                n = tp_x(layer, half)
                if layer == 0:
                    pe.wait_ge(x_in[half], nth(b, 16, 16))
                else:
                    pe.wait_ge(ln_done, nth(b, LN_PER, (layer - 1) * NT + TPH * (half + 1)))
                for ft in range(FT):
                    if n >= 2:
                        pe.wait_ge(tp_free, nth(b, TP_UNITS, n - 1))
                    for t in range(TPH):
                        last = pe.transpose(ps[:, TP + n % 2, t * P:(t + 1) * P],
                                            xn[:, TPH * half + t, ft * P:(ft + 1) * P], ident)
                    last.then_inc(tp_full, 1)
                    n += 1

            def transpose_adj(b, layer, j):
                for half in range(HALVES):
                    n = tp_a(layer, j) + half
                    if n >= 2:
                        pe.wait_ge(tp_free, nth(b, TP_UNITS, n - 1))
                    for t in range(TPH):
                        i = TPH * half + t
                        if layer == 0 and j == 0:
                            pe.wait_ge(adj_in[i], nth(b, 16, 16))
                        last = pe.transpose(ps[:, TP + n % 2, t * P:(t + 1) * P],
                                            adjn[:, i, j * P:(j + 1) * P], ident)
                    last.then_inc(tp_full, 1)

            def project(dst, w, rows, a_hi=xt_hi, a_lo=xt_lo):
                for ft in range(FT):
                    last = three(dst, a_hi[:, ft, rows * P:(rows + 1) * P], a_lo[:, ft, rows * P:(rows + 1) * P],
                                 w_hi[:, w, ft, :], w_lo[:, w, ft, :], ft == 0, ft == FT - 1)
                return last

            def pr_bank(b, n):
                if n >= 2 and PR_ORDER[n - 2][0] == "z":
                    pe.wait_ge(pr_act, nth(b, NT + PAIRS, NT + PR_ORDER[n - 2][1] + 1))
                elif n >= 2:
                    pe.wait_ge(pr_free, nth(b, PR_UNITS, n - 1))
                return ps[:, PR + n % 2, :]

            def project_pairs(b, name, w, rows_ready, pairs=range(PAIRS)):
                for k in pairs:
                    pe.wait_ge(*rows_ready(k))
                    dst = pr_bank(b, pr[name, k])
                    for s in range(2):
                        last = project(dst[:, s * F:(s + 1) * F], w, 2 * k + s)
                    last.then_inc(pr_full, 1)

            def rows_wait(b, name, j):
                if j % 2 == 0:
                    if name == "z":
                        pe.wait_ge(u_ready, nth(b, 4 + PAIRS, 4 + j // 2 + 1))
                    else:
                        pe.wait_ge(pr_free, nth(b, PR_UNITS, pr[name, j // 2] + 1))

            def transposed_product(dst, ft, j, half, first, last):
                return three(dst, uh[:, j, ft * P:(ft + 1) * P], ul[:, j, ft * P:(ft + 1) * P],
                             t_hi[:, j, half * 512:(half + 1) * 512], t_lo[:, j, half * 512:(half + 1) * 512],
                             first, last)

            def repeated(w, ft):
                return w[:, ft, 1:2].broadcast_to([P, P])

            def transposed_products(j):
                for half in range(HALVES):
                    for ft in range(FT):
                        last = transposed_product(ps[:, ACC + 2 * half + ft, :], ft, j, half, j == 0, j == NT - 1)
                        if j == NT - 1:
                            last.then_inc(acc_full, 1)

            def sj_columns(b, half):
                dst = pr_bank(b, pr["sj", half])
                for t in range(TPH):
                    rows = slice((TPH * half + t) * P, (TPH * half + t + 1) * P)
                    for ft in range(FT):
                        for part in (xt_hi, xt_lo):
                            last = pe.matmul(dst[:, 2 * t:2 * t + 2], part[:, ft, rows], wsj_pair[:, ft, :],
                                             start=(ft == 0 and part is xt_hi), stop=(ft == FT - 1 and part is xt_lo))
                last.then_inc(pr_full, 1)

            def xt_wait(b, layer):
                return lambda k: (tp_free, nth(b, TP_UNITS, tp_x(layer, k // (PAIRS // 2)) + 2))

            def row_product(b, t, af):
                k = 0 if af == AF_P2 else NT
                if t >= 4:
                    pe.wait_ge(acc_free, nth(b, 2 * NT, k + t - 3))
                for j in range(NT):
                    if t == 0:
                        rows_wait(b, "z" if af == AF_P2 else "conv 2", j)
                    last = three(ps[:, ACC + t % 4, 0:F], t_hi[:, j, t * P:(t + 1) * P], t_lo[:, j, t * P:(t + 1) * P],
                                 uh[:, j, :], ul[:, j, :], j == 0, j == NT - 1)
                last.then_inc(acc_full, 1)

            def stack_copies(b, n):
                h, m, half = n // 4, n // 2 % 2, n % 2
                if n >= 4:
                    pe.wait_ge(copies_dve if n % 2 else copies_act, nth(b, COPIES // 2, n // 2 - 1))
                at = slice(half * 512, (half + 1) * 512)
                block = lambda k, count: placer[:, (4 * h + k) * HD:(4 * h + k + count) * HD]
                dst = ps[0:STACK, ACC + n % 4, :]
                if m == 0:
                    pe.matmul(dst, block(2, 3), qk0_hi[:, 0, at], start=True, stop=False)
                    last = pe.matmul(dst, block(0, 3), qk0_lo[:, 0, at], start=False, stop=True)
                else:
                    pe.matmul(dst, block(1, 3), qk0_hi[:, 1, at], start=True, stop=False)
                    last = pe.matmul(dst, block(3, 3), qk0_lo[:, 1, at], start=False, stop=True)
                last.then_inc(copies_full, 1)

            def scores(b, u):
                qt, h = divmod(u, H)
                if u == 0:
                    pe.wait_ge(copies_act, nth(b, COPIES // 2, COPIES // 2))
                    pe.wait_ge(copies_dve, nth(b, COPIES // 2, COPIES // 2))
                if u == G:
                    pe.wait_ge(stacked[0], nth(b, 16 * 3, 16 * 3))
                    pe.wait_ge(stacked[1], nth(b, 16 * 3, 16 * 3))
                if u >= 2:
                    pe.wait_ge(masked, nth(b, UNITS, u - 1))
                for half in range(HALVES):
                    last = pe.matmul(ps[:, 2 * (u % 2) + half, :], q_stack[0:STACK, h, qt * P:(qt + 1) * P],
                                     k_stack[0:STACK, h, half * 512:(half + 1) * 512], start=True, stop=True)
                last.then_inc(s_full, 1)

            def transpose_p(b, u):
                pe.wait_ge(exp_done, nth(b, UNITS, u + 1))
                for half in range(HALVES):
                    if u >= 1:
                        pe.wait_ge(p_dve if half == 0 else p_act, nth(b, UNITS, u))
                    for t in range(TPH):
                        last = pe.transpose(ps[:, TP + half, t * P:(t + 1) * P],
                                            r[:, u % RSLOTS, (TPH * half + t) * P:(TPH * half + t + 1) * P], ident)
                    last.then_inc(p_full, 1)

            def context(b, grp, part):
                qt, g = divmod(grp, 2)
                pe.wait_ge(p_act if part else p_dve, nth(b, UNITS, G * grp + G))
                if g == 0 and qt >= 1 and part == 0:
                    pe.wait_ge(c_raw, nth(b, NT, qt))
                for kt in range(part * TPH, (part + 1) * TPH):
                    for hh in range(G):
                        h = g * G + hh
                        last = pe.matmul(ps[HD * hh:HD * (hh + 1), 6, g * P:(g + 1) * P],
                                         xn[:, kt, h * HD:(h + 1) * HD], pt[:, (grp * G + hh) % PSLOTS, kt, :],
                                         start=(kt == 0), stop=(kt == NT - 1), tile_position=(0, HD * hh))
                if part:
                    last.then_inc(ctx_done, 1)

            def denominators(b, qt):
                pe.wait_ge(rp_ready, nth(b, NT, qt + 1))
                if qt >= 1:
                    pe.wait_ge(h_sum, nth(b, NT, qt))
                pe.matmul(ps[0:H, 7, 0:P], rprow[:, qt % 2, :], ident[:, :], start=True, stop=True).then_inc(rt_full, 1)

            def spread_denominators(b, qt):
                pe.wait_ge(rt_ready, nth(b, NT, qt + 1))
                for g in range(2):
                    last = pe.matmul(ps[:, 7, g * P:(g + 1) * P], sel[:, g, :], rt[:, :], start=True, stop=True)
                last.then_inc(rbc_full, 1)

            def output(b, qt):
                pe.wait_ge(c_ready, nth(b, NT, qt + 1))
                for g in range(2):
                    last = three(ps[:, 7, 0:F], c_hi[:, g, :], c_lo[:, g, :], w_hi[:, W_O, g, :], w_lo[:, W_O, g, :],
                                 g == 0, g == 1)
                last.then_inc(o_full, 1)

            with pe.Fori(0, B) as b:
                transpose_adj(b, 0, 0)
                for j in range(NT):
                    if j + 1 < NT:
                        transpose_adj(b, 0, j + 1)
                    pe.wait_ge(tp_free, nth(b, TP_UNITS, tp_a(0, j) + 2))
                    if j % TPH == 0:
                        pe.wait_ge(x_split, nth(b, 2, j // TPH + 1))
                    transposed_products(j)
                transpose_x(b, 0)
                pe.wait_ge(drained, b + 1)
                for t in range(NT):
                    if t == 0:
                        pe.wait_ge(tp_free, nth(b, TP_UNITS, tp_x(0, 1) + 2))
                    if t == NT - 1:
                        transpose_x_half(b, 1, 0)
                    dst = pr_bank(b, pr["layer 0", t])
                    project(dst[:, 0:F], W_L0X, t)
                    if t % TPH == 0:
                        pe.wait_ge(u_ready, nth(b, 4 + PAIRS, 2 * (t // TPH) + 2))
                    project(dst[:, F:2 * F], W_L0G, t, gh, gl).then_inc(pr_full, 1)

                for half in range(HALVES):
                    if half == 1:
                        transpose_x_half(b, 1, 1)
                    pe.wait_ge(tp_free, nth(b, TP_UNITS, tp_x(1, half) + 2))
                    dst = pr_bank(b, pr["si", half])
                    cols_h = slice(half * 512, (half + 1) * 512)
                    for ft in range(FT):
                        last = three(dst, repeated(wsj_hi, ft), repeated(wsj_lo, ft), xt_hi[:, ft, cols_h],
                                     xt_lo[:, ft, cols_h], ft == 0, ft == FT - 1)
                    last.then_inc(pr_full, 1)
                    if half == 0:
                        sj_columns(b, 0)
                        project_pairs(b, "v", W_K2, xt_wait(b, 1), range(2))
                transpose_adj(b, 1, 0)
                project_pairs(b, "v", W_K2, xt_wait(b, 1), range(2, PAIRS))
                sj_columns(b, 1)
                transpose_adj(b, 1, 1)
                for j in range(NT):
                    if j + 2 < NT:
                        transpose_adj(b, 1, j + 2)
                    rows_wait(b, "v", j)
                    if j == NT - 1:
                        pe.wait_ge(al_summed, nth(b, NT, NT))
                        for i in range(NT):
                            last = pe.matmul(ps[:, TP, 2 * i:2 * i + 2], asum[:, i * P:(i + 1) * P], ones_2[:, :],
                                             start=True, stop=True)
                        last.then_inc(sums_full, 1)
                        project_pairs(b, "z", W_K1, xt_wait(b, 1), range(2))
                    pe.wait_ge(al_ready, nth(b, 2 * NT, 2 * j + 2))
                    for i in range(NT):
                        dst = ps[:, ACC + i // 2, (i % 2) * F:(i % 2 + 1) * F]
                        last = three(dst, t_hi[:, j, i * P:(i + 1) * P], t_lo[:, j, i * P:(i + 1) * P], uh[:, j, :],
                                     ul[:, j, :], j == 0 and i % 2 == 0, j == NT - 1, True)
                last.then_inc(hop_full, 1)
                project_pairs(b, "z", W_K1, xt_wait(b, 1), range(2, PAIRS))
                for t in range(NT):
                    project(pr_bank(b, pr["h", t])[:, 0:F], W_K0, t).then_inc(pr_full, 1)
                    row_product(b, t, AF_P2)
                    if t == NT - 3:
                        transpose_x_half(b, 2, 0)

                transpose_adj(b, 2, 0)
                project_pairs(b, "conv 0", W_G1, xt_wait(b, 2), range(2))
                transpose_x_half(b, 2, 1)
                project_pairs(b, "conv 0", W_G1, xt_wait(b, 2), range(2, PAIRS))
                pe.wait_ge(acc_free, nth(b, 2 * NT, NT))
                for j in range(NT):
                    if j + 1 < NT:
                        transpose_adj(b, 2, j + 1)
                    rows_wait(b, "conv 0", j)
                    pe.wait_ge(tp_free, nth(b, TP_UNITS, tp_a(2, j) + 2))
                    transposed_products(j)
                h_wait = lambda c: (lambda k: (h_ready, nth(b, 8, 4 * c + (2 if k < NT // 4 else 4))))
                project_pairs(b, "conv 1", W_G2, h_wait(0))
                for half in range(HALVES):
                    for ft in range(FT):
                        for j in range(NT):
                            if half == 0 and ft == 0:
                                rows_wait(b, "conv 1", j)
                            last = transposed_product(ps[:, ACC + 2 * half + ft, :], ft, j, half, j == 0, j == NT - 1)
                        last.then_inc(acc_full, 1)
                project_pairs(b, "conv 2", W_G3, h_wait(1))
                for t in range(NT):
                    row_product(b, t, AF_C3)
                    if t == NT - 3:
                        transpose_x_half(b, 3, 0)

                for n, (ft, m, half) in enumerate(QK):
                    if n == 3:
                        transpose_x_half(b, 3, 1)
                    pe.wait_ge(tp_free, nth(b, TP_UNITS, tp_x(3, half) + 2))
                    dst = pr_bank(b, pr["qk", (ft, m, half)])
                    cols_h, w = slice(half * 512, (half + 1) * 512), (W_Q, W_K)[m]
                    for et in range(FT):
                        last = three(dst, w_hi[:, w, et, ft * P:(ft + 1) * P], w_lo[:, w, et, ft * P:(ft + 1) * P],
                                     xt_hi[:, et, cols_h], xt_lo[:, et, cols_h], et == 0, et == FT - 1)
                    last.then_inc(pr_full, 1)
                project_pairs(b, "values", W_V, xt_wait(b, 3))
                pe.wait_ge(pr_free, nth(b, PR_UNITS, PR_UNITS))
                for n in range(COPIES):
                    stack_copies(b, n)
                scores(b, 0)
                for s in range(UNITS + 10):
                    if s + 1 < UNITS:
                        scores(b, s + 1)
                    if LAG <= s < UNITS + LAG:
                        transpose_p(b, s - LAG)
                    for part in range(2):
                        if s - part >= LAG + G and (s - part - LAG) % G == 0 and (s - part - LAG) // G <= 2 * NT:
                            context(b, (s - part - LAG) // G - 1, part)
                    if s >= 11 and (s - 11) % H == 0 and (s - 11) // H < NT:
                        denominators(b, (s - 11) // H)
                    if s >= 13 and (s - 13) % H == 0 and (s - 13) // H < NT:
                        spread_denominators(b, (s - 13) // H)
                    if s >= 17 and (s - 17) % H == 0 and (s - 17) // H < NT:
                        output(b, (s - 17) // H)

        @block.scalar
        def _(act):
            copy = lambda dst, src, scale=1.0: nc.scalar.activation(dst, src, ACT.Copy, scale=scale)

            act.wait_ge(set_in, SET_LOADS)
            act.wait_ge(set_const, 9)
            for n, slot in enumerate((W_L0X, W_L0G, W_Q, W_K, W_V, W_O)):
                act.wait_ge(set_pe, n + 1)
                copy(w_hi[:, slot, :, :].rearrange("p k o -> p (k o)"), ps[:, TP + n % 2, :],
                     QSCALE if slot == W_Q else 1.0).then_inc(set_act, 1)
            copy(w_hi[:, W_K0:W_G3 + 1, :, :].rearrange("p w k o -> p (w k o)"),
                 st_nat[:, :, :, :].rearrange("p w k o -> p (w k o)")).then_inc(set_act, 1)
            copy(ones_2[:, :], ones[:, 0:2])
            for k in range(0, 4 * G * HD, P):
                copy(placer[:, k:k + P], ones[:, :], 0.0)
            copy(placer[:, 4 * G * HD:], ones[:, 0:2 * HD], 0.0).then_inc(set_act, 1)
            act.wait_ge(set_act, 8)
            for h in range(G):
                for k in (2, 3):
                    copy(placer[:, (4 * h + k) * HD:(4 * h + k + 1) * HD], ident[:, HD * h:HD * (h + 1)])
            for k in range(2):
                for t in range(FT):
                    last = copy(st_bb[:, k, t, :], ones[:, :], st_bc[:, k, t:t + 1])
            last.then_inc(set_act, 1)
            copy(cols[:, 2, :], cols[:, 2, :], QSCALE).then_inc(set_act, 1)
            act.wait_ge(set_pe, 8)
            wa = ps[:, PR, 0:2 * FT].rearrange("p (t k) -> p t k", k=2)
            copy(wsj_hi[:, :, :], wa).then_inc(set_act, 1)
            act.wait_ge(set_pe, 9)
            copy(bias_k[:, :], ps[:, ACC, 0:F])
            copy(bias_g3[:, :], ps[:, ACC + 1, 0:F])
            copy(bias_o[:, :], ps[:, ACC + 2, 0:F]).then_inc(set_act, 1)
            act.wait_ge(set_dve, 11)
            copy(wsj_pair[:, :, 0], f32(wsj_hi[:, :, 0]))
            copy(wsj_pair[:, :, 1], f32(wsj_lo[:, :, 0]))

            def x_transposed(b, layer, half):
                for ft in range(FT):
                    n = tp_x(layer, half) + ft
                    act.wait_ge(tp_full, nth(b, TP_UNITS, n + 1))
                    copy(xt_hi[:, ft, half * 512:(half + 1) * 512], ps[:, TP + n % 2, :]).then_inc(tp_hi, 1)

            def adj_transposed(b, layer, j):
                for half in range(HALVES):
                    n = tp_a(layer, j) + half
                    act.wait_ge(tp_full, nth(b, TP_UNITS, n + 1))
                    copy(t_hi[:, j, half * 512:(half + 1) * 512], ps[:, TP + n % 2, :]).then_inc(tp_hi, 1)

            def rows_from_pr(b, name, pairs=range(PAIRS)):
                for k in pairs:
                    n = pr[name, k]
                    act.wait_ge(pr_full, nth(b, PR_UNITS, n + 1))
                    copy(u_hi[:, k * 512:(k + 1) * 512], ps[:, PR + n % 2, :]).then_inc(u_act, 1)

            def hidden(b, c, af):
                for k in range(2 * FT):
                    n, half, ft = 4 * c + k, k // FT, k % FT
                    act.wait_ge(acc_full, nth(b, AF_PER, af(k)))
                    if n >= 2:
                        act.wait_ge(h_ready, nth(b, 8, n - 1))
                    act.activation(ev[:, n % 2, 0:512], ps[:, ACC + k, :], ACT.Relu,
                                   bias=cols[:, c, ft:ft + 1]).then_inc(h_raw, 1)
                    act.wait_ge(h_raw, nth(b, 8, n + 1))
                    copy(xt_hi[:, ft, half * 512:(half + 1) * 512], ev[:, n % 2, 0:512]).then_inc(h_hi, 1)

            def normalise(b, layer, t):
                act.wait_ge(shift_ready, nth(b, LN_PER, layer * NT + t + 1))
                src, dst = (y[:, t % 4, :], xn[:, t, :]) if layer < 3 else (xr[:, t % 2, :], xr[:, t % 2, :])
                act.activation(dst, src, ACT.Identity, bias=shift[:, t % 4:t % 4 + 1],
                               scale=rstd[:, t % 4:t % 4 + 1]).then_inc(ln_done, 1)

            with act.Fori(0, B) as b:
                for j in range(NT):
                    adj_transposed(b, 0, j)
                    if j < 2:
                        act.wait_ge(x_in[j], nth(b, 16, 16))
                        copy(u_hi[:, j * N:(j + 1) * N],
                             xn[:, TPH * j:TPH * (j + 1), :].rearrange("p t f -> p (t f)")).then_inc(x_split_hi, 1)
                x_transposed(b, 0, 0)
                for k in range(2 * FT):
                    half, ft = k // FT, k % FT
                    if k == 2:
                        x_transposed(b, 0, 1)
                    act.wait_ge(acc_full, nth(b, AF_PER, AF_L0 + k + 1))
                    copy(gh[:, ft, half * 512:(half + 1) * 512], ps[:, ACC + k, :]).then_inc(u_act, 1)
                act.wait_ge(deg_ready, nth(b, 2, 1))
                for t in range(NT):
                    n = pr["layer 0", t]
                    act.wait_ge(pr_full, nth(b, PR_UNITS, n + 1))
                    if t >= 2:
                        act.wait_ge(pr_free, nth(b, PR_UNITS, n - 1))
                    copy(ev[:, t % 2, 0:F], ps[:, PR + n % 2, F:2 * F], rdeg[:, t:t + 1]).then_inc(pr_act, 1)
                    if t >= 2:
                        normalise(b, 0, t - 2)
                    if t == NT - 2:
                        x_transposed(b, 1, 0)

                normalise(b, 0, NT - 2)
                rows_from_pr(b, "v", range(1))
                normalise(b, 0, NT - 1)
                rows_from_pr(b, "v", range(1, 2))
                x_transposed(b, 1, 1)
                act.wait_ge(pr_free, nth(b, PR_UNITS, pr["si", 1] + 1))
                act.wait_ge(sj_ready, nth(b, 2, 1))

                def scaled(j):
                    if j == TPH:
                        act.wait_ge(sj_ready, nth(b, 2, 2))
                    act.activation(e_area[:, 1, j, :], si[:, :], ACT.Identity, bias=sj_scaled[:, j:j + 1],
                                   scale=SLOPE).then_inc(e_scaled, 1)

                def exponential(j):
                    act.wait_ge(e_lin, nth(b, NT, j + 1))
                    act.activation(e_area[:, 1, j, :], e_area[:, 1, j, :], ACT.Exp).then_inc(e_exp, 1)

                scaled(0)
                scaled(1)
                exponential(0)
                rows_from_pr(b, "v", range(2, PAIRS))
                exponential(1)
                scaled(2)
                for j in range(NT):
                    act.wait_ge(tp_free, nth(b, TP_UNITS, tp_a(1, j) + 2))
                    copy(t_hi[:, j, :], ev[:, j % 2, :]).then_inc(al_hi, 1)
                    if j + 2 < NT:
                        exponential(j + 2)
                    if j + 3 < NT:
                        scaled(j + 3)
                act.wait_ge(al_ready, nth(b, 2 * NT, 2 * NT))
                act.wait_ge(al_summed, nth(b, NT, NT))
                for k in range(NT // 2 + 1):
                    if k < NT // 2:
                        n = pr["z", k]
                        act.wait_ge(pr_full, nth(b, PR_UNITS, n + 1))
                        if k >= 2:
                            act.wait_ge(pr_free, nth(b, PR_UNITS, pr["z", k - 2] + 1))
                        copy(ev[:, k % 2, 0:512], ps[:, PR + n % 2, :]).then_inc(pr_act, 1)
                    if k >= 1:
                        act.wait_ge(pr_free, nth(b, PR_UNITS, pr["z", k - 1] + 1))
                        copy(u_hi[:, (k - 1) * 512:k * 512], ev[:, (k - 1) % 2, 512:1024]).then_inc(u_act, 1)

                for t in range(NT - 3):
                    normalise(b, 1, t)
                x_transposed(b, 2, 0)
                normalise(b, 1, NT - 3)
                normalise(b, 1, NT - 2)

                adj_transposed(b, 2, 0)
                rows_from_pr(b, "conv 0", range(1))
                normalise(b, 1, NT - 1)
                rows_from_pr(b, "conv 0", range(1, 2))
                x_transposed(b, 2, 1)
                rows_from_pr(b, "conv 0", range(2, PAIRS))
                for j in range(1, NT):
                    adj_transposed(b, 2, j)
                hidden(b, 0, lambda k: AF_C1 + k + 1)
                rows_from_pr(b, "conv 1")
                hidden(b, 1, lambda k: AF_C2 + k + 1)
                rows_from_pr(b, "conv 2")
                for t in range(NT - 3):
                    normalise(b, 2, t)
                x_transposed(b, 3, 0)
                normalise(b, 2, NT - 3)
                normalise(b, 2, NT - 2)

                for k, part in enumerate(QK):
                    if k == 2:
                        normalise(b, 2, NT - 1)
                    if k == 3:
                        x_transposed(b, 3, 1)
                    ft, m, half = part
                    n = pr["qk", part]
                    act.wait_ge(pr_full, nth(b, PR_UNITS, n + 1))
                    act.activation(qk_place(part, u_hi, qk0_hi), ps[:, PR + n % 2, :], ACT.Identity,
                                   bias=cols[:, 2 + m, ft:ft + 1]).then_inc(qk_hi, 1)
                for n in range(0, COPIES, 2):
                    act.wait_ge(copies_full, nth(b, COPIES, n + 1))
                    copy(copies_place(n), ps[0:STACK, ACC + n % 4, :]).then_inc(copies_act, 1)
                for k in range(2):
                    act.wait_ge(qk_out[k], nth(b, 32, 32))
                for s in range(UNITS + 14):
                    if s >= 21 and (s - 21) % H == 0 and (s - 21) // H < NT:
                        normalise(b, 3, (s - 21) // H)
                    if LAG <= s < UNITS + LAG:
                        u = s - LAG
                        act.wait_ge(p_full, nth(b, 2 * UNITS, 2 * u + 2))
                        if u >= PSLOTS:
                            act.wait_ge(ctx_done, nth(b, 2 * NT, (u - PSLOTS) // G + 1))
                        copy(pt[:, u % PSLOTS, TPH:NT, :].rearrange("p t q -> p (t q)"),
                             ps[:, TP + 1, :]).then_inc(p_act, 1)
                    if s < UNITS:
                        qt, h = divmod(s, H)
                        act.wait_ge(neg_max, nth(b, UNITS, s + 1))
                        if h == 0 and qt >= 2:
                            act.wait_ge(rp_ready, nth(b, NT, qt - 1))
                        act.activation(r[:, s % RSLOTS, :], r[:, s % RSLOTS, :], ACT.Exp, bias=nmax[:, s % 4:s % 4 + 1],
                                       accum_out=prow[:, qt % 2, h:h + 1]).then_inc(exp_done, 1)
                    if s >= 11 and (s - 11) % H == 0 and (s - 11) // H < NT:
                        qt = (s - 11) // H
                        act.wait_ge(rt_full, nth(b, NT, qt + 1))
                        copy(rt[:, :], ps[0:H, 7, 0:P]).then_inc(rt_ready, 1)
                    if s >= 13 and (s - 13) % H == 0 and (s - 13) // H < NT:
                        qt = (s - 13) // H
                        act.wait_ge(rbc_full, nth(b, NT, qt + 1))
                        if qt >= 1:
                            act.wait_ge(c_raw, nth(b, NT, qt))
                        copy(rbc[:, :, :].rearrange("p g q -> p (g q)"), ps[:, 7, 0:2 * P]).then_inc(rbc_ready, 1)
                    if s >= 15 and (s - 15) % H == 0 and (s - 15) // H < NT:
                        qt = (s - 15) // H
                        act.wait_ge(c_raw, nth(b, NT, qt + 1))
                        if qt >= 1:
                            act.wait_ge(o_full, nth(b, NT, qt))
                        copy(c_hi[:, :, :], c_f[:, :, :]).then_inc(c_hi_ready, 1)

        @block.vector
        def _(dve):
            dve.wait_ge(set_in, SET_LOADS)
            for n, slot in enumerate((W_L0X, W_L0G, W_Q, W_K, W_V, W_O)):
                dve.wait_ge(set_act, n + 1)
                scale = QSCALE if slot == W_Q else 1.0
                dve.scalar_tensor_tensor(out=w_lo[:, slot, :, :].rearrange("p k o -> p (k o)"),
                                         in0=ps[:, TP + n % 2, :], scalar=scale,
                                         in1=f32(w_hi[:, slot, :, :].rearrange("p k o -> p (k o)")),
                                         op0=ALU.mult, op1=ALU.subtract).then_inc(set_dve, 1)
            dve.wait_ge(set_pe, 7)
            dve.tensor_copy(st_wvt[:, :, :].rearrange("p k o -> p (k o)"), ps[:, TP, :]).then_inc(set_dve, 1)
            dve.memset(st_ab[:, 1:2], 0.0).then_inc(set_dve, 1)
            dve.wait_ge(set_act, 7)
            dve.tensor_tensor(w_lo[:, W_K0:W_G3 + 1, :, :].rearrange("p w k o -> p (w k o)"),
                              st_nat[:, :, :, :].rearrange("p w k o -> p (w k o)"),
                              f32(w_hi[:, W_K0:W_G3 + 1, :, :].rearrange("p w k o -> p (w k o)")),
                              ALU.subtract).then_inc(set_dve, 1)
            dve.wait_ge(set_act, 11)
            dve.tensor_tensor(wsj_lo[:, :, :], ps[:, PR, 0:2 * FT].rearrange("p (t k) -> p t k", k=2),
                              f32(wsj_hi[:, :, :]), ALU.subtract).then_inc(set_dve, 1)
            dve.tensor_reduce(e_const[:, :], ps[:, PR, 8:10], AX.X, ALU.add).then_inc(set_dve, 1)
            dve.wait_ge(set_act, 12)
            dve.wait_ge(set_dve, 11)
            dve.memset(vare[:, :], 0.0).then_inc(drained, 1)

            def alone():
                dve.sem_inc(passed, 1)

            def rest(dst, value, hi, done):
                dve.tensor_tensor(dst, value, f32(hi), ALU.subtract).then_inc(done, 1)

            def x_transposed(b, layer, half):
                for ft in range(FT):
                    n = tp_x(layer, half) + ft
                    at = slice(half * 512, (half + 1) * 512)
                    dve.wait_ge(tp_hi, nth(b, TP_UNITS - 2 * NT, hi_at(n)))
                    dve.tensor_tensor(xt_lo[:, ft, at], ps[:, TP + n % 2, :], f32(xt_hi[:, ft, at]),
                                      ALU.subtract).then_inc(tp_free, 1)

            def hi_at(n):
                return n + 1 - (2 * NT if n >= tp_a(1, 0) else 0)

            def adj_transposed(b, layer, j):
                for half in range(HALVES):
                    n = tp_a(layer, j) + half
                    at = slice(half * 512, (half + 1) * 512)
                    dve.wait_ge(tp_hi, nth(b, TP_UNITS - 2 * NT, hi_at(n)))
                    dve.tensor_tensor(t_lo[:, j, at], ps[:, TP + n % 2, :], f32(t_hi[:, j, at]),
                                      ALU.subtract).then_inc(tp_free, 1)

            def rows_from_pr(b, name, u0, pairs=range(PAIRS)):
                for k in pairs:
                    n = pr[name, k]
                    at = slice(k * 512, (k + 1) * 512)
                    dve.wait_ge(u_act, nth(b, U_PER, u0 + k + 1))
                    dve.tensor_tensor(u_lo[:, at], ps[:, PR + n % 2, :], f32(u_hi[:, at]),
                                      ALU.subtract).then_inc(pr_free, 1)

            def tile_stats(b, layer, t):
                raw_stats(b, layer, t)
                mean_variance(b, layer, t)

            def raw_stats(b, layer, t):
                src = y[:, t % 4, :] if layer < 3 else xr[:, t % 2, :]
                if layer < 3:
                    dve.wait_ge(y_ready, nth(b, 3 * NT, layer * NT + t + 1))
                else:
                    dve.wait_ge(h_sum, nth(b, NT, t + 1))
                dve.bn_stats(stats[:, t % 4, :], src).then_inc(bn_raw, 1)

            def mean_variance(b, layer, t):
                dve.wait_ge(bn_raw, nth(b, LN_PER, layer * NT + t + 1))
                alone()
                dve.bn_aggr(mv[:, t % 4, :], stats[:, t % 4, :]).then_inc(stat_ready, 1)

            def y_free(b, layer, t):
                if t >= 4:
                    dve.wait_ge(ln_done, nth(b, LN_PER, layer * NT + t - 3))

            def relu_residual(b, layer, t):
                y_free(b, layer, t)
                dve.scalar_tensor_tensor(out=y[:, t % 4, :], in0=ev[:, t % 2, F:2 * F], scalar=0.0, in1=xn[:, t, :],
                                         op0=ALU.max, op1=ALU.add).then_inc(y_ready, 1)

            def sj_half(b, half):
                n, rows = pr["sj", half], slice(TPH * half, TPH * (half + 1))
                dve.wait_ge(pr_full, nth(b, PR_UNITS, n + 1))
                dve.tensor_reduce(sj[:, rows], ps[:, PR + n % 2, 0:2 * TPH].rearrange("p (t k) -> p t k", k=2),
                                  AX.X, ALU.add).then_inc(pr_free, 1)
                dve.wait_ge(pr_free, nth(b, PR_UNITS, n + 1))
                dve.tensor_scalar(sj_scaled[:, rows], sj[:, rows], SLOPE, None, ALU.mult).then_inc(sj_ready, 1)

            def hidden(b, c):
                for k in range(2 * FT):
                    n, half, ft = 4 * c + k, k // FT, k % FT
                    at = slice(half * 512, (half + 1) * 512)
                    dve.wait_ge(h_hi, nth(b, 8, n + 1))
                    rest(xt_lo[:, ft, at], ev[:, n % 2, 0:512], xt_hi[:, ft, at], h_ready)

            with dve.Fori(0, B) as b:
                for j in range(NT):
                    adj_transposed(b, 0, j)
                    if j == 0:
                        dve.wait_ge(xr_free, b + 1)
                    if j < 2:
                        at = slice(j * N, (j + 1) * N)
                        dve.wait_ge(x_split_hi, nth(b, 2, j + 1))
                        rest(u_lo[:, at], xn[:, TPH * j:TPH * (j + 1), :].rearrange("p t f -> p (t f)"), u_hi[:, at],
                             x_split)
                    dve.tensor_reduce(rsum[:, j:j + 1], adjn[:, j, :], AX.X, ALU.add).then_inc(deg_sum, 1)
                dve.wait_ge(deg_sum, nth(b, NT + 1, NT))
                dve.tensor_scalar(rsum[:, :], rsum[:, :], EPS_DEG, None, ALU.max).then_inc(deg_sum, 1)
                dve.wait_ge(deg_sum, nth(b, NT + 1, NT + 1))
                dve.reciprocal(rdeg[:, :], rsum[:, :]).then_inc(deg_ready, 1)
                x_transposed(b, 0, 0)
                for k in range(2 * FT):
                    if k == 2:
                        x_transposed(b, 0, 1)
                    half, ft = k // FT, k % FT
                    at = slice(half * 512, (half + 1) * 512)
                    dve.wait_ge(u_act, nth(b, U_PER, U_G + k + 1))
                    rest(gl[:, ft, at], ps[:, ACC + k, :], gh[:, ft, at], u_ready)
                for t in range(NT + 1):
                    if t < NT:
                        n = pr["layer 0", t]
                        dve.wait_ge(pr_act, nth(b, NT + NT // 2, t + 1))
                        dve.tensor_tensor(ev[:, t % 2, F:2 * F], ps[:, PR + n % 2, 0:F], ev[:, t % 2, 0:F],
                                          ALU.add).then_inc(pr_free, 1)
                    if t >= 1:
                        raw_stats(b, 0, t - 1)
                    if t < NT:
                        dve.wait_ge(pr_free, nth(b, PR_UNITS, n + 1))
                        relu_residual(b, 0, t)
                    if t >= 1:
                        mean_variance(b, 0, t - 1)
                    if t == NT - 2:
                        x_transposed(b, 1, 0)

                for half in range(HALVES):
                    if half == 1:
                        sj_half(b, 0)
                        rows_from_pr(b, "v", U_V, range(2))
                        x_transposed(b, 1, 1)
                    n = pr["si", half]
                    dve.wait_ge(pr_full, nth(b, PR_UNITS, n + 1))
                    if half == 0:
                        dve.wait_ge(ln_done, nth(b, LN_PER, NT - 2))
                    dve.tensor_scalar(si[:, half * 512:(half + 1) * 512], ps[:, PR + n % 2, :], e_const[:, 0:1], None,
                                      ALU.add).then_inc(pr_free, 1)
                def linear(j):
                    dve.wait_ge(e_scaled, nth(b, NT, j + 1))
                    dve.scalar_tensor_tensor(out=e_area[:, 1, j, :], in0=si[:, :], scalar=sj[:, j:j + 1],
                                             in1=e_area[:, 1, j, :], op0=ALU.add, op1=ALU.max).then_inc(e_lin, 1)

                def alpha_rest(j):
                    dve.wait_ge(al_hi, nth(b, NT, j + 1))
                    for half in range(HALVES):
                        at = slice(half * 512, (half + 1) * 512)
                        rest(t_lo[:, j, at], ev[:, j % 2, at], t_hi[:, j, at], al_ready)

                linear(0)
                linear(1)
                rows_from_pr(b, "v", U_V, range(2, PAIRS))
                for j in range(NT):
                    if j == 1:
                        alpha_rest(0)
                    dve.wait_ge(e_exp, nth(b, NT, j + 1))
                    if j >= 2:
                        dve.wait_ge(al_ready, nth(b, 2 * NT, 2 * (j - 2) + 2))
                        dve.wait_ge(al_summed, nth(b, NT, j - 1))
                    for half in range(HALVES):
                        n = tp_a(1, j) + half
                        at = slice(half * 512, (half + 1) * 512)
                        dve.wait_ge(tp_full, nth(b, TP_UNITS, n + 1))
                        dve.tensor_tensor(ev[:, j % 2, at], ps[:, TP + n % 2, :], e_area[:, 1, j, at],
                                          ALU.mult).then_inc(tp_free, 1)
                    if j == 0:
                        sj_half(b, 1)
                    if j >= 2:
                        alpha_rest(j - 1)
                    if j + 2 < NT:
                        linear(j + 2)
                alpha_rest(NT - 1)
                dve.wait_ge(sums_full, b + 1)
                dve.tensor_scalar(rsum[:, :], ps[:, TP, 0:2 * NT].rearrange("p (t k) -> p t k", k=2)[:, :, 0],
                                  EPS_ROW, None, ALU.add).then_inc(sums_read, 1)
                dve.wait_ge(sums_read, b + 1)
                dve.reciprocal(rdeg[:, :], rsum[:, :]).then_inc(deg_ready, 1)
                dve.wait_ge(deg_ready, nth(b, 2, 2))
                dve.wait_ge(hop_full, b + 1)
                for k in range(NT // 2 + 1):
                    if k < NT // 2:
                        dve.wait_ge(pr_act, nth(b, NT + NT // 2, NT + k + 1))
                        if k >= 2:
                            dve.wait_ge(u_ready, nth(b, 4 + NT // 2, 4 + k - 1))
                        for s in range(2):
                            t = 2 * k + s
                            last = dve.scalar_tensor_tensor(
                                out=ev[:, k % 2, 512 + s * F:512 + (s + 1) * F],
                                in0=ps[:, ACC + k, s * F:(s + 1) * F], scalar=rdeg[:, t:t + 1],
                                in1=ev[:, k % 2, s * F:(s + 1) * F], op0=ALU.mult, op1=ALU.add)
                        last.then_inc(pr_free, 1)
                    if k >= 1:
                        at = slice((k - 1) * 512, k * 512)
                        dve.wait_ge(u_act, nth(b, U_PER, U_Z + k))
                        rest(u_lo[:, at], ev[:, (k - 1) % 2, 512:1024], u_hi[:, at], u_ready)
                for t in range(NT + 1):
                    if t < NT:
                        n = pr["h", t]
                        dve.wait_ge(pr_full, nth(b, PR_UNITS, n + 1))
                        dve.tensor_tensor(ev[:, t % 2, 0:F], ps[:, PR + n % 2, 0:F], bias_k[:, :],
                                          ALU.add).then_inc(pr_free, 1)
                        dve.wait_ge(pr_free, nth(b, PR_UNITS, n + 1))
                        dve.wait_ge(acc_full, nth(b, AF_PER, AF_P2 + t + 1))
                        dve.scalar_tensor_tensor(out=ev[:, t % 2, F:2 * F], in0=ps[:, ACC + t % 4, 0:F],
                                                 scalar=rdeg[:, t:t + 1], in1=ev[:, t % 2, 0:F], op0=ALU.mult,
                                                 op1=ALU.add).then_inc(acc_free, 1)
                        dve.wait_ge(acc_free, nth(b, 2 * NT, t + 1))
                        relu_residual(b, 1, t)
                        tile_stats(b, 1, t)
                    if t == NT - 3:
                        x_transposed(b, 2, 0)

                adj_transposed(b, 2, 0)
                rows_from_pr(b, "conv 0", U_C, range(2))
                x_transposed(b, 2, 1)
                rows_from_pr(b, "conv 0", U_C, range(2, PAIRS))
                for j in range(1, NT):
                    adj_transposed(b, 2, j)
                hidden(b, 0)
                rows_from_pr(b, "conv 1", U_C + PAIRS)
                hidden(b, 1)
                rows_from_pr(b, "conv 2", U_C + 2 * PAIRS)
                for t in range(NT + 1):
                    if t < NT:
                        dve.wait_ge(acc_full, nth(b, AF_PER, AF_C3 + t + 1))
                        dve.tensor_tensor(ev[:, t % 2, 0:F], ps[:, ACC + t % 4, 0:F], bias_g3[:, :],
                                          ALU.add).then_inc(acc_free, 1)
                        dve.wait_ge(acc_free, nth(b, 2 * NT, NT + t + 1))
                        y_free(b, 2, t)
                        dve.tensor_tensor(y[:, t % 4, :], ev[:, t % 2, 0:F], xn[:, t, :], ALU.add).then_inc(y_ready, 1)
                        tile_stats(b, 2, t)
                    if t == NT - 3:
                        x_transposed(b, 3, 0)

                for k, part in enumerate(QK):
                    if k == 3:
                        x_transposed(b, 3, 1)
                    ft, m, half = part
                    n = pr["qk", part]
                    dve.wait_ge(qk_hi, nth(b, 8, k + 1))
                    dve.scalar_tensor_tensor(out=qk_place(part, u_lo, qk0_lo), in0=ps[:, PR + n % 2, :],
                                             scalar=cols[:, 2 + m, ft:ft + 1], in1=f32(qk_place(part, u_hi, qk0_hi)),
                                             op0=ALU.add, op1=ALU.subtract).then_inc(pr_free, 1)
                dve.wait_ge(spilled, nth(b, 16 * NT, 16 * NT))
                for k in range(NT // 2):
                    n = pr["values", k]
                    dve.wait_ge(pr_full, nth(b, PR_UNITS, n + 1))
                    dve.tensor_copy(xn[:, 2 * k:2 * k + 2, :].rearrange("p t f -> p (t f)"),
                                    ps[:, PR + n % 2, :]).then_inc(pr_free, 1)
                for n in range(1, COPIES, 2):
                    dve.wait_ge(copies_full, nth(b, COPIES, n + 1))
                    dve.tensor_copy(copies_place(n), ps[0:STACK, ACC + n % 4, :]).then_inc(copies_dve, 1)
                for k in range(2):
                    dve.wait_ge(qk_out[k], nth(b, 32, 32))
                for s in range(UNITS + 13):
                    if s < UNITS:
                        qt, h = divmod(s, H)
                        dve.wait_ge(s_full, nth(b, UNITS, s + 1))
                        if s >= RSLOTS:
                            dve.wait_ge(p_full, nth(b, 2 * UNITS, 2 * (s - RSLOTS) + 2))
                        if s >= 4:
                            dve.wait_ge(neg_max, nth(b, UNITS, s - 3))
                        alone()
                        dve.tensor_tensor_reduce(
                            out=r[:, s % RSLOTS, :], in0=ps[:, 2 * (s % 2):2 * (s % 2) + 2, :].rearrange("p a c -> p (a c)"),
                            in1=adjn[:, qt, :], scale=1.0, scalar=-3.0e38, op0=ALU.mult, op1=ALU.max,
                            accum_out=mmax[:, s % 4:s % 4 + 1]).then_inc(masked, 1)
                    if LAG <= s < UNITS + LAG:
                        u = s - LAG
                        dve.wait_ge(p_full, nth(b, 2 * UNITS, 2 * u + 1))
                        if u >= PSLOTS:
                            dve.wait_ge(ctx_done, nth(b, 2 * NT, (u - PSLOTS) // G + 1))
                        dve.tensor_copy(pt[:, u % PSLOTS, 0:TPH, :].rearrange("p t q -> p (t q)"),
                                        ps[:, TP, :]).then_inc(p_dve, 1)
                    if s >= 8 and (s - 8) % H == 0 and (s - 8) // H < NT:
                        qt = (s - 8) // H
                        dve.wait_ge(exp_done, nth(b, UNITS, H * (qt + 1)))
                        if qt >= 2:
                            dve.wait_ge(rt_full, nth(b, NT, qt - 1))
                        dve.reciprocal(rprow[:, qt % 2, :], prow[:, qt % 2, :]).then_inc(rp_ready, 1)
                    if s >= 14 and (s - 14) % H == 0 and (s - 14) // H < NT:
                        qt = (s - 14) // H
                        dve.wait_ge(rbc_ready, nth(b, NT, qt + 1))
                        dve.wait_ge(ctx_done, nth(b, 2 * NT, 2 * qt + 2))
                        dve.tensor_tensor(c_f[:, :, :].rearrange("p g q -> p (g q)"), ps[:, 6, 0:2 * P],
                                          rbc[:, :, :].rearrange("p g q -> p (g q)"), ALU.mult).then_inc(c_raw, 1)
                    if s >= 16 and (s - 16) % H == 0 and (s - 16) // H < NT:
                        qt = (s - 16) // H
                        dve.wait_ge(c_hi_ready, nth(b, NT, qt + 1))
                        rest(c_lo[:, :, :], c_f[:, :, :], c_hi[:, :, :], c_ready)
                    if s >= 18 and (s - 18) % H == 0 and (s - 18) // H < NT:
                        qt = (s - 18) // H
                        dve.wait_ge(o_full, nth(b, NT, qt + 1))
                        dve.wait_ge(xr_biased, nth(b, NT, qt + 1))
                        dve.tensor_tensor(xr[:, qt % 2, :], ps[:, 7, 0:F], xr[:, qt % 2, :],
                                          ALU.add).then_inc(h_sum, 1)
                        dve.wait_ge(h_sum, nth(b, NT, qt + 1))
                        if qt == NT - 1:
                            dve.sem_inc(drained, 1)
                        tile_stats(b, 3, qt)


def kernel(**inputs):
    import numpy as np
    import concourse.bacc as bacc
    from concourse.bass_utils import run_bass_kernel_spmd

    nc = bacc.Bacc("TRN2", target_bir_lowering=False, num_devices=1)
    nc.disable_value_cache = True
    arrays, drams = {}, {}
    for name, value in inputs.items():
        a = np.ascontiguousarray(value)
        arrays[f"in_{name}"] = a
        drams[name] = nc.dram_tensor(f"in_{name}", a.shape, mybir.dt.from_np(a.dtype), kind="ExternalInput").ap()
    shape = arrays["in_x"].shape
    out = nc.dram_tensor("out", shape, F32, kind="ExternalOutput").ap()
    build_program(nc, drams, out)
    got = run_bass_kernel_spmd(nc, [arrays], core_ids=[0])
    return got.results[0]["out"]
```
